# Optimizing a Trainium2 kernel written in Bass

```python
import numpy as np
import jax
import jax.numpy as jnp

def _softmax(x, axis=-1):
    return jax.nn.softmax(x, axis=axis)

def _gelu(x):
    return jax.nn.gelu(x, approximate=True)

def _silu(x):
    return jax.nn.silu(x)

def _sigmoid(x):
    return jax.nn.sigmoid(x)

def _layernorm(x, axis=-1, eps=1e-05):
    m = jnp.mean(x, axis=axis, keepdims=True)
    v = jnp.var(x, axis=axis, keepdims=True)
    return (x - m) / jnp.sqrt(v + eps)

def _scatter_add(tgt, idx, src, axis=0):
    return tgt.at[idx].add(src)

def _segment_sum(src, seg, n):
    return jax.ops.segment_sum(src, seg, n)
kernel_name = 'mk_perceiver_d1_seqx_r4_7b0d8c'

def setup_inputs(seed: int=0):
    np.random.seed(seed)
    _w = jnp.asarray

    def _rec_inputs():
        import jax
        import jax.numpy as jnp
        _rk = jax.random.key(seed)
        x = 7.22e-05 + 1 * jax.random.normal(jax.random.fold_in(_rk, 1), (32, 32, 256), jnp.float32)
        _lenS = 32 - jax.random.randint(jax.random.fold_in(_rk, 7), (32,), 0, max(1, 32 // 4) + 1, jnp.int32)
        _lenS2 = 257 - jax.random.randint(jax.random.fold_in(_rk, 8), (32,), 0, max(1, 257 // 4) + 1, jnp.int32)
        _ctx_1024P = jax.random.normal(jax.random.fold_in(_rk, 11), (32, 16, 256), jnp.float32)
        _ctx_1024c = jax.random.dirichlet(jax.random.fold_in(_rk, 511), 0.3 * jnp.ones((16,), jnp.float32), (32, 257))
        _ctx_1024t = jnp.einsum('bsk,bkd->bsd', _ctx_1024c, _ctx_1024P)
        _ctx_1024t = _ctx_1024t * jax.lax.rsqrt(jnp.mean(jnp.square(_ctx_1024t)) + 1e-12) * 0.953939
        ctx_1024 = 4.13588e-05 + 0.999923 * (_ctx_1024t + 0.3 * jax.random.normal(jax.random.fold_in(_rk, 611), (32, 257, 256), jnp.float32))
        return (x, ctx_1024)
    x, ctx_1024 = _rec_inputs()

    def _L0_xattn_setup():
        import jax, jax.numpy as jnp
        import numpy as np
        D_MODEL = 256
        D_K = 64
        D_V = 64
        H = 16
        B = 4
        NQ = 512
        NK = 512
        key = jax.random.key(seed)
        ks = jax.random.split(key, 11)

        def xavier(k, shape):
            fan_in, fan_out = (shape[1], shape[0])
            lim = jnp.sqrt(6.0 / (fan_in + fan_out))
            return jax.random.uniform(k, shape, jnp.float32, -lim, lim)
        return {'queries': jax.random.normal(ks[0], (B, NQ, D_MODEL), jnp.float32), 'keys': jax.random.normal(ks[1], (B, NK, D_MODEL), jnp.float32), 'values': jax.random.normal(ks[2], (B, NK, D_MODEL), jnp.float32), 'Wq': xavier(ks[3], (H * D_K, D_MODEL)), 'bq': jnp.zeros((H * D_K,), jnp.float32), 'Wk': xavier(ks[4], (H * D_K, D_MODEL)), 'bk': jnp.zeros((H * D_K,), jnp.float32), 'Wv': xavier(ks[5], (H * D_V, D_MODEL)), 'bv': jnp.zeros((H * D_V,), jnp.float32), 'Wo': xavier(ks[6], (D_MODEL, H * D_V)), 'bo': jnp.zeros((D_MODEL,), jnp.float32)}
    _L0_xattn_all = _L0_xattn_setup()
    _L0_xattn_in = {k: v for k, v in _L0_xattn_all.items() if k in ('Wq', 'bq', 'Wk', 'bk', 'Wv', 'bv', 'Wo', 'bo')}
    del _L0_xattn_all

    def _L0_attn_setup():
        import jax, jax.numpy as jnp
        import numpy as np
        N_HEADS = 16
        EPS = 1e-06

        def _phi(x):
            return jax.nn.softplus(x) + EPS

        def _reference_tuple_inner(x, Wq, Wk, Wv, Wo):
            B, T, D = x.shape
            H = N_HEADS
            dh = D // H

            def proj(W):
                y = jnp.einsum('btd,ed->bte', x, W)
                return y.reshape(B, T, H, dh).transpose(1, 0, 2, 3)
            q = proj(Wq)
            k = proj(Wk)
            v = proj(Wv)
            qf = _phi(q)
            kf = _phi(k)
            kv0 = jnp.zeros((B, H, dh, dh), dtype=x.dtype)
            z0 = jnp.zeros((B, H, dh), dtype=x.dtype)

            def step(carry, inp):
                kv, z = carry
                qt, kt, vt = inp
                kv = kv + jnp.einsum('bhd,bhe->bhde', kt, vt)
                z = z + kt
                num = jnp.einsum('bhd,bhde->bhe', qt, kv)
                den = jnp.einsum('bhd,bhd->bh', qt, z) + EPS
                return ((kv, z), num / den[..., None])
            (kv_acc, z_acc), out_t = jax.lax.scan(step, (kv0, z0), (qf, kf, v))
            out = out_t.transpose(1, 0, 2, 3).reshape(B, T, D)
            out = jnp.einsum('btd,ed->bte', out, Wo)
            return (out, kv_acc, z_acc)
        key = jax.random.key(seed)
        ks = jax.random.split(key, 5)
        D = 256
        s = 1.0 / np.sqrt(D)
        x = jax.random.normal(ks[0], (4, 1024, D), dtype=jnp.float32)
        Wq = jax.random.normal(ks[1], (D, D), dtype=jnp.float32) * s
        Wk = jax.random.normal(ks[2], (D, D), dtype=jnp.float32) * s
        Wv = jax.random.normal(ks[3], (D, D), dtype=jnp.float32) * s
        Wo = jax.random.normal(ks[4], (D, D), dtype=jnp.float32) * s
        return {'x': x, 'Wq': Wq, 'Wk': Wk, 'Wv': Wv, 'Wo': Wo}
    _L0_attn_all = _L0_attn_setup()
    _L0_attn_in = {k: v for k, v in _L0_attn_all.items() if k in ('Wq', 'Wk', 'Wv', 'Wo')}
    del _L0_attn_all

    def _L0_ffn_setup():
        import jax, jax.numpy as jnp
        import numpy as np
        B, S, D = (1, 512, 256)
        E, K, F = (8, 2, 352)
        NS = 2
        SCALE = 2.5

        def _swiglu_mlp(x, wg, wu, wd):
            return jax.nn.silu(x @ wg) * (x @ wu) @ wd
        key = jax.random.key(seed)
        ks = jax.random.split(key, 8)
        s = 0.02
        return {'hidden_states': jax.random.normal(ks[0], (B, S, D), jnp.float32), 'gate_w': jax.random.normal(ks[1], (E, D), jnp.float32) * s, 'w_gate': jax.random.normal(ks[2], (E, D, F), jnp.float32) * s, 'w_up': jax.random.normal(ks[3], (E, D, F), jnp.float32) * s, 'w_down': jax.random.normal(ks[4], (E, F, D), jnp.float32) * s, 'sw_gate': jax.random.normal(ks[5], (D, F * NS), jnp.float32) * s, 'sw_up': jax.random.normal(ks[6], (D, F * NS), jnp.float32) * s, 'sw_down': jax.random.normal(ks[7], (F * NS, D), jnp.float32) * s}
    _L0_ffn_all = _L0_ffn_setup()
    _L0_ffn_in = {k: v for k, v in _L0_ffn_all.items() if k in ('gate_w', 'w_gate', 'w_up', 'w_down', 'sw_gate', 'sw_up', 'sw_down')}
    del _L0_ffn_all
    return {'x': x, 'ctx_1024': ctx_1024, 'L0_xattn_Wq': _L0_xattn_in['Wq'], 'L0_xattn_bq': _L0_xattn_in['bq'], 'L0_xattn_Wk': _L0_xattn_in['Wk'], 'L0_xattn_bk': _L0_xattn_in['bk'], 'L0_xattn_Wv': _L0_xattn_in['Wv'], 'L0_xattn_bv': _L0_xattn_in['bv'], 'L0_xattn_Wo': _L0_xattn_in['Wo'], 'L0_xattn_bo': _L0_xattn_in['bo'], 'L0_attn_Wq': _L0_attn_in['Wq'], 'L0_attn_Wk': _L0_attn_in['Wk'], 'L0_attn_Wv': _L0_attn_in['Wv'], 'L0_attn_Wo': _L0_attn_in['Wo'], 'L0_ffn_gate_w': _L0_ffn_in['gate_w'], 'L0_ffn_w_gate': _L0_ffn_in['w_gate'], 'L0_ffn_w_up': _L0_ffn_in['w_up'], 'L0_ffn_w_down': _L0_ffn_in['w_down'], 'L0_ffn_sw_gate': _L0_ffn_in['sw_gate'], 'L0_ffn_sw_up': _L0_ffn_in['sw_up'], 'L0_ffn_sw_down': _L0_ffn_in['sw_down']}

def reference(x, ctx_1024, L0_xattn_Wq, L0_xattn_bq, L0_xattn_Wk, L0_xattn_bk, L0_xattn_Wv, L0_xattn_bv, L0_xattn_Wo, L0_xattn_bo, L0_attn_Wq, L0_attn_Wk, L0_attn_Wv, L0_attn_Wo, L0_ffn_gate_w, L0_ffn_w_gate, L0_ffn_w_up, L0_ffn_w_down, L0_ffn_sw_gate, L0_ffn_sw_up, L0_ffn_sw_down):
    import jax
    import jax.numpy as jnp

    def _L0_xattn_ref(queries, keys, values, Wq, bq, Wk, bk, Wv, bv, Wo, bo):
        import jax, jax.numpy as jnp
        import numpy as np
        D_MODEL = 256
        D_K = 64
        D_V = 64
        H = 16
        B = 4
        NQ = 512
        NK = 512
        b_s, nq, _ = queries.shape
        nk = keys.shape[1]
        q = (queries @ Wq.T + bq).reshape(b_s, nq, H, D_K).transpose(0, 2, 1, 3)
        k = (keys @ Wk.T + bk).reshape(b_s, nk, H, D_K).transpose(0, 2, 1, 3)
        v = (values @ Wv.T + bv).reshape(b_s, nk, H, D_V).transpose(0, 2, 1, 3)
        att = jnp.einsum('bhqd,bhkd->bhqk', q, k) / jnp.sqrt(jnp.float32(D_K))
        att = jax.nn.softmax(att, axis=-1)
        out = jnp.einsum('bhqk,bhkd->bhqd', att, v)
        out = out.transpose(0, 2, 1, 3).reshape(b_s, nq, H * D_V)
        return out @ Wo.T + bo

    def _L0_attn_ref(x, Wq, Wk, Wv, Wo):
        import jax, jax.numpy as jnp
        import numpy as np
        N_HEADS = 16
        EPS = 1e-06

        def _phi(x):
            return jax.nn.softplus(x) + EPS

        def _reference_tuple_inner(x, Wq, Wk, Wv, Wo):
            B, T, D = x.shape
            H = N_HEADS
            dh = D // H

            def proj(W):
                y = jnp.einsum('btd,ed->bte', x, W)
                return y.reshape(B, T, H, dh).transpose(1, 0, 2, 3)
            q = proj(Wq)
            k = proj(Wk)
            v = proj(Wv)
            qf = _phi(q)
            kf = _phi(k)
            kv0 = jnp.zeros((B, H, dh, dh), dtype=x.dtype)
            z0 = jnp.zeros((B, H, dh), dtype=x.dtype)

            def step(carry, inp):
                kv, z = carry
                qt, kt, vt = inp
                kv = kv + jnp.einsum('bhd,bhe->bhde', kt, vt)
                z = z + kt
                num = jnp.einsum('bhd,bhde->bhe', qt, kv)
                den = jnp.einsum('bhd,bhd->bh', qt, z) + EPS
                return ((kv, z), num / den[..., None])
            (kv_acc, z_acc), out_t = jax.lax.scan(step, (kv0, z0), (qf, kf, v))
            out = out_t.transpose(1, 0, 2, 3).reshape(B, T, D)
            out = jnp.einsum('btd,ed->bte', out, Wo)
            return (out, kv_acc, z_acc)
        return _reference_tuple_inner(x, Wq, Wk, Wv, Wo)[0]

    def _L0_ffn_ref(hidden_states, gate_w, w_gate, w_up, w_down, sw_gate, sw_up, sw_down):
        import jax, jax.numpy as jnp
        import numpy as np
        B, S, D = (1, 512, 256)
        E, K, F = (8, 2, 352)
        NS = 2
        SCALE = 2.5

        def _swiglu_mlp(x, wg, wu, wd):
            return jax.nn.silu(x @ wg) * (x @ wu) @ wd
        identity = hidden_states
        x = hidden_states.reshape(-1, hidden_states.shape[-1])
        T = x.shape[0]
        logits = x.astype(jnp.float32) @ gate_w.astype(jnp.float32).T
        scores = jax.nn.softmax(logits, axis=-1)
        topk_w, topk_i = jax.lax.top_k(scores, K)
        topk_w = topk_w / (topk_w.sum(-1, keepdims=True) + 1e-20) * SCALE
        combine = jnp.zeros((T, E), jnp.float32).at[jnp.arange(T)[:, None], topk_i].set(topk_w)
        g = jax.nn.silu(jnp.einsum('td,edf->etf', x, w_gate)) * jnp.einsum('td,edf->etf', x, w_up)
        expert_out = jnp.einsum('etf,efd->etd', g, w_down)
        y = jnp.einsum('te,etd->td', combine, expert_out).astype(x.dtype)
        y = y.reshape(identity.shape)
        return y + _swiglu_mlp(identity, sw_gate, sw_up, sw_down)
    x = x + _L0_xattn_ref(_layernorm(x, axis=-1), ctx_1024, ctx_1024, L0_xattn_Wq, L0_xattn_bq, L0_xattn_Wk, L0_xattn_bk, L0_xattn_Wv, L0_xattn_bv, L0_xattn_Wo, L0_xattn_bo)
    x = x + _L0_attn_ref(_layernorm(x, axis=-1), L0_attn_Wq, L0_attn_Wk, L0_attn_Wv, L0_attn_Wo)
    x = x + _L0_ffn_ref(_layernorm(x, axis=-1), L0_ffn_gate_w, L0_ffn_w_gate, L0_ffn_w_up, L0_ffn_w_down, L0_ffn_sw_gate, L0_ffn_sw_up, L0_ffn_sw_down)
    return x

_drawn_inputs = setup_inputs


def setup_inputs(seed=0):
    import zlib

    import numpy as np

    out = dict(_drawn_inputs(seed))
    spreads = {'L0_xattn_bq': (0.0, 0.678),
     'L0_xattn_bk': (0.0, 0.8),
     'L0_xattn_bv': (0.0, 0.1),
     'L0_xattn_bo': (0.0, 0.1)}
    factors = {'L0_attn_Wq': 2.74}
    for name, (base, spread) in spreads.items():
        noise = np.random.default_rng([zlib.crc32(name.encode()), seed]).standard_normal(out[name].shape)
        drawn = base * np.exp(spread * noise) if base else spread * noise
        out[name] = jnp.asarray(drawn.astype(out[name].dtype))
    for name, factor in factors.items():
        out[name] = (out[name] * factor).astype(out[name].dtype)
    return out
```

```python
from contextlib import ExitStack

import numpy as np
import concourse.bass as bass
from concourse import mybir

F32 = mybir.dt.float32
F32R = mybir.dt.float32r
ALU = mybir.AluOpType
ACT = mybir.ActivationFunctionType
AX = mybir.AxisListType

P = 128
D = 256
KC = D // P
B, T = 32, 32
NK = 257
NKP = NK + 1
H, DK = 16, 64
HP = H // 2
LH, LD = 16, 16
LV = LD + 2
GB = 8
NG = B // GB
GR = GB * T
RT = GR // P
ROWS = B * T
TILES = ROWS // P
E, FE = 8, 352
NX = 10
FT = [(0, 128), (128, 128), (256, 96)]
FW = 2 * KC * FE + len(FT) * D
HALF = 512
SCALE = 1.0 / 8.0
LN_EPS = 1e-5
EPS = 1e-6
ROUTE_SCALE = 2.5

U_XN1, U_QB, U_Q, U_QP, U_ATT, U_O, U_XN2, U_LQ, U_LK, U_V, U_SC, U_PV, U_OT, U_Y = (
    0, 1, 2, 6, 22, 26, 27, 28, 29, 30, 31, 39, 41, 42)
NU = 43

class Steps:

    def __init__(self, eng, sem, base=0):
        self.eng, self.sem, self.base, self.n = eng, sem, base, 0

    def add(self, ins):
        ins.then_inc(self.sem, 1)
        self.n += 1

    def wait(self):
        self.eng.wait_ge(self.sem, self.base + self.n)

    def link(self, ins):
        self.add(ins)
        self.wait()


def build(nc, a, out):
    ctx = ExitStack()
    with ctx:
        def sem(name):
            return ctx.enter_context(nc.semaphore(name))

        SB0 = 16512
        place = {"at": SB0}

        def at(offset, name, shape, dt):
            return nc.alloc_sbuf_tensor_at(name, shape, dt, offset=offset)

        def sb(name, shape, dt):
            size = int(np.prod(shape[1:])) * 4
            offset = place["at"]
            place["at"] = (offset + size + 31) // 32 * 32
            return at(offset, name, shape, dt)

        ident = sb("ident", [P, P], F32)
        causal = sb("causal", [P, P], F32)
        parity = sb("parity", [P, 2], F32)
        zero = sb("zero", [P, 1], F32)
        lower = sb("lower", [P, E, E], F32)
        bq_sb = sb("bq_sb", [P, HP], F32)
        bk_sb = sb("bk_sb", [P, HP], F32)
        bv_sb = sb("bv_sb", [P, HP], F32)
        bo_sb = sb("bo_sb", [P, D], F32)
        gateT = sb("gateT", [P, KC, E], F32)
        gate_h = sb("gate_h", [P, KC, E], F32R)
        gate_l = sb("gate_l", [P, KC, E], F32R)
        PHASE = place["at"]

        bkd = sb("bkd", [P, HP, H], F32)
        bqk = sb("bqk", [H, 1], F32)
        wqb = sb("wqb", [P, KC, H], F32)
        wqb_h = sb("wqb_h", [P, KC, H], F32R)
        wqb_l = sb("wqb_l", [P, KC, H], F32R)
        wq_h = sb("wq_h", [P, KC, H * DK], F32R)
        wq_l = sb("wq_l", [P, KC, H * DK], F32R)
        wk_h = sb("wk_h", [P, HP, D], F32R)
        wk_l = sb("wk_l", [P, HP, D], F32R)
        wv_h = sb("wv_h", [P, KC, HP, 3 * DK], F32R)
        wv_l = sb("wv_l", [P, KC, HP, 3 * DK], F32R)
        wo_h = sb("wo_h", [P, HP, D], F32R)
        wo_l = sb("wo_l", [P, HP, D], F32R)
        lw_h = sb("lw_h", [P, 4, KC, D], F32R)
        lw_l = sb("lw_l", [P, 4, KC, D], F32R)
        xin = sb("xin", [P, RT, D], F32)
        xg = sb("xg", [P, RT, D], F32)
        stats = sb("stats", [P, RT, 6], F32)
        mv = sb("mv", [P, RT, 2], F32)
        lnt = sb("lnt", [P, 4, RT], F32)
        qb_sb = sb("qb_sb", [H, GR], F32)
        qbt = sb("qbt", [P, 4, GB], F32)
        vaug = sb("vaug", [P, RT, LH, LV], F32)
        mxq = sb("mxq", [P, 3, 4], F32)
        qbs = sb("qbs", [P, 4, GB], F32)
        psum_e = sb("psum_e", [P, 4], F32)
        rsum = sb("rsum", [P, 4], F32)
        cn_raw = [sb(f"cn_raw{s}", [P, 2, D], F32) for s in range(1)]
        ct_raw = [sb(f"ct_raw{s}", [P, KC, NKP], F32) for s in range(1)]
        cn_h = [sb(f"cn_h{s}", [P, 2, D], F32R) for s in range(2)]
        cn_l = [sb(f"cn_l{s}", [P, 2, D], F32R) for s in range(2)]
        ct_h = [sb(f"ct_h{s}", [P, KC, NKP], F32R) for s in range(2)]
        ct_l = [sb(f"ct_l{s}", [P, KC, NKP], F32R) for s in range(2)]
        c3 = [sb(f"c3_{s}", [3, D], F32R) for s in range(2)]
        RA = place["at"]
        q_h = at(RA, "q_h", [P, HP, GR], F32R)
        q_l = at(RA + 8192, "q_l", [P, HP, GR], F32R)
        pt_h = at(RA, "pt_h", [P, 2, 512], F32R)
        pt_l = at(RA + 4096, "pt_l", [P, 2, 512], F32R)
        pr = at(RA + 8192, "pr", [P, 4, NKP], F32)
        pl3 = at(RA + 12320, "pl3", [3, 512], F32R)
        l3 = at(RA + 14368, "l3", [P, 4, 3], F32R)
        at_h = at(RA, "at_h", [P, HP, GR], F32R)
        at_l = at(RA + 8192, "at_l", [P, HP, GR], F32R)
        RB = RA + 16384
        qu_h = at(RB, "qu_h", [P, KC, GB, H * T], F32R)
        qu_l = at(RB + 32768, "qu_l", [P, KC, GB, H * T], F32R)
        END = RB + 65536
        wq_raw = at(RB, "wq_raw", [P, KC, H * DK], F32)
        wqn_raw = at(RB + 8192, "wqn_raw", [P, HP, D], F32)
        wk_raw = at(RB + 16384, "wk_raw", [P, HP, D], F32)
        wv_raw = at(RB + 24576, "wv_raw", [P, KC, HP, P], F32)
        wo_raw = at(RB + 32768, "wo_raw", [P, HP, D], F32)
        lw_raw = at(RB + 40960, "lw_raw", [P, 4, KC, D], F32)
        cl_raw = at(RB + 49152, "cl_raw", [B, D], F32)
        cl_h = at(RB + 50176, "cl_h", [B, D], F32R)
        cl_l = at(RB + 51200, "cl_l", [B, D], F32R)
        xn1 = at(RB + 57344, "xn1", [P, RT, D], F32)
        x1_h = at(RB + 59392, "x1_h", [P, KC, GR], F32R)
        x1_l = at(RB + 61440, "x1_l", [P, KC, GR], F32R)
        xn2 = at(RB, "xn2", [P, RT, D], F32)
        x2_h = at(RB + 2048, "x2_h", [P, KC, GR], F32R)
        x2_l = at(RB + 4096, "x2_l", [P, KC, GR], F32R)
        fa = at(RB + 6144, "fa", [P, 2, KC, GR], F32)
        fb = at(RB + 10240, "fb", [P, 2, KC, GR], F32)
        k_h = at(RB + 14336, "k_h", [P, KC, GR], F32R)
        k_l = at(RB + 16384, "k_l", [P, KC, GR], F32R)
        qf_h = at(RB + 18432, "qf_h", [P, KC, GR], F32R)
        qf_l = at(RB + 20480, "qf_l", [P, KC, GR], F32R)
        qx_h = at(RB + 22528, "qx_h", [P, KC, 2, GR], F32R)
        qx_l = at(RB + 26624, "qx_l", [P, KC, 2, GR], F32R)
        am = at(RB + 30720, "am", [P, RT, LH, P], F32)
        den = at(RB + 47104, "den", [P, 2, RT, LH], F32)
        lo = at(RB + 47616, "lo", [P, RT, D], F32)
        ot_h = at(RB + 49664, "ot_h", [P, KC, GR], F32R)
        ot_l = at(RB + 51712, "ot_l", [P, KC, GR], F32R)
        assert END <= nc.sbuf_usable_end, (END, nc.sbuf_usable_end)

        place["at"] = PHASE
        fx = sb("fx", [P, TILES, D], F32)
        fst = sb("fst", [P, TILES, 6], F32)
        fmv = sb("fmv", [P, TILES, 2], F32)
        fln = sb("fln", [P, 4, TILES], F32)
        fxn = sb("fxn", [P, TILES, D], F32)
        ft_h = sb("ft_h", [P, KC, ROWS], F32R)
        ft_l = sb("ft_l", [P, KC, ROWS], F32R)
        rl = sb("rl", [P, TILES, E], F32)
        rsm = sb("rsm", [P, 4, TILES], F32)
        rgt = sb("rgt", [P, TILES, E, E], F32)
        req = sb("req", [P, TILES, E, E], F32)
        rank = sb("rank", [P, TILES, E], F32)
        comb = sb("comb", [P, TILES, E], F32)
        combT = sb("combT", [E, ROWS], F32)
        combB = sb("combB", [P, E, ROWS], F32)
        fw_raw = [sb(f"fw_raw{s}", [P, FW], F32) for s in range(2)]
        fw_h = [sb(f"fw_h{s}", [P, FW], F32R) for s in range(2)]
        fw_l = [sb(f"fw_l{s}", [P, FW], F32R) for s in range(2)]
        sg = [sb(f"sg{s}", [P, HALF], F32) for s in range(2)]
        hm = [sb(f"hm{s}", [P, HALF], F32) for s in range(2)]
        hh = [sb(f"hh{s}", [P, HALF], F32R) for s in range(2)]
        hl = [sb(f"hl{s}", [P, HALF], F32R) for s in range(2)]
        fo = sb("fo", [P, KC, ROWS], F32)
        fy = sb("fy", [P, TILES, D], F32)
        assert place["at"] <= nc.sbuf_usable_end, place["at"]

        ps = ctx.enter_context(nc.psum_tensor("ps", [P, 8, 512], F32))

        c3_d = nc.dram_tensor("c3_scratch", [B, 3, D], F32).ap()
        qb_d = nc.dram_tensor("qb_scratch", [NG, H, GR], F32).ap()
        x2_d = nc.dram_tensor("x2_scratch", [ROWS, D], F32).ap()
        cb_d = nc.dram_tensor("comb_scratch", [E, ROWS], F32).ap()

        def bank3(i, n):
            return ps[:, i, :].rearrange("p (n c) -> p n c", n=n)

        def head(t, h):
            return t[:, :, :, T * h:T * h + T]

        def by_batch(ap):
            return ap.rearrange("p k (b q) -> p k b q", q=T)

        def B_(u):
            return (u - U_ATT) % 8

        def rows_of(s):
            return FT[s // 2][1]

        def diag(ap, j):
            flat = ap.rearrange("p a h -> p (a h)")
            return flat[:, j:j + (HP - 1) * (H + 2) + 1:H + 2]

        def for_units(eng, unit, routed=None, with_expert=False, with_slot=False):
            def one(i, s, e, es, is_routed):
                if with_slot:
                    unit(i, s, e, es)
                elif with_expert:
                    unit(i, s, e if is_routed else None)
                else:
                    unit(i, s)

            for e in range(2):
                for s in range(6):
                    one(6 * e + s, s, e, e, False)
            if routed:
                routed()
            with eng.Fori(0, E // 2) as j:
                for es in range(2):
                    for s in range(6):
                        e = j * 2 + es
                        one(j * 12 + 12 + 6 * es + s, s, e + 2 if with_slot else e, es, True)

        const_ld = sem("const_loaded")
        weight_ld = [sem(f"weight_loaded{i}") for i in range(6)]
        mask_ready = sem("mask_ready")
        setup_pe = sem("setup_pe")
        setup_dve = sem("setup_dve")
        whi = sem("weight_high")
        wlo = sem("weight_low")
        c3_stored = sem("c3_stored")
        x_ld = sem("x_loaded")
        xin_free = sem("xin_free")
        ln_var = sem("ln_var_ready")
        ln_y = sem("ln_guess_ready")
        xn_ready = sem("xn_ready")
        made = sem("unit_made")
        high = sem("unit_high")
        drained = sem("unit_drained")
        qb_stored = sem("qb_stored")
        qb_ld = sem("qb_loaded")
        raw_ld = sem("context_loaded")
        c3_ld = [sem(f"c3_loaded{s}") for s in range(2)]
        c_steps = sem("context_split_steps")
        scores_made = sem("scores_made")
        bias_ready = sem("exp_bias_ready")
        exp_done = sem("exp_done")
        p_ready = sem("probs_ready")
        pt_made = sem("probs_transposed")
        pt_hi = sem("probs_high")
        pt_lo = sem("probs_low")
        u_made = sem("attended_made")
        u_hi = sem("attended_high")
        u_lo = sem("attended_low")
        act_steps = sem("act_steps")
        dve_steps = sem("dve_steps")
        f_ln = sem("feature_log_ready")
        f_map = sem("feature_map_ready")
        f_hi = sem("feature_high_ready")
        f_ready = sem("features_ready")
        am_ready = sem("masked_scores_ready")
        lo_ready = sem("linear_out_ready")
        x2_stored = sem("x2_stored")
        fx_ld = sem("ffn_x_loaded")
        f_steps = sem("ffn_dve_steps")
        fa_steps = sem("ffn_act_steps")
        fxn_ready = sem("ffn_xn_ready")
        ftr = sem("ffn_xT_made")
        fth = sem("ffn_xT_high")
        ftl = sem("ffn_xT_low")
        logit_made = sem("logits_made")
        comb_ready = sem("comb_ready")
        combT_made = sem("combT_made")
        combT_sb = sem("combT_copied")
        comb_st = sem("comb_stored")
        comb_ld = sem("comb_loaded")
        fw_ld = [sem(f"ffn_weights_loaded{s}") for s in range(2)]
        fw_split = sem("ffn_weights_split")
        gu_made = sem("gate_up_made")
        silu_done = sem("silu_done")
        h_done = sem("h_done")
        h_mid = sem("h_unweighted_done")
        h_hi = sem("h_high")
        h_lo = sem("h_low")
        down_done = sem("down_done")
        acc_done = sem("ffn_sum_done")
        fo_ready = sem("ffn_sum_copied")
        fy_made = sem("ffn_rows_made")
        fy_ready = sem("ffn_rows_ready")
        stored = sem("out_stored")

        def f32(ap):
            return ap.bitcast(F32)

        N_CONST = 5
        SHARED = 12
        NUNITS = 6 * NX
        MASKS = 10
        with_high = ([U_XN1] + list(range(U_Q, U_ATT + 4)) + [U_XN2, U_OT])
        HIGH_OF = {u: n + 1 for n, u in enumerate(with_high)}
        N_HIGH = len(with_high)
        FS_VAR = 2 * TILES + 2
        FS_LOGIT = FS_VAR + 4 + 2

        ACT_STEPS, DVE_STEPS = 6, 88

        block = ctx.enter_context(nc.Block())

        @block.sync
        def _(sp):
            sp.dma_start(bq_sb[:], a["bq"]).then_inc(const_ld, 16)
            sp.dma_start(bk_sb[:], a["bk"]).then_inc(const_ld, 16)
            sp.dma_start(bv_sb[:], a["bv"]).then_inc(const_ld, 16)
            sp.dma_start(bo_sb[:], a["bo"].partition_broadcast(P)).then_inc(const_ld, 16)
            sp.dma_start(gateT[:], a["gateT"]).then_inc(const_ld, 16)
            sp.dma_start(wqn_raw[:], a["wqn"]).then_inc(weight_ld[0], 16)
            sp.dma_start(cl_raw[:], a["ctx"][:, NK - 1, :]).then_inc(weight_ld[0], 16)
            sp.dma_start(wq_raw[:], a["wqT"]).then_inc(weight_ld[1], 16)
            sp.dma_start(wk_raw[:], a["wk"]).then_inc(weight_ld[2], 16)
            sp.dma_start(wv_raw[:], a["wvT"]).then_inc(weight_ld[3], 16)
            sp.dma_start(wo_raw[:], a["woT"]).then_inc(weight_ld[4], 16)
            sp.dma_start(lw_raw[:], a["lwT"]).then_inc(weight_ld[5], 16)
            sp.wait_ge(wlo, 1)
            for j, src in enumerate((cl_h, cl_h, cl_l)):
                sp.dma_start(c3_d[:, j, :], f32(src[:])).then_inc(c3_stored, 16)
            sp.wait_ge(c3_stored, 48)
            with sp.Fori(0, NG) as g:
                sp.wait_ge(xin_free, g + 1)
                sp.dma_start(xin[:], a["x"][bass.ds(g * GR, GR), :].rearrange("(r p) d -> p r d", p=P)
                             ).then_inc(x_ld, 16)
                for b in range(GB):
                    n = g * GB + b
                    sp.wait_ge(c_steps, 4 * n + 4)
                    sp.dma_start(cn_raw[0][:], a["ctx"][bass.ds(n, 1), 0:2 * P, :].rearrange(
                        "o (k p) d -> p (o k) d", p=P)).then_inc(raw_ld, 16)
                    sp.dma_start(ct_raw[0][:], a["ctxT"][bass.ds(n, 1)].rearrange(
                        "o p k c -> p (o k) c")).then_inc(raw_ld, 16)
                    sp.wait_ge(u_made, 2 * n + 2)
                    sp.dma_start(f32(c3[b % 2][:]), c3_d[bass.ds(n, 1)].rearrange("o j d -> (o j) d")
                                 ).then_inc(c3_ld[b % 2], 16)
                    if b == 0:
                        sp.wait_ge(qb_stored, 16 * (g + 1))
                        for h4 in range(4):
                            sp.dma_start(
                                qbt[32 * h4:32 * h4 + 32, :, :],
                                qb_d[bass.ds(g, 1)].rearrange(
                                    "o (t f) (q b) -> (o f) q t b", f=4, b=GB)[h4]
                            ).then_inc(qb_ld, 16)
            sp.wait_ge(x2_stored, 16 * NG + 16)
            sp.dma_start(fx[:], x2_d.rearrange("(r p) d -> p r d", p=P)).then_inc(fx_ld, 16)
            for e in range(2):
                sp.dma_start(fw_raw[e][:], a["ffn"][e]).then_inc(fw_ld[e], 16)
            sp.wait_ge(combT_sb, 2)
            sp.dma_start(cb_d, combT[:]).then_inc(comb_st, 16)
            sp.wait_ge(comb_st, 16)
            sp.dma_start(combB[:].rearrange("p e t -> p (e t)"),
                         cb_d.rearrange("e t -> (e t)").partition_broadcast(P)).then_inc(comb_ld, 16)
            with sp.Fori(0, E // 2) as j:
                for s in range(2):
                    e = j * 2 + s
                    sp.wait_ge(fw_split, 2 * (e + 1))
                    sp.dma_start(fw_raw[s][:], a["ffn"][bass.ds(e + 2, 1)].rearrange("o p w -> p (o w)")
                                 ).then_inc(fw_ld[s], 16)
            for h in range(2):
                sp.wait_ge(fy_ready, 4 * (h + 1))
                sp.dma_start(out[h * HALF:(h + 1) * HALF, :].rearrange("(r p) d -> p r d", p=P),
                             fy[:, 4 * h:4 * h + 4, :]).then_inc(stored, 16)
            sp.wait_ge(stored, 32)

        @block.gpsimd
        def _(pool):
            def round_high(dst, src):
                return nc.gpsimd.tensor_tensor(dst, src, zero[:, 0:1].broadcast_to(list(src.shape)), ALU.add)

            st = Steps(pool, mask_ready)
            st.link(nc.gpsimd.memset(zero[:], 0.0))
            st.link(nc.gpsimd.memset(ident[:], 0.0))
            st.link(nc.gpsimd.affine_select(out=ident[:], in_=ident[:], compare_op=ALU.not_equal, fill=1.0,
                                            base=0, pattern=[[-1, P]], channel_multiplier=1))
            st.link(nc.gpsimd.memset(causal[:], 1.0))
            st.link(nc.gpsimd.affine_select(out=causal[:], in_=causal[:], compare_op=ALU.is_ge, fill=0.0,
                                            base=0, pattern=[[1, P]], channel_multiplier=-1))
            for b4 in range(1, 4):
                st.link(nc.gpsimd.affine_select(
                    out=causal[:, T * b4:T * b4 + T], in_=causal[:, T * b4:T * b4 + T],
                    compare_op=ALU.is_ge, fill=0.0, base=-T * b4, pattern=[[0, T]], channel_multiplier=1))
            st.link(nc.gpsimd.memset(lower[:], 1.0))
            st.link(nc.gpsimd.affine_select(out=lower[:], in_=lower[:], compare_op=ALU.is_gt, fill=0.0,
                                            base=0, pattern=[[1, E], [-1, E]], channel_multiplier=0))
            nc.gpsimd.memset(f32(wv_h[:, :, :, DK:2 * DK]), 0.0).then_inc(xin_free, 1)
            nc.gpsimd.memset(f32(wv_l[:, :, :, DK:2 * DK]), 0.0).then_inc(u_made, 4)
            nc.gpsimd.memset(vaug[:, :, :, LD:LD + 1], 1.0).then_inc(c_steps, 4)
            nc.gpsimd.memset(vaug[:, :, :, LD + 1:LV], 0.0).then_inc(x2_stored, 16)
            with pool.Fori(0, NG) as g:
                cs = Steps(pool, c_steps, g * (4 * GB) + 4)
                for b in range(GB):
                    n = g * GB + b
                    s = b % 2
                    pool.wait_ge(raw_ld, 32 * (n + 1))
                    pool.wait_ge(u_made, 2 * n + 2)
                    cs.link(round_high(ct_h[s][:].rearrange("p k c -> p (k c)"), ct_raw[0][:].rearrange("p k c -> p (k c)")))
                    cs.link(nc.gpsimd.tensor_tensor(ct_l[s][:], ct_raw[0][:], f32(ct_h[s][:]), ALU.subtract))
                    cs.link(round_high(cn_h[s][:].rearrange("p k c -> p (k c)"), cn_raw[0][:].rearrange("p k c -> p (k c)")))
                    cs.link(nc.gpsimd.tensor_tensor(cn_l[s][:], cn_raw[0][:], f32(cn_h[s][:]), ALU.subtract))

            def split(e, s, turn):
                pool.wait_ge(fw_ld[s], 16 * turn)
                if not isinstance(e, int):
                    pool.wait_ge(down_done, 6 * (e - 1))
                round_high(fw_h[s][:], fw_raw[s][:]).then_inc(fw_split, 1)
                pool.wait_ge(fw_split, 2 * e + 1)
                nc.gpsimd.tensor_tensor(fw_l[s][:], fw_raw[s][:], f32(fw_h[s][:]), ALU.subtract
                                        ).then_inc(fw_split, 1)

            pool.wait_ge(x2_stored, 16 * NG + 16)
            for s in range(2):
                split(s, s, 1)
            with pool.Fori(0, E // 2) as j:
                for s in range(2):
                    split(j * 2 + s + 2, s, j + 2)

        @block.scalar
        def _(act):
            def copy(dst, src):
                return nc.scalar.activation(dst, src, ACT.Identity)

            act.wait_ge(weight_ld[0], 32)
            copy(cl_h[:], cl_raw[:]).then_inc(whi, 1)
            act.wait_ge(const_ld, 16 * N_CONST)
            copy(gate_h[:], gateT[:]).then_inc(whi, 1)
            for i, (hi, raw) in enumerate((
                    (wq_h[:], wq_raw[:]), (wk_h[:], wk_raw[:]),
                    (wv_h[:, :, :, 0:DK], wv_raw[:, :, :, 0:DK]),
                    (wv_h[:, :, :, 2 * DK:3 * DK], wv_raw[:, :, :, DK:2 * DK]),
                    (wo_h[:], wo_raw[:]), (lw_h[:], lw_raw[:]))):
                act.wait_ge(weight_ld[(1, 2, 3, 3, 4, 5)[i]], 16)
                copy(hi, raw).then_inc(whi, 1)
            act.wait_ge(setup_dve, 4)
            copy(wqb_h[:], wqb[:]).then_inc(whi, 1)

            with act.Fori(0, NG) as g:
                steps = Steps(act, act_steps, g * ACT_STEPS)

                def layernorm(n):
                    act.wait_ge(ln_var, g * 2 + n)
                    steps.link(nc.scalar.activation(lnt[:, 1, :], lnt[:, 0, :], ACT.Ln))
                    nc.scalar.activation(lnt[:, 2, :], lnt[:, 1, :], ACT.Exp, scale=-0.5).then_inc(ln_y, 1)

                n_high = [0]

                def high_part(u, dst, src, bias=None):
                    act.wait_ge(made, g * NU + u + 1)
                    for k in range(len(dst)):
                        ins = nc.scalar.activation(dst[k], src[k], ACT.Identity,
                                                   **({} if bias is None else {"bias": bias[k]}))
                    ins.then_inc(high, 1)

                layernorm(1)
                high_part(U_XN1, [x1_h[:]], [bank3(0, KC)])
                act.wait_ge(drained, g * NU + U_QB + 1)
                act.dma_start(qb_d[bass.ds(g, 1)].rearrange("o h r -> (o h) r"), qb_sb[:]).then_inc(qb_stored, 16)
                for i in range(4):
                    high_part(U_Q + i, [q_h[:, 2 * i + k, :] for k in range(2)],
                              [bank3((U_Q + i) % 8, 2)[:, k, :] for k in range(2)],
                              [bq_sb[:, 2 * i + k:2 * i + k + 1] for k in range(2)])
                for h in range(H):
                    high_part(U_QP + h, [head(qu_h, h)], [by_batch(bank3((U_QP + h) % 8, KC))])

                def exps(b):
                    for t in range(4):
                        act.wait_ge(bias_ready, g * (2 * GB) + 2 * b + t // 2 + 1)
                        nc.scalar.activation(pr[:, t, 0:NK], ps[:, t, 0:NK], ACT.Exp, bias=mxq[:, 2, t:t + 1],
                                             scale=SCALE, accum_out=psum_e[:, t:t + 1]).then_inc(exp_done, 1)

                exps(0)
                for b in range(GB):
                    for k in range(3):
                        act.wait_ge(pt_made, g * (3 * GB) + 3 * b + k + 1)
                        if k < 2:
                            copy(pt_h[:, k, :], ps[:, 4 + k, :]).then_inc(pt_hi, 1)
                        else:
                            copy(pl3[:], ps[0:3, 7, :]).then_inc(pt_hi, 1)
                    if b + 1 < GB:
                        exps(b + 1)
                    for dt in range(KC):
                        act.wait_ge(u_made, g * (2 * GB) + 4 + 2 * b + dt + 1)
                        copy(qu_h[:, dt, b, :], ps[:, 6 + dt, :]).then_inc(u_hi, 1)
                for i in range(4):
                    high_part(U_ATT + i, [at_h[:, 2 * i + k, :] for k in range(2)],
                              [bank3(i, 2)[:, k, :] for k in range(2)],
                              [bv_sb[:, 2 * i + k:2 * i + k + 1] for k in range(2)])
                layernorm(2)
                high_part(U_XN2, [x2_h[:]], [bank3(B_(U_XN2), KC)])
                for j, u in enumerate((U_LQ, U_LK)):
                    act.wait_ge(made, g * NU + u + 1)
                    steps.link(nc.scalar.activation(fa[:, j], bank3(B_(u), KC), ACT.Abs))
                    steps.link(nc.scalar.activation(fb[:, j], fa[:, j], ACT.Exp, scale=-1.0))
                    nc.scalar.activation(fb[:, j], fb[:, j], ACT.Ln, bias=1.0).then_inc(f_ln, 1)
                for j, dst in enumerate((qf_h, k_h)):
                    act.wait_ge(f_map, g * 2 + j + 1)
                    copy(dst[:], fa[:, j]).then_inc(f_hi, 1)
                high_part(U_OT, [ot_h[:]], [bank3(B_(U_OT), KC)])
                act.wait_ge(drained, g * NU + U_Y + 1)
                act.dma_start(x2_d[bass.ds(g * GR, GR), :].rearrange("(r p) d -> p r d", p=P), xg[:]
                              ).then_inc(x2_stored, 16)
                assert steps.n == ACT_STEPS, steps.n

            act.wait_ge(f_steps, FS_VAR)
            fs = Steps(act, fa_steps)
            fs.link(nc.scalar.activation(fln[:, 1, :], fln[:, 0, :], ACT.Ln))
            fs.link(nc.scalar.activation(fln[:, 2, :], fln[:, 1, :], ACT.Exp, scale=-0.5))
            for i in range(4):
                act.wait_ge(ftr, i + 1)
                kc, half = i // 2, i % 2
                copy(ft_h[:, kc, half * HALF:(half + 1) * HALF], ps[:, i, :]).then_inc(fth, 1)
            act.wait_ge(f_steps, FS_LOGIT)
            fs.link(nc.scalar.activation(rl[:], rl[:], ACT.Exp))
            assert fs.n == 3

            def unit(i, s):
                act.wait_ge(gu_made, 2 * i + 1)
                if not isinstance(i, int) or i >= 2:
                    act.wait_ge(h_done, i - 1)
                rows = rows_of(s)
                nc.scalar.activation(sg[s % 2][0:rows], ps[0:rows, 4 + 2 * (s % 2), :], ACT.Silu
                                     ).then_inc(silu_done, 1)
                act.wait_ge(h_done, i + 1)
                if not isinstance(i, int) or i >= 2:
                    act.wait_ge(down_done, i - 1)
                copy(hh[s % 2][0:rows], hm[s % 2][0:rows]).then_inc(h_hi, 1)

            for_units(act, unit)
            for r in range(4):
                if r % 2 == 0:
                    act.wait_ge(down_done, NUNITS)
                    copy(fo[:, r // 2, 0:HALF], ps[:, r, :]).then_inc(fo_ready, 1)

        @block.vector
        def _(dve):
            V = nc.vector
            st = Steps(dve, setup_dve)
            dve.wait_ge(const_ld, 16 * N_CONST)
            st.link(V.memset(bkd[:], 0.0))
            st.add(V.tensor_copy(diag(bkd[0:DK], 0), bk_sb[0:DK, :]))
            st.add(V.tensor_copy(diag(bkd[DK:P], 1), bk_sb[DK:P, :]))
            dve.wait_ge(mask_ready, MASKS)
            blocks = ident[:].rearrange("p (k j c) -> p j k c", j=2, c=LD)
            for j in range(2):
                V.tensor_reduce(parity[:, j:j + 1], blocks[:, j], AX.XY, ALU.add).then_inc(mask_ready, 1)
            dve.wait_ge(whi, 1)
            V.tensor_tensor(cl_l[:], cl_raw[:], f32(cl_h[:]), ALU.subtract).then_inc(wlo, 1)
            dve.wait_ge(whi, 2)
            V.tensor_tensor(gate_l[:], gateT[:], f32(gate_h[:]), ALU.subtract).then_inc(wlo, 1)
            dve.wait_ge(setup_pe, 1)
            st.link(V.tensor_copy(wqb[:].rearrange("p k h -> p (k h)"), ps[:, 0, 0:KC * H]))
            dve.wait_ge(setup_pe, 2)
            st.add(V.tensor_copy(bqk[:], ps[0:H, 1, 0:1]))
            for i, (lo_, raw, hi) in enumerate((
                    (wq_l[:], wq_raw[:], wq_h[:]), (wk_l[:], wk_raw[:], wk_h[:]),
                    (wv_l[:, :, :, 0:DK], wv_raw[:, :, :, 0:DK], wv_h[:, :, :, 0:DK]),
                    (wv_l[:, :, :, 2 * DK:3 * DK], wv_raw[:, :, :, DK:2 * DK], wv_h[:, :, :, 2 * DK:3 * DK]),
                    (wo_l[:], wo_raw[:], wo_h[:]), (lw_l[:], lw_raw[:], lw_h[:]),
                    (wqb_l[:], wqb[:], wqb_h[:]))):
                dve.wait_ge(whi, i + 3)
                V.tensor_tensor(lo_, raw, f32(hi), ALU.subtract).then_inc(wlo, 1)

            def layernorm(steps, x, tiles, stats, mv, t, eps_done, y_ready, xn, xn_done):
                for r in range(tiles):
                    steps.add(V.bn_stats(stats[:, r, :], x[:, r, :]))
                steps.wait()
                steps.add(V.memset(t[:, 3, :], 0.0))
                for r in range(tiles):
                    steps.add(V.bn_aggr(mv[:, r, :], stats[:, r, :]))
                steps.wait()
                eps_done(V.tensor_scalar(t[:, 0, :], mv[:, :, 1], LN_EPS, None, ALU.add))
                y_ready()
                steps.link(V.tensor_tensor(t[:, 3, :], t[:, 2, :], t[:, 2, :], ALU.mult))
                steps.link(V.tensor_tensor(t[:, 3, :], t[:, 3, :], t[:, 0, :], ALU.mult))
                steps.link(V.tensor_scalar(t[:, 3, :], t[:, 3, :], -0.5, 1.5, ALU.mult, ALU.add))
                steps.link(V.tensor_tensor(t[:, 3, :], t[:, 2, :], t[:, 3, :], ALU.mult))
                for r in range(tiles):
                    ins = V.tensor_scalar(xn[:, r, :], x[:, r, :], mv[:, r, 0:1], t[:, 3, r:r + 1],
                                          ALU.subtract, ALU.mult)
                    xn_done(r, ins)

            with dve.Fori(0, NG) as g:
                steps = Steps(dve, dve_steps, g * DVE_STEPS)

                def group_norm(n, x, xn):
                    layernorm(steps, x, RT, stats, mv, lnt,
                              lambda ins: ins.then_inc(ln_var, 1),
                              lambda: dve.wait_ge(ln_y, g * 2 + n),
                              xn, lambda r, ins: ins.then_inc(xn_ready, 1))

                def low_part(u, dst, src, hi, bias=None):
                    dve.wait_ge(high, g * N_HIGH + HIGH_OF[u])
                    for k in range(len(dst)):
                        if bias is None:
                            ins = V.tensor_tensor(dst[k], src[k], f32(hi[k]), ALU.subtract)
                        else:
                            ins = V.scalar_tensor_tensor(dst[k], src[k], bias[k], f32(hi[k]), ALU.add, ALU.subtract)
                    ins.then_inc(drained, 1)

                dve.wait_ge(x_ld, 16 * (g + 1))
                group_norm(1, xin, xn1)
                dve.wait_ge(x2_stored, 16 * (g + 1))
                for r in range(RT):
                    ins = V.tensor_tensor(xg[:, r, :], xin[:, r, :], bo_sb[:], ALU.add)
                ins.then_inc(xin_free, 1)
                low_part(U_XN1, [x1_l[:]], [bank3(0, KC)], [x1_h[:]])
                dve.wait_ge(made, g * NU + U_QB + 1)
                V.tensor_scalar(qb_sb[:], ps[0:H, U_QB, 0:GR], bqk[:, 0:1], None, ALU.add).then_inc(drained, 1)
                for i in range(4):
                    low_part(U_Q + i, [q_l[:, 2 * i + k, :] for k in range(2)],
                             [bank3((U_Q + i) % 8, 2)[:, k, :] for k in range(2)],
                             [q_h[:, 2 * i + k, :] for k in range(2)],
                             [bq_sb[:, 2 * i + k:2 * i + k + 1] for k in range(2)])
                for h in range(H):
                    low_part(U_QP + h, [head(qu_l, h)], [by_batch(bank3((U_QP + h) % 8, KC))], [head(qu_h, h)])
                dve.wait_ge(qb_ld, 64 * (g + 1))
                steps.link(V.tensor_scalar(qbs[:], qbt[:], SCALE, None, ALU.mult))

                def maxima(b):
                    for p in range(2):
                        tt = slice(2 * p, 2 * p + 2)
                        dve.wait_ge(scores_made, g * (4 * GB) + 4 * b + 2 * p + 2)
                        steps.link(V.tensor_reduce(mxq[:, 0, tt], ps[:, tt, 0:NK], AX.X, ALU.max))
                        steps.link(V.tensor_tensor(mxq[:, 1, tt], mxq[:, 0, tt], qbt[:, tt, b], ALU.add))
                        V.scalar_tensor_tensor(mxq[:, 2, tt], mxq[:, 1, tt], -SCALE, qbs[:, tt, b],
                                               ALU.mult, ALU.add).then_inc(bias_ready, 1)

                def normalize(b):
                    for p in range(2):
                        tt = slice(2 * p, 2 * p + 2)
                        dve.wait_ge(exp_done, g * (4 * GB) + 4 * b + 2 * p + 2)
                        steps.link(V.reciprocal(rsum[:, tt], psum_e[:, tt]))
                        for t in (2 * p, 2 * p + 1):
                            V.tensor_scalar(pr[:, t, 0:NK], pr[:, t, 0:NK], rsum[:, t:t + 1], None,
                                            ALU.mult).then_inc(p_ready, 1)
                    dve.wait_ge(p_ready, g * (5 * GB) + 5 * b + 4)
                    steps.link(V.tensor_copy(l3[:, :, 0], pr[:, :, NK - 1]))
                    steps.link(V.tensor_tensor(l3[:, :, 1], pr[:, :, NK - 1], f32(l3[:, :, 0]), ALU.subtract))
                    V.tensor_copy(l3[:, :, 2], l3[:, :, 0]).then_inc(p_ready, 1)

                maxima(0)
                normalize(0)
                for b in range(GB):
                    for k in range(2):
                        dve.wait_ge(pt_hi, g * (3 * GB) + 3 * b + k + 1)
                        V.tensor_tensor(pt_l[:, k, :], ps[:, 4 + k, :], f32(pt_h[:, k, :]), ALU.subtract
                                        ).then_inc(pt_lo, 1)
                    if b + 1 < GB:
                        maxima(b + 1)
                        normalize(b + 1)
                    for dt in range(KC):
                        dve.wait_ge(u_hi, g * (2 * GB) + 2 * b + dt + 1)
                        V.tensor_tensor(qu_l[:, dt, b, :], ps[:, 6 + dt, :], f32(qu_h[:, dt, b, :]),
                                        ALU.subtract).then_inc(u_lo, 1)
                for i in range(4):
                    low_part(U_ATT + i, [at_l[:, 2 * i + k, :] for k in range(2)],
                             [bank3(i, 2)[:, k, :] for k in range(2)],
                             [at_h[:, 2 * i + k, :] for k in range(2)],
                             [bv_sb[:, 2 * i + k:2 * i + k + 1] for k in range(2)])
                dve.wait_ge(made, g * NU + U_O + 1)
                V.tensor_tensor(xg[:], bank3(B_(U_O), RT), xg[:], ALU.add).then_inc(drained, 1)
                dve.wait_ge(drained, g * NU + U_O + 1)
                group_norm(2, xg, xn2)
                low_part(U_XN2, [x2_l[:]], [bank3(B_(U_XN2), KC)], [x2_h[:]])
                for j, u in enumerate((U_LQ, U_LK)):
                    dve.wait_ge(f_ln, g * 2 + j + 1)
                    V.scalar_tensor_tensor(fa[:, j].rearrange("p k r -> p (k r)"), ps[:, B_(u), :], 0.0,
                                           fb[:, j].rearrange("p k r -> p (k r)"), ALU.max, ALU.add
                                           ).then_inc(drained, 1)
                    dve.wait_ge(drained, g * NU + u + 1)
                    V.tensor_scalar(fa[:, j], fa[:, j], EPS, None, ALU.add).then_inc(f_map, 1)
                dve.wait_ge(made, g * NU + U_V + 1)
                V.tensor_copy(vaug[:, :, :, 0:LD], bank3(B_(U_V), RT).rearrange("p r (h e) -> p r h e", e=LD)
                              ).then_inc(drained, 1)
                dve.wait_ge(f_hi, g * 2 + 1)
                steps.link(V.tensor_tensor(qf_l[:], fa[:, 0], f32(qf_h[:]), ALU.subtract))
                for par in range(2):
                    V.tensor_scalar(qx_h[:, :, par, :], f32(qf_h[:]), parity[:, par:par + 1], None,
                                    ALU.mult).then_inc(f_ready, 1)
                    V.tensor_scalar(qx_l[:, :, par, :], f32(qf_l[:]), parity[:, par:par + 1], None,
                                    ALU.mult).then_inc(f_ready, 1)
                dve.wait_ge(f_hi, g * 2 + 2)
                V.tensor_tensor(k_l[:], fa[:, 1], f32(k_h[:]), ALU.subtract).then_inc(f_ready, 1)
                for r in range(RT):
                    for j in range(4):
                        u = U_SC + 4 * r + j
                        dve.wait_ge(made, g * NU + u + 1)
                        V.tensor_tensor(am[:, r].rearrange("p (e j h) t -> p j e h t", e=KC, h=2)[:, j],
                                        ps[:, B_(u), :].rearrange("p (e h t) -> p e h t", e=KC, t=P),
                                        causal[:, None, None, :].broadcast_to([P, KC, 2, P]), ALU.mult
                                        ).then_inc(drained, 1)
                for r in range(RT):
                    u = U_PV + r
                    dve.wait_ge(made, g * NU + u + 1)
                    nd = ps[:, B_(u), 0:LH * LV].rearrange("p (h e) -> p h e", e=LV)
                    steps.link(V.tensor_scalar(den[:, 0, r, :], nd[:, :, LD], EPS, None, ALU.add))
                    steps.link(V.reciprocal(den[:, 1, r, :], den[:, 0, r, :]))
                    V.tensor_tensor(lo[:, r, :].rearrange("p (h e) -> p h e", e=LD), nd[:, :, 0:LD],
                                    den[:, 1, r, :, None].broadcast_to([P, LH, LD]), ALU.mult
                                    ).then_inc(drained, 1)
                low_part(U_OT, [ot_l[:]], [bank3(B_(U_OT), KC)], [ot_h[:]])
                dve.wait_ge(made, g * NU + U_Y + 1)
                V.tensor_tensor(xg[:], bank3(B_(U_Y), RT), xg[:], ALU.add).then_inc(drained, 1)
                assert steps.n == DVE_STEPS, steps.n

            dve.wait_ge(fx_ld, 16)
            fs = Steps(dve, f_steps)
            layernorm(fs, fx, TILES, fst, fmv, fln, lambda ins: fs.link(ins),
                      lambda: dve.wait_ge(fa_steps, 2), fxn, lambda r, ins: ins.then_inc(fxn_ready, 1))
            assert FS_VAR == 2 * TILES + 2
            for i in range(4):
                kc, half = i // 2, i % 2
                dve.wait_ge(fth, i + 1)
                V.tensor_tensor(ft_l[:, kc, half * HALF:(half + 1) * HALF], ps[:, i, :],
                                f32(ft_h[:, kc, half * HALF:(half + 1) * HALF]), ALU.subtract).then_inc(ftl, 1)
            dve.wait_ge(logit_made, 1)
            lg = ps[:, 4, 0:TILES * E].rearrange("p (t e) -> p t e", e=E)
            fs.link(V.tensor_reduce(rsm[:, 0, :], lg, AX.X, ALU.max))
            fs.link(V.tensor_tensor(rl[:], lg, rsm[:, 0, :, None].broadcast_to([P, TILES, E]), ALU.subtract))
            assert fs.n == FS_LOGIT, fs.n
            dve.wait_ge(fa_steps, 3)
            fs.link(V.tensor_reduce(rsm[:, 1, :], rl[:], AX.X, ALU.add))
            fs.link(V.reciprocal(rsm[:, 1, :], rsm[:, 1, :]))
            fs.link(V.tensor_tensor(rl[:], rl[:], rsm[:, 1, :, None].broadcast_to([P, TILES, E]), ALU.mult))
            of_e = rl[:, :, :, None].broadcast_to([P, TILES, E, E])
            of_f = rl[:, :, None, :].broadcast_to([P, TILES, E, E])
            low4 = lower[:, None].broadcast_to([P, TILES, E, E])
            fs.link(V.tensor_tensor(rgt[:], of_f, of_e, ALU.is_gt))
            fs.link(V.tensor_tensor(req[:], of_f, of_e, ALU.is_equal))
            for t in range(TILES):
                fs.add(V.tensor_tensor(req[:, t], req[:, t], lower[:], ALU.mult))
            fs.wait()
            fs.link(V.tensor_tensor(rgt[:], rgt[:], req[:], ALU.add))
            fs.link(V.tensor_reduce(rank[:], rgt[:], AX.X, ALU.add))
            fs.link(V.tensor_scalar(rank[:], rank[:], 1.5, None, ALU.is_lt))
            fs.link(V.tensor_tensor(rl[:], rl[:], rank[:], ALU.mult))
            fs.link(V.tensor_reduce(rsm[:, 2, :], rl[:], AX.X, ALU.add))
            fs.link(V.tensor_scalar(rsm[:, 2, :], rsm[:, 2, :], 1e-20, None, ALU.add))
            fs.link(V.reciprocal(rsm[:, 3, :], rsm[:, 2, :]))
            fs.link(V.tensor_scalar(rsm[:, 3, :], rsm[:, 3, :], ROUTE_SCALE, None, ALU.mult))
            V.tensor_tensor(comb[:], rl[:], rsm[:, 3, :, None].broadcast_to([P, TILES, E]), ALU.mult
                            ).then_inc(comb_ready, 1)
            for half in range(2):
                dve.wait_ge(combT_made, half + 1)
                V.tensor_copy(combT[:, half * HALF:(half + 1) * HALF], ps[0:E, 6 + half, :]).then_inc(combT_sb, 1)

            def unit(i, s, e=None):
                rows = rows_of(s)
                dve.wait_ge(gu_made, 2 * i + 2)
                dve.wait_ge(silu_done, i + 1)
                if not isinstance(i, int) or i >= 2:
                    dve.wait_ge(h_hi, i - 1)
                up = ps[0:rows, 5 + 2 * (s % 2), :]
                if e is None:
                    V.tensor_tensor(hm[s % 2][0:rows], up, sg[s % 2][0:rows], ALU.mult).then_inc(h_done, 1)
                else:
                    V.tensor_tensor(sg[s % 2][0:rows], up, sg[s % 2][0:rows], ALU.mult).then_inc(h_mid, 1)
                    dve.wait_ge(h_mid, i - SHARED + 1)
                    half = s % 2
                    V.tensor_tensor(hm[s % 2][0:rows], sg[s % 2][0:rows],
                                    combB[0:rows, bass.ds(e, 1), half * HALF:(half + 1) * HALF].rearrange(
                                        "p o t -> p (o t)"), ALU.mult).then_inc(h_done, 1)
                dve.wait_ge(h_hi, i + 1)
                V.tensor_tensor(hl[s % 2][0:rows], hm[s % 2][0:rows], f32(hh[s % 2][0:rows]), ALU.subtract
                                ).then_inc(h_lo, 1)

            for_units(dve, unit, routed=lambda: dve.wait_ge(comb_ld, 16), with_expert=True)
            for r in range(4):
                if r % 2:
                    dve.wait_ge(down_done, NUNITS)
                    V.tensor_copy(fo[:, r // 2, HALF:ROWS], ps[:, r, :]).then_inc(fo_ready, 1)
            for r in range(TILES):
                if r % 2 == 0:
                    dve.wait_ge(fy_made, r // 2 + 1)
                V.tensor_tensor(fy[:, r, :], ps[:, 4 + r // 2, (r % 2) * D:(r % 2 + 1) * D], fx[:, r, :],
                                ALU.add).then_inc(fy_ready, 1)

        @block.tensor
        def _(pe):
            mm = nc.tensor.matmul

            def mm3(dst, w, x, start, stop):
                mm(dst, w[0], x[0], start=start, stop=False)
                mm(dst, w[0], x[1], start=False, stop=False)
                return mm(dst, w[1], x[0], start=False, stop=stop)

            pe.wait_ge(weight_ld[0], 32)
            pe.wait_ge(setup_dve, 3)
            for kc in range(KC):
                for hp in range(HP):
                    ins = mm(ps[:, 0, kc * H:(kc + 1) * H], wqn_raw[:, hp, kc * P:(kc + 1) * P], bkd[:, hp, :],
                             start=hp == 0, stop=hp == HP - 1)
            ins.then_inc(setup_pe, 1)
            for hp in range(HP):
                ins = mm(ps[0:H, 1, 0:1], bkd[:, hp, :], bq_sb[:, hp:hp + 1], start=hp == 0, stop=hp == HP - 1)
            ins.then_inc(setup_pe, 1)
            pe.wait_ge(wlo, 9)
            pe.wait_ge(setup_dve, 5)
            pe.wait_ge(mask_ready, MASKS + 2)

            with pe.Fori(0, NG) as g:
                def reuse(u):
                    first = 8 if u < U_ATT else U_ATT + 8
                    if u >= first:
                        pe.wait_ge(drained, g * NU + u - 7)

                def transposes(u, b_, src):
                    for kc in range(KC):
                        for r in range(RT):
                            ins = nc.tensor.transpose(ps[:, b_, kc * GR + r * P:kc * GR + (r + 1) * P],
                                                      src[:, r, kc * P:(kc + 1) * P], ident[:])
                    ins.then_inc(made, 1)

                pe.wait_ge(xn_ready, 2 * RT * g + RT)
                transposes(U_XN1, 0, xn1)
                pe.wait_ge(drained, g * NU + U_XN1 + 1)
                for kc in range(KC):
                    x = [t[:, kc, :].rearrange("p (b q) -> p q b", q=T) for t in (x1_h, x1_l)]
                    ins = mm3(ps[0:H, U_QB, 0:GR], (wqb_h[:, kc, :], wqb_l[:, kc, :]), x, kc == 0, kc == 1)
                ins.then_inc(made, 1)
                for i in range(4):
                    for k in range(2):
                        hp = 2 * i + k
                        for kc in range(KC):
                            w = slice(hp * P, (hp + 1) * P)
                            ins = mm3(ps[:, (U_Q + i) % 8, k * GR:(k + 1) * GR],
                                      (wq_h[:, kc, w], wq_l[:, kc, w]), (x1_h[:, kc, :], x1_l[:, kc, :]),
                                      kc == 0, kc == 1)
                    ins.then_inc(made, 1)
                for h in range(H):
                    reuse(U_QP + h)
                    pe.wait_ge(drained, g * NU + U_Q + h // 4 + 1)
                    rows = slice(DK * (h % 2), DK * (h % 2) + DK)
                    for dt in range(KC):
                        w = slice(dt * P, (dt + 1) * P)
                        ins = mm3(ps[:, (U_QP + h) % 8, dt * GR:(dt + 1) * GR],
                                  (wk_h[rows, h // 2, w], wk_l[rows, h // 2, w]),
                                  (q_h[rows, h // 2, :], q_l[rows, h // 2, :]), True, True)
                    ins.then_inc(made, 1)
                pe.wait_ge(drained, g * NU + U_QP + H)

                def scores(b):
                    s = b % 2
                    pe.wait_ge(c_steps, g * (4 * GB) + 4 * b + 4 + 2)
                    for t in range(4):
                        if b:
                            pe.wait_ge(exp_done, g * (4 * GB) + 4 * (b - 1) + t + 1)
                        for kc in range(KC):
                            q = [x[:, kc, b, P * t:P * t + P] for x in (qu_h, qu_l)]
                            ins = mm3(ps[:, t, 0:NKP], q, (ct_h[s][:, kc, :], ct_l[s][:, kc, :]), kc == 0, kc == 1)
                        ins.then_inc(scores_made, 1)

                def probs_t(b):
                    for k in range(2):
                        for t in range(4):
                            if k == 0:
                                pe.wait_ge(p_ready, g * (5 * GB) + 5 * b + t + 1)
                            ins = nc.tensor.transpose(ps[:, 4 + k, t * P:(t + 1) * P],
                                                      pr[:, t, k * P:(k + 1) * P], ident[:])
                        ins.then_inc(pt_made, 1)
                    pe.wait_ge(p_ready, g * (5 * GB) + 5 * b + 5)
                    if b:
                        pe.wait_ge(u_lo, g * (2 * GB) + 2 * b)
                    for t in range(4):
                        ins = nc.tensor.transpose(ps[0:3, 7, t * P:(t + 1) * P], f32(l3[:, t, :]), ident[:])
                    ins.then_inc(pt_made, 1)

                def attend(b):
                    s = b % 2
                    pe.wait_ge(c_steps, g * (4 * GB) + 4 * b + 4 + 4)
                    pe.wait_ge(c3_ld[s], 16 * (g * (GB // 2) + b // 2 + 1))
                    for dt in range(KC):
                        w = slice(dt * P, (dt + 1) * P)
                        for k in range(2):
                            if dt == 0:
                                pe.wait_ge(pt_lo, g * (2 * GB) + 2 * b + k + 1)
                            mm3(ps[:, 6 + dt, :], (cn_h[s][:, k, w], cn_l[s][:, k, w]),
                                (pt_h[:, k, :], pt_l[:, k, :]), k == 0, False)
                        if dt == 0:
                            pe.wait_ge(pt_hi, g * (3 * GB) + 3 * b + 3)
                        mm(ps[:, 6 + dt, :], c3[s][0:3, w], pl3[0:3, :], start=False, stop=True
                           ).then_inc(u_made, 1)

                scores(0)
                for b in range(GB):
                    probs_t(b)
                    if b + 1 < GB:
                        scores(b + 1)
                    attend(b)
                pe.wait_ge(u_lo, g * (2 * GB) + 2 * GB)
                for i in range(4):
                    for k in range(2):
                        hp = 2 * i + k
                        for j in range(2):
                            w = slice(DK * j, DK * j + P)
                            for kc in range(KC):
                                ins = mm3(ps[:, i, k * GR:(k + 1) * GR], (wv_h[:, kc, hp, w], wv_l[:, kc, hp, w]),
                                          (head(qu_h, 2 * hp + j)[:, kc], head(qu_l, 2 * hp + j)[:, kc]),
                                          j == 0 and kc == 0, j == 1 and kc == 1)
                    ins.then_inc(made, 1)
                pe.wait_ge(drained, g * NU + U_ATT + 4)
                for r in range(RT):
                    w = slice(r * P, (r + 1) * P)
                    for hp in range(HP):
                        ins = mm3(ps[:, B_(U_O), r * D:(r + 1) * D], (at_h[:, hp, w], at_l[:, hp, w]),
                                  (wo_h[:, hp, :], wo_l[:, hp, :]), hp == 0, hp == HP - 1)
                ins.then_inc(made, 1)
                pe.wait_ge(xn_ready, 2 * RT * g + 2 * RT)
                transposes(U_XN2, B_(U_XN2), xn2)
                pe.wait_ge(drained, g * NU + U_XN2 + 1)
                for j, u in enumerate((U_LQ, U_LK)):
                    for et in range(KC):
                        w = slice(et * P, (et + 1) * P)
                        for kc in range(KC):
                            ins = mm3(ps[:, B_(u), et * GR:(et + 1) * GR], (lw_h[:, j, kc, w], lw_l[:, j, kc, w]),
                                      (x2_h[:, kc, :], x2_l[:, kc, :]), kc == 0, kc == 1)
                    ins.then_inc(made, 1)
                reuse(U_V)
                for r in range(RT):
                    w = slice(r * P, (r + 1) * P)
                    for kc in range(KC):
                        ins = mm3(ps[:, B_(U_V), r * D:(r + 1) * D], (x2_h[:, kc, w], x2_l[:, kc, w]),
                                  (lw_h[:, 2, kc, :], lw_l[:, 2, kc, :]), kc == 0, kc == 1)
                ins.then_inc(made, 1)
                pe.wait_ge(f_ready, g * 5 + 5)
                for r in range(RT):
                    for j in range(4):
                        u = U_SC + 4 * r + j
                        reuse(u)
                        for i in range(2):
                            et, quad = i, j
                            rows = slice(32 * quad, 32 * quad + 32)
                            w = slice(r * P, (r + 1) * P)
                            ins = mm3(ps[:, B_(u), i * 2 * P:(i + 1) * 2 * P],
                                      (k_h[rows, et, w], k_l[rows, et, w]),
                                      (qx_h[rows, et, :, w], qx_l[rows, et, :, w]), True, True)
                        ins.then_inc(made, 1)
                for r in range(RT):
                    u = U_PV + r
                    pe.wait_ge(drained, g * NU + U_SC + 4 * r + 4)
                    reuse(u)
                    for h in range(LH):
                        ins = mm(ps[:, B_(u), h * LV:(h + 1) * LV], am[:, r, h, :], vaug[:, r, h, :],
                                 start=True, stop=True)
                    ins.then_inc(made, 1)
                pe.wait_ge(drained, g * NU + U_PV + RT)
                transposes(U_OT, B_(U_OT), lo)
                pe.wait_ge(drained, g * NU + U_OT + 1)
                for r in range(RT):
                    w = slice(r * P, (r + 1) * P)
                    for kc in range(KC):
                        ins = mm3(ps[:, B_(U_Y), r * D:(r + 1) * D], (ot_h[:, kc, w], ot_l[:, kc, w]),
                                  (lw_h[:, 3, kc, :], lw_l[:, 3, kc, :]), kc == 0, kc == 1)
                ins.then_inc(made, 1)

            for i in range(4):
                kc, half = i // 2, i % 2
                for r in range(4):
                    if i < 2:
                        pe.wait_ge(fxn_ready, 4 * half + r + 1)
                    ins = nc.tensor.transpose(ps[:, i, r * P:(r + 1) * P],
                                              fxn[:, 4 * half + r, kc * P:(kc + 1) * P], ident[:])
                ins.then_inc(ftr, 1)
            pe.wait_ge(ftl, 4)
            for t in range(TILES):
                w = slice(t * P, (t + 1) * P)
                for kc in range(KC):
                    ins = mm3(ps[:, 4, t * E:(t + 1) * E], (ft_h[:, kc, w], ft_l[:, kc, w]),
                              (gate_h[:, kc, :], gate_l[:, kc, :]), kc == 0, kc == 1)
            ins.then_inc(logit_made, 1)
            pe.wait_ge(comb_ready, 1)
            for t in range(TILES):
                ins = nc.tensor.transpose(ps[0:E, 6 + t // 4, (t % 4) * P:(t % 4 + 1) * P], comb[:, t, :], ident[:])
                if t % 4 == 3:
                    ins.then_inc(combT_made, 1)
            pe.wait_ge(combT_sb, 2)

            def down(i, s, es, start=False, stop=False):
                rows, tile, half = rows_of(s), s // 2, s % 2
                pe.wait_ge(h_lo, i + 1)
                for dt in range(KC):
                    w = slice(2 * KC * FE + tile * D + dt * P, 2 * KC * FE + tile * D + (dt + 1) * P)
                    ps_ = ps[:, 2 * dt + half, :]
                    x = (hh[s % 2][0:rows], hl[s % 2][0:rows])
                    mm(ps_, fw_h[es][0:rows, w], x[0], start=start, stop=False, skip_group_check=True)
                    mm(ps_, fw_h[es][0:rows, w], x[1], start=False, stop=False, skip_group_check=True)
                    ins = mm(ps_, fw_l[es][0:rows, w], x[0], start=False, stop=stop, skip_group_check=True)
                ins.then_inc(down_done, 1)

            def unit(i, s, e=None, es=0):
                tile, half = s // 2, s % 2
                f0, rows = FT[tile]
                if s == 0:
                    pe.wait_ge(fw_split, 2 * e + 2)
                if not isinstance(i, int) or i >= 2:
                    pe.wait_ge(h_lo, i - 1)
                for gu in range(2):
                    for kc in range(KC):
                        w = slice(gu * KC * FE + kc * FE + f0, gu * KC * FE + kc * FE + f0 + rows)
                        tok = slice(half * HALF, (half + 1) * HALF)
                        ins = mm3(ps[0:rows, 4 + 2 * (s % 2) + gu, :], (fw_h[es][:, w], fw_l[es][:, w]),
                                  (ft_h[:, kc, tok], ft_l[:, kc, tok]), kc == 0, kc == 1)
                    ins.then_inc(gu_made, 1)
                if not isinstance(i, int) or i >= 1:
                    ps_, pes = (s - 1, es) if s else (5, 1 - es)
                    down(i - 1, ps_, pes, start=isinstance(i, int) and i <= 2)

            for_units(pe, unit, with_expert=True, with_slot=True)
            down(NUNITS - 1, 5, 1, stop=True)
            pe.wait_ge(fo_ready, 4)
            for r in range(TILES):
                for dt in range(KC):
                    ins = nc.tensor.transpose(ps[:, 4 + r // 2, (r % 2) * D + dt * P:(r % 2) * D + (dt + 1) * P],
                                              fo[:, dt, r * P:(r + 1) * P], ident[:])
                if r % 2:
                    ins.then_inc(fy_made, 1)


def kernel(**inputs):
    import numpy as _np
    import concourse.bacc as _bacc
    from concourse import mybir as _mybir
    from concourse.bass_utils import run_bass_kernel_spmd as _run

    x = {k: _np.ascontiguousarray(v) for k, v in inputs.items()}

    def in_chunks(w):
        return w.reshape(w.shape[0] // 128, 128, w.shape[1]).transpose(1, 0, 2)

    ctx = x["ctx_1024"]
    ctxT = _np.zeros((32, 128, 2, 258), ctx.dtype)
    ctxT[:, :, :, 0:257] = ctx.transpose(0, 2, 1).reshape(32, 2, 128, 257).transpose(0, 2, 1, 3)

    def expert(gate, up, down):
        d = _np.zeros((128, 3, 256), down.dtype)
        for t in range(3):
            part = down[128 * t:min(128 * (t + 1), 352)]
            d[0:len(part), t] = part
        return _np.concatenate([in_chunks(gate).reshape(128, -1), in_chunks(up).reshape(128, -1),
                                d.reshape(128, -1)], axis=1)

    p = "L0_ffn_"
    ffn = [expert(x[p + "sw_gate"][:, 352 * j:352 * (j + 1)], x[p + "sw_up"][:, 352 * j:352 * (j + 1)],
                  x[p + "sw_down"][352 * j:352 * (j + 1)]) for j in range(2)]
    ffn += [expert(x[p + "w_gate"][e], x[p + "w_up"][e], x[p + "w_down"][e]) for e in range(8)]
    p = "L0_xattn_"
    laid = {
        "x": x["x"].reshape(1024, 256),
        "ctx": ctx,
        "ctxT": ctxT,
        "wqn": in_chunks(x[p + "Wq"]),
        "wqT": in_chunks(x[p + "Wq"].T),
        "wk": in_chunks(x[p + "Wk"]),
        "wvT": in_chunks(x[p + "Wv"].T).reshape(128, 2, 8, 128),
        "woT": in_chunks(x[p + "Wo"].T),
        "bq": x[p + "bq"].reshape(8, 128).T,
        "bk": x[p + "bk"].reshape(8, 128).T,
        "bv": x[p + "bv"].reshape(8, 128).T,
        "bo": x[p + "bo"],
        "lwT": _np.stack([in_chunks(x["L0_attn_" + w].T) for w in ("Wq", "Wk", "Wv", "Wo")], axis=1),
        "gateT": in_chunks(x["L0_ffn_gate_w"].T),
        "ffn": _np.stack(ffn),
    }
    nc = _bacc.Bacc("TRN2", target_bir_lowering=False, num_devices=1)
    arrays, aps = {}, {}
    for name, v in laid.items():
        v = _np.ascontiguousarray(v)
        arrays[f"in_{name}"] = v
        aps[name] = nc.dram_tensor(f"in_{name}", v.shape, _mybir.dt.from_np(v.dtype), kind="ExternalInput").ap()
    out = nc.dram_tensor("out_0", (1024, 256), _mybir.dt.float32, kind="ExternalOutput").ap()
    build(nc, aps, out)
    r = _run(nc, [arrays], core_ids=[0])
    return r.results[0]["out_0"].reshape(32, 32, 256)
```

```python
from contextlib import ExitStack

import numpy as np
import concourse.bass as bass
from concourse import mybir

F32 = mybir.dt.float32
F32R = mybir.dt.float32r
ALU = mybir.AluOpType
ACT = mybir.ActivationFunctionType
AX = mybir.AxisListType

P = 128
D = 256
KC = D // P
B, T = 32, 32
NK = 257
NKP = NK + 1
H, DK = 16, 64
HP = H // 2
LH, LD = 16, 16
LV = LD + 2
GB = 8
NG = B // GB
GR = GB * T
RT = GR // P
ROWS = B * T
TILES = ROWS // P
E, FE = 8, 352
NX = 10
FT = [(0, 128), (128, 128), (256, 96)]
FW = 2 * KC * FE + len(FT) * D
HALF = 512
SCALE = 1.0 / 8.0
LN_EPS = 1e-5
EPS = 1e-6
ROUTE_SCALE = 2.5

U_Q, U_QP, U_ATT, U_O = 0, 4, 20, 24
NU = 25
NEXT = ("xn1", "qb")
LINEAR = ("xn2", "lq", "lk", "v", "sc0", "pv0", "sc1", "pv1", "ot", "y")
FULL = LINEAR + ("xn1", "xn3", "log", "qb", "ct")
LAST = LINEAR + ("xn3", "log", "ct")
WITH_HIGH = ("xn1", "xn2", "lq", "lk", "ot", "xn3")
TAIL = 2 * GB
SLOT = {"xn2": 0, "lq": 1, "lk": 2, "v": 3, "sc0": 6, "pv0": 7, "sc1": 8, "pv1": 9, "ot": 10, "y": 11,
        "xn1": 13, "xn3": 14, "log": 15, "qb": TAIL, "ct": TAIL}


class Side:

    def __init__(self, units, base, base_high):
        self.units, self.base, self.base_high = units, base, base_high
        self.highs = [u for u in units if u in WITH_HIGH]

    def count(self, u):
        return self.base + self.units.index(u) + 1

    def before(self, u):
        return self.base + self.units.index(u)

    def high(self, u):
        return self.base_high + self.highs.index(u) + 1

    def at(self, slot):
        return [u for u in self.units if SLOT[u] == slot]


def side_of(g):
    if isinstance(g, int):
        assert g == 0
        return Side(NEXT, len(NEXT), 1)
    return Side(FULL, (g - 1) * len(FULL) + 2 * len(NEXT), (g - 1) * 6 + 2)


FIRST_SIDE = Side(NEXT, 0, 0)
LAST_SIDE = Side(LAST, (NG - 1) * len(FULL) + 2 * len(NEXT), (NG - 1) * 6 + 2)


class Steps:

    def __init__(self, eng, sem, base=0):
        self.eng, self.sem, self.base, self.n = eng, sem, base, 0

    def add(self, ins):
        ins.then_inc(self.sem, 1)
        self.n += 1

    def wait(self):
        self.eng.wait_ge(self.sem, self.base + self.n)

    def link(self, ins):
        self.add(ins)
        self.wait()


def build(nc, a, out):
    ctx = ExitStack()
    with ctx:
        def sem(name):
            return ctx.enter_context(nc.semaphore(name))

        place = {"at": 16512}

        def at(offset, name, shape, dt):
            return nc.alloc_sbuf_tensor_at(name, shape, dt, offset=offset)

        def sb(name, shape, dt):
            offset = place["at"]
            place["at"] = (offset + int(np.prod(shape[1:])) * 4 + 31) // 32 * 32
            return at(offset, name, shape, dt)

        ident = sb("ident", [P, P], F32)
        causal = sb("causal", [P, T], F32)
        of_head = sb("of_head", [P, LH // KC], F32)
        zero = sb("zero", [P, 1], F32)
        minus_half = sb("minus_half", [P, 1], F32)
        lower = sb("lower", [P, E, E], F32)
        bq_sb = sb("bq_sb", [P, HP], F32)
        bv_sb = sb("bv_sb", [P, HP], F32)
        bo_sb = sb("bo_sb", [P, D], F32)
        gate_h = sb("gate_h", [P, KC, E], F32R)
        gate_l = sb("gate_l", [P, KC, E], F32R)
        stats = sb("stats", [P, RT, 6], F32)
        mv = sb("mv", [P, RT, 2], F32)
        lnt = sb("lnt", [P, 4, RT], F32)
        rl = sb("rl", [P, RT, E], F32)
        rsm = sb("rsm", [P, 4, RT], F32)
        rank = sb("rank", [P, RT, E], F32)
        comb = sb("comb", [P, RT, E], F32)
        PHASE = place["at"]
        bqk = sb("bqk", [H, 1], F32)
        wqb_h = sb("wqb_h", [P, KC, H], F32R)
        wqb_l = sb("wqb_l", [P, KC, H], F32R)
        wq_h = sb("wq_h", [P, KC, H * DK], F32R)
        wq_l = sb("wq_l", [P, KC, H * DK], F32R)
        wk_h = sb("wk_h", [P, HP, D], F32R)
        wk_l = sb("wk_l", [P, HP, D], F32R)
        wv_h = sb("wv_h", [P, KC, HP, 3 * DK], F32R)
        wv_l = sb("wv_l", [P, KC, HP, 3 * DK], F32R)
        wo_h = sb("wo_h", [P, HP, D], F32R)
        wo_l = sb("wo_l", [P, HP, D], F32R)
        lw_h = sb("lw_h", [P, 4, KC, D], F32R)
        lw_l = sb("lw_l", [P, 4, KC, D], F32R)
        xg = sb("xg", [P, RT, D], F32)
        xn = sb("xn", [P, RT, D], F32)
        qbt = sb("qbt", [P, 4, GB], F32)
        qbs = sb("qbs", [P, 4, GB], F32)
        vaug = sb("vaug", [P, RT, LH, LV], F32)
        den = sb("den", [P, 2, RT, LH], F32)
        mxq = sb("mxq", [P, 3, 4], F32)
        psum_e = sb("psum_e", [P, 4], F32)
        rsum = sb("rsum", [P, 4], F32)
        SF = place["at"]
        fm = sb("fm", [P, 2, KC, GR], F32)
        combT = at(SF, "combT", [E, GR], F32)
        qb_sb = at(SF + 1024, "qb_sb", [H, GR], F32)
        SA = place["at"]
        x2s = at(SA, "x2s", [P, 2, KC, GR], F32R)
        am = at(SA, "am", [P, RT, LH, T], F32)
        SB = SA + 4096
        fa = at(SB, "fa", [P, 2, KC, GR], F32)
        ot_h = at(SB, "ot_h", [P, KC, GR], F32R)
        ot_l = at(SB + 2048, "ot_l", [P, KC, GR], F32R)
        rgt = at(SB, "rgt", [P, RT, E, E], F32)
        req = at(SB + 512, "req", [P, RT, E, E], F32)
        SC = SB + 4096
        qx = [at((SB, SC)[et], f"qx{et}", [P, LH // KC, P], F32) for et in range(KC)]
        x1_h = at(SC, "x1_h", [P, KC, GR], F32R)
        x1_l = at(SC + 2048, "x1_l", [P, KC, GR], F32R)
        place["at"] = SC + 4096
        cn_raw = sb("cn_raw", [P, 2, D], F32)
        ct_raw = sb("ct_raw", [P, KC, NKP], F32)
        cn_h = sb("cn_h", [P, 2, D], F32R)
        cn_l = sb("cn_l", [P, 2, D], F32R)
        ct_h = sb("ct_h", [P, KC, NKP], F32R)
        ct_l = sb("ct_l", [P, KC, NKP], F32R)
        c3 = [sb(f"c3_{s}", [3, D], F32R) for s in range(2)]
        RA = place["at"]
        q_h = at(RA, "q_h", [P, HP, GR], F32R)
        q_l = at(RA + 8192, "q_l", [P, HP, GR], F32R)
        pt_h = at(RA, "pt_h", [P, 2, 512], F32R)
        pt_l = at(RA + 4096, "pt_l", [P, 2, 512], F32R)
        pr = at(RA + 8192, "pr", [P, 4, NKP], F32)
        pl3 = at(RA + 12320, "pl3", [3, 512], F32R)
        l3 = at(RA + 14368, "l3", [P, 4, 3], F32R)
        at_h = at(RA, "at_h", [P, HP, GR], F32R)
        at_l = at(RA + 8192, "at_l", [P, HP, GR], F32R)
        RB = RA + 16384
        qu_h = at(RB, "qu_h", [P, KC, GB, H * T], F32R)
        qu_l = at(RB + 32768, "qu_l", [P, KC, GB, H * T], F32R)
        END = RB + 65536
        wq_raw = at(RB, "wq_raw", [P, KC, H * DK], F32)
        wqn_raw = at(RB + 8192, "wqn_raw", [P, HP, D], F32)
        wk_raw = at(RB + 16384, "wk_raw", [P, HP, D], F32)
        wv_raw = at(RB + 24576, "wv_raw", [P, KC, HP, P], F32)
        wo_raw = at(RB + 32768, "wo_raw", [P, HP, D], F32)
        lw_raw = at(RB + 40960, "lw_raw", [P, 4, KC, D], F32)
        cl_raw = at(RB + 49152, "cl_raw", [B, D], F32)
        cl_h = at(RB + 50176, "cl_h", [B, D], F32R)
        cl_l = at(RB + 51200, "cl_l", [B, D], F32R)
        bk_sb = at(RB + 52224, "bk_sb", [P, HP], F32)
        bkd = at(RB + 52288, "bkd", [P, HP, H], F32)
        wqb = at(RB + 52800, "wqb", [P, KC, H], F32)
        gateT = at(RB + 52928, "gateT", [P, KC, E], F32)
        assert END <= nc.sbuf_usable_end, (END, nc.sbuf_usable_end)

        place["at"] = RA
        fts = sb("fts", [P, 2, KC, ROWS], F32R)
        fw_raw = [sb(f"fw_raw{s}", [P, FW], F32) for s in range(2)]
        fw_h = [sb(f"fw_h{s}", [P, FW], F32R) for s in range(2)]
        fw_l = [sb(f"fw_l{s}", [P, FW], F32R) for s in range(2)]
        assert place["at"] <= nc.sbuf_usable_end, place["at"]
        place["at"] = PHASE
        combB = sb("combB", [P, E, ROWS], F32)
        fx = sb("fx", [P, TILES, D], F32)
        sg = [sb(f"sg{s}", [P, HALF], F32) for s in range(2)]
        hm = [sb(f"hm{s}", [P, HALF], F32) for s in range(2)]
        hh = [sb(f"hh{s}", [P, HALF], F32R) for s in range(2)]
        hl = [sb(f"hl{s}", [P, HALF], F32R) for s in range(2)]
        fo = sb("fo", [P, KC, ROWS], F32)
        fy = sb("fy", [P, TILES, D], F32)
        assert place["at"] <= SA, place["at"]

        ps = ctx.enter_context(nc.psum_tensor("ps", [P, 8, 512], F32))
        UB, SIDE = 6, 7

        c3_d = nc.dram_tensor("c3_scratch", [B, 3, D], F32).ap()
        qb_d = nc.dram_tensor("qb_scratch", [NG + 1, H, GR], F32).ap()
        x2_d = nc.dram_tensor("x2_scratch", [ROWS, D], F32).ap()
        ft_d = nc.dram_tensor("xt_scratch", [NG, P, 2, KC, GR], F32).ap()
        cb_d = nc.dram_tensor("comb_scratch", [NG, E, GR], F32).ap()

        def bank3(i, n):
            return ps[:, i, :].rearrange("p (n c) -> p n c", n=n)

        def head(t, h):
            return t[:, :, :, T * h:T * h + T]

        def by_batch(ap):
            return ap.rearrange("p k (b q) -> p k b q", q=T)

        def rows_of(s):
            return FT[s // 2][1]

        def diag(ap, j):
            flat = ap.rearrange("p a h -> p (a h)")
            return flat[:, j:j + (HP - 1) * (H + 2) + 1:H + 2]

        def groups(eng, body):
            body(0)
            with eng.Fori(1, NG) as g:
                body(g)

        def for_units(eng, unit, routed=None, with_expert=False, with_slot=False):
            def one(i, s, e, es, is_routed):
                if with_slot:
                    unit(i, s, e, es)
                elif with_expert:
                    unit(i, s, e if is_routed else None)
                else:
                    unit(i, s)

            for e in range(2):
                for s in range(6):
                    one(6 * e + s, s, e, e, False)
            if routed:
                routed()
            with eng.Fori(0, E // 2) as j:
                for es in range(2):
                    for s in range(6):
                        e = j * 2 + es
                        one(j * 12 + 12 + 6 * es + s, s, e + 2 if with_slot else e, es, True)

        const_ld = sem("const_loaded")
        weight_ld = [sem(f"weight_loaded{i}") for i in range(6)]
        mask_ready = sem("mask_ready")
        setup_pe = sem("setup_pe")
        setup_dve = sem("setup_dve")
        whi = sem("weight_high")
        wlo = sem("weight_low")
        c3_stored = sem("c3_stored")
        xn_ld = sem("next_rows_loaded")
        xg_ld = sem("residual_rows_loaded")
        ln_var = sem("ln_var_ready")
        ln_y = sem("ln_guess_ready")
        xn_ready = sem("xn_ready")
        made = sem("unit_made")
        high = sem("unit_high")
        drained = sem("unit_drained")
        side_made = sem("side_unit_made")
        side_high = sem("side_unit_high")
        side_drained = sem("side_unit_drained")
        qb_stored = sem("qb_stored")
        qb_ld = sem("qb_loaded")
        ct_ld = sem("context_transposed_loaded")
        cn_ld = sem("context_loaded")
        c3_ld = [sem(f"c3_loaded{s}") for s in range(2)]
        ct_split = sem("context_transposed_split")
        cn_split = sem("context_split")
        scores_made = sem("scores_made")
        bias_ready = sem("exp_bias_ready")
        exp_done = sem("exp_done")
        sum_ready = sem("exp_sum_inverted")
        p_ready = sem("probs_ready")
        l3_ready = sem("last_key_ready")
        pt_made = sem("probs_transposed")
        pt_hi = sem("probs_high")
        pt_lo = sem("probs_low")
        u_made = sem("attended_made")
        u_hi = sem("attended_high")
        u_lo = sem("attended_low")
        act_steps = sem("feature_exp_done")
        dve_steps = sem("dve_steps")
        f_ln = sem("feature_log_ready")
        f_sum = sem("features_ready")
        f_ready = sem("head_queries_ready")
        logit_sub = sem("logits_less_max")
        logit_exp = sem("logits_exp")
        comb_ready = sem("comb_ready")
        x2_stored = sem("x2_stored")
        x3_stored = sem("xt_stored")
        cb_stored = sem("comb_stored")
        ft_ld = sem("ffn_xT_loaded")
        fx_ld = sem("ffn_x_loaded")
        comb_ld = sem("comb_loaded")
        fw_ld = [sem(f"ffn_weights_loaded{s}") for s in range(2)]
        fw_split = sem("ffn_weights_split")
        gu_made = sem("gate_up_made")
        silu_done = sem("silu_done")
        h_mid = sem("h_unweighted_done")
        h_done = sem("h_done")
        h_hi = sem("h_high")
        h_lo = sem("h_low")
        down_done = sem("down_done")
        fo_ready = sem("ffn_sum_copied")
        fy_made = sem("ffn_rows_made")
        fy_ready = sem("ffn_rows_ready")
        stored = sem("out_stored")

        def f32(ap):
            return ap.bitcast(F32)

        N_CONST = 5
        SHARED = 12
        NUNITS = 6 * NX
        MASKS = 11
        HIGH_OF = {u: u + 1 for u in range(U_O)}
        N_HIGH = U_O
        DVE_FIRST, DVE_0, DVE_G = 9, 60, 97
        ACT_G = 1
        LN = (1, 4)

        def dve_base(g):
            return DVE_FIRST if isinstance(g, int) else (g - 1) * DVE_G + DVE_FIRST + DVE_0

        def ln_base(g):
            return 1 if isinstance(g, int) else (g - 1) * 3 + 2

        LN_LAST = 2 + 3 * (NG - 1)

        block = ctx.enter_context(nc.Block())

        @block.sync
        def _(sp):
            sp.dma_start(bq_sb[:], a["bq"]).then_inc(const_ld, 16)
            sp.dma_start(bk_sb[:], a["bk"]).then_inc(const_ld, 16)
            sp.dma_start(bv_sb[:], a["bv"]).then_inc(const_ld, 16)
            sp.dma_start(bo_sb[:], a["bo"].partition_broadcast(P)).then_inc(const_ld, 16)
            sp.dma_start(gateT[:], a["gateT"]).then_inc(const_ld, 16)
            sp.dma_start(xn[:], a["x"][0:GR, :].rearrange("(r p) d -> p r d", p=P)).then_inc(xn_ld, 16)
            sp.dma_start(wqn_raw[:], a["wqn"]).then_inc(weight_ld[0], 16)
            sp.dma_start(cl_raw[:], a["ctx"][:, NK - 1, :]).then_inc(weight_ld[0], 16)
            sp.dma_start(wq_raw[:], a["wqT"]).then_inc(weight_ld[1], 16)
            sp.dma_start(wk_raw[:], a["wk"]).then_inc(weight_ld[2], 16)
            sp.dma_start(wv_raw[:], a["wvT"]).then_inc(weight_ld[3], 16)
            sp.dma_start(wo_raw[:], a["woT"]).then_inc(weight_ld[4], 16)
            sp.dma_start(lw_raw[:], a["lwT"]).then_inc(weight_ld[5], 16)
            sp.dma_start(xg[:], a["x"][0:GR, :].rearrange("(r p) d -> p r d", p=P)).then_inc(xg_ld, 16)
            sp.wait_ge(wlo, 1)
            for j, src in enumerate((cl_h, cl_h, cl_l)):
                sp.dma_start(c3_d[:, j, :], f32(src[:])).then_inc(c3_stored, 16)
            sp.wait_ge(c3_stored, 48)
            with sp.Fori(0, NG) as g:
                sp.wait_ge(qb_stored, 16 * (g + 1))
                for f in range(4):
                    sp.dma_start(qbt[T * f:T * f + T, :, :],
                                 qb_d[bass.ds(g, 1)].rearrange("o (t f) (q b) -> (o f) q t b", f=4, b=GB)[f]
                                 ).then_inc(qb_ld, 16)
                for b in range(GB + 1):
                    n = g * GB + b
                    if b < GB:
                        sp.wait_ge(ct_split, 2 * n + 2)
                        sp.dma_start(ct_raw[:], a["ctxT"][bass.ds(n, 1)].rearrange("o p k c -> p (o k) c")
                                     ).then_inc(ct_ld, 16)
                    if b > 0:
                        sp.wait_ge(cn_split, 2 * n)
                        sp.dma_start(cn_raw[:], a["ctx"][bass.ds(n - 1, 1), 0:2 * P, :].rearrange(
                            "o (k p) d -> p (o k) d", p=P)).then_inc(cn_ld, 16)
                        s = (b - 1) % 2
                        sp.wait_ge(u_made, 2 * n)
                        sp.dma_start(f32(c3[s][:]), c3_d[bass.ds(n - 1, 1)].rearrange("o j d -> (o j) d")
                                     ).then_inc(c3_ld[s], 16)
            sp.wait_ge(drained, NG * NU)
            for e in range(2):
                sp.dma_start(fw_raw[e][:], a["ffn"][e]).then_inc(fw_ld[e], 16)
            for g in range(NG):
                sp.wait_ge(x3_stored, 16 * (g + 2))
                for k in range(2):
                    sp.dma_start(f32(fts[:, k, :, g * GR:(g + 1) * GR]), ft_d[g, :, k]).then_inc(ft_ld, 16)
            sp.wait_ge(x2_stored, 16 * (NG + 1))
            sp.dma_start(fx[:], x2_d.rearrange("(r p) d -> p r d", p=P)).then_inc(fx_ld, 16)
            sp.wait_ge(cb_stored, 16 * (NG + 1))
            for e in range(E):
                sp.dma_start(combB[:, e, :].rearrange("p (g t) -> p g t", g=NG),
                             cb_d[:, e, :].partition_broadcast(P)).then_inc(comb_ld, 16)
            with sp.Fori(0, E // 2) as j:
                for s in range(2):
                    e = j * 2 + s
                    sp.wait_ge(fw_split, 2 * (e + 1))
                    sp.dma_start(fw_raw[s][:], a["ffn"][bass.ds(e + 2, 1)].rearrange("o p w -> p (o w)")
                                 ).then_inc(fw_ld[s], 16)
            for h in range(2):
                sp.wait_ge(fy_ready, 4 * (h + 1))
                sp.dma_start(out[h * HALF:(h + 1) * HALF, :].rearrange("(r p) d -> p r d", p=P),
                             fy[:, 4 * h:4 * h + 4, :]).then_inc(stored, 16)
            sp.wait_ge(stored, 32)

        @block.gpsimd
        def _(pool):
            def round_high(dst, src):
                return nc.gpsimd.tensor_tensor(dst, src, zero[:, 0:1].broadcast_to(list(src.shape)), ALU.add)

            st = Steps(pool, mask_ready)
            st.link(nc.gpsimd.memset(zero[:], 0.0))
            st.link(nc.gpsimd.memset(minus_half[:], -0.5))
            st.link(nc.gpsimd.memset(ident[:], 0.0))
            st.link(nc.gpsimd.affine_select(out=ident[:], in_=ident[:], compare_op=ALU.not_equal, fill=1.0,
                                            base=0, pattern=[[-1, P]], channel_multiplier=1))
            st.link(nc.gpsimd.memset(causal[:], 1.0))
            for b4 in range(4):
                st.link(nc.gpsimd.affine_select(
                    out=causal[T * b4:T * b4 + T, :], in_=causal[T * b4:T * b4 + T, :],
                    compare_op=ALU.is_ge, fill=0.0, base=0, pattern=[[1, T]], channel_multiplier=-1))
            st.link(nc.gpsimd.memset(lower[:], 1.0))
            st.link(nc.gpsimd.affine_select(out=lower[:], in_=lower[:], compare_op=ALU.is_gt, fill=0.0,
                                            base=0, pattern=[[1, E], [-1, E]], channel_multiplier=0))
            for t in (wv_h, wv_l):
                nc.gpsimd.memset(f32(t[:, :, :, DK:2 * DK]), 0.0).then_inc(ct_split, 1)
            nc.gpsimd.memset(vaug[:, :, :, LD:LD + 1], 1.0).then_inc(cn_split, 2)
            nc.gpsimd.memset(vaug[:, :, :, LD + 1:LV], 0.0).then_inc(scores_made, 4)
            nc.gpsimd.memset(combT[:], 0.0).then_inc(u_made, 4)
            nc.gpsimd.memset(rsm[:], 0.0).then_inc(x2_stored, 16)
            nc.gpsimd.memset(rank[:], 0.0).then_inc(x3_stored, 16)
            nc.gpsimd.memset(comb[:], 0.0).then_inc(cb_stored, 16)

            def root(n):
                pool.wait_ge(ln_var, n)
                nc.gpsimd.tensor_tensor(lnt[:, 2, :], lnt[:, 0, :], minus_half[:, 0:1].broadcast_to([P, RT]),
                                        ALU.pow).then_inc(ln_y, 1)

            def head_queries(r, g, side):
                pool.wait_ge(f_sum, g + 1)
                if r:
                    pool.wait_ge(side_made, side.count("sc0"))
                nc.gpsimd.tensor_tensor(qx[1][:], fm[:, 0, 1, None, r * P:(r + 1) * P].broadcast_to([P, LH // KC, P]),
                                        of_head[:, :, None].broadcast_to([P, LH // KC, P]), ALU.mult
                                        ).then_inc(f_ready, 1)

            def split_ct(n):
                pool.wait_ge(ct_ld, 16 * (n + 1))
                pool.wait_ge(scores_made, 4 * n + 4)
                flat = [t[:].rearrange("p k c -> p (k c)") for t in (ct_h, ct_l, ct_raw)]
                round_high(flat[0], flat[2]).then_inc(ct_split, 1)
                pool.wait_ge(ct_split, 2 * n + 3)
                nc.gpsimd.tensor_tensor(flat[1], flat[2], f32(flat[0]), ALU.subtract).then_inc(ct_split, 1)

            def split_cn(n):
                pool.wait_ge(cn_ld, 16 * (n + 1))
                pool.wait_ge(u_made, 2 * n + 4)
                flat = [t[:].rearrange("p k c -> p (k c)") for t in (cn_h, cn_l, cn_raw)]
                round_high(flat[0], flat[2]).then_inc(cn_split, 1)
                pool.wait_ge(cn_split, 2 * n + 3)
                nc.gpsimd.tensor_tensor(flat[1], flat[2], f32(flat[0]), ALU.subtract).then_inc(cn_split, 1)

            root(1)

            def group(g):
                side = side_of(g)
                ln = ln_base(g)
                full = len(side.units) > 2
                if full:
                    root(ln + 1)
                    ln = ln + 1
                split_ct(g * GB)
                split_cn(g * GB)
                split_ct(g * GB + 1)
                for b in range(GB):
                    n = g * GB + b
                    if b + 2 < GB:
                        split_ct(n + 2)
                    if b == 3 and full:
                        head_queries(0, g - 1, side)
                    if b == 4 and full:
                        head_queries(1, g - 1, side)
                    if b == 6:
                        root(ln + 1)
                        if full:
                            root(ln + 2)
                    if b + 1 < GB:
                        split_cn(n + 1)

            groups(pool, group)
            root(LN_LAST + 1)
            def split(e, s, turn):
                pool.wait_ge(fw_ld[s], 16 * turn)
                if not isinstance(e, int):
                    pool.wait_ge(down_done, 6 * (e - 1))
                round_high(fw_h[s][:], fw_raw[s][:]).then_inc(fw_split, 1)
                pool.wait_ge(fw_split, 2 * e + 1)
                nc.gpsimd.tensor_tensor(fw_l[s][:], fw_raw[s][:], f32(fw_h[s][:]), ALU.subtract
                                        ).then_inc(fw_split, 1)

            head_queries(0, NG - 1, LAST_SIDE)
            head_queries(1, NG - 1, LAST_SIDE)
            split(0, 0, 1)
            root(LN_LAST + 2)
            split(1, 1, 1)
            with pool.Fori(0, E // 2) as j:
                for s in range(2):
                    split(j * 2 + s + 2, s, j + 2)

        @block.scalar
        def _(act):
            def copy(dst, src):
                return nc.scalar.activation(dst, src, ACT.Identity)

            act.wait_ge(weight_ld[0], 32)
            copy(cl_h[:], cl_raw[:]).then_inc(whi, 1)
            act.wait_ge(const_ld, 16 * N_CONST)
            copy(gate_h[:], gateT[:]).then_inc(whi, 1)
            for i, (hi, raw) in enumerate((
                    (wq_h[:], wq_raw[:]), (wk_h[:], wk_raw[:]),
                    (wv_h[:, :, :, 0:DK], wv_raw[:, :, :, 0:DK]),
                    (wv_h[:, :, :, 2 * DK:3 * DK], wv_raw[:, :, :, DK:2 * DK]),
                    (wo_h[:], wo_raw[:]), (lw_h[:], lw_raw[:]))):
                act.wait_ge(weight_ld[(1, 2, 3, 3, 4, 5)[i]], 16)
                copy(hi, raw).then_inc(whi, 1)
            act.wait_ge(setup_dve, 4)
            copy(wqb_h[:], wqb[:]).then_inc(whi, 1)

            def side_unit(side, u, g):
                if u in WITH_HIGH:
                    act.wait_ge(side_made, side.count(u))
                src = bank3(SIDE, KC)
                if u == "xn1":
                    copy(x1_h[:], src).then_inc(side_high, 1)
                elif u == "qb":
                    act.wait_ge(side_drained, side.count(u))
                    act.dma_start(qb_d[bass.ds(g, 1)].rearrange("o h r -> (o h) r"), qb_sb[:]
                                  ).then_inc(qb_stored, 16)
                elif u == "xn2":
                    act.wait_ge(x3_stored, 16 * (g + 1))
                    copy(x2s[:, 0], src).then_inc(side_high, 1)
                elif u in ("lq", "lk"):
                    nc.scalar.activation(fa[:, int(u == "lk")], src, ACT.Abs).then_inc(side_high, 1)
                    if u == "lk":
                        act.wait_ge(side_high, side.high(u))
                        nc.scalar.activation(fa[:], fa[:], ACT.Exp, scale=-1.0).then_inc(act_steps, 1)
                elif u == "v":
                    act.wait_ge(act_steps, g + 1)
                    nc.scalar.activation(fa[:], fa[:], ACT.Ln, bias=1.0).then_inc(f_ln, 1)
                elif u == "ot":
                    copy(ot_h[:], src).then_inc(side_high, 1)
                elif u == "y":
                    act.wait_ge(side_drained, side.count(u))
                    act.dma_start(x2_d[bass.ds(g * GR, GR), :].rearrange("(r p) d -> p r d", p=P), xg[:]
                                  ).then_inc(x2_stored, 16)
                elif u == "xn3":
                    copy(x2s[:, 0], src).then_inc(side_high, 1)
                    act.wait_ge(side_drained, side.count(u))
                    act.dma_start(ft_d[bass.ds(g, 1)].rearrange("o p k c r -> p (o k c) r"),
                                  f32(x2s[:].rearrange("p k c r -> p (k c) r"))).then_inc(x3_stored, 16)
                elif u == "log":
                    act.wait_ge(logit_sub, g + 1)
                    nc.scalar.activation(rl[:], rl[:], ACT.Exp).then_inc(logit_exp, 1)
                elif u == "ct":
                    act.wait_ge(side_drained, side.count(u))
                    act.dma_start(cb_d[bass.ds(g, 1)].rearrange("o e r -> (o e) r"), combT[:]
                                  ).then_inc(cb_stored, 16)

            side_unit(FIRST_SIDE, "xn1", 0)
            side_unit(FIRST_SIDE, "qb", 0)

            def group(g):
                side = side_of(g)

                def high_part(u, dst, src, bias=None):
                    act.wait_ge(made, g * NU + u + 1)
                    for k in range(len(dst)):
                        ins = nc.scalar.activation(dst[k], src[k], ACT.Identity,
                                                   **({} if bias is None else {"bias": bias[k]}))
                    ins.then_inc(high, 1)

                for i in range(4):
                    high_part(U_Q + i, [q_h[:, 2 * i + k, :] for k in range(2)],
                              [bank3(U_Q + i, 2)[:, k, :] for k in range(2)],
                              [bq_sb[:, 2 * i + k:2 * i + k + 1] for k in range(2)])
                for h in range(H):
                    high_part(U_QP + h, [head(qu_h, h)], [by_batch(bank3(4 + h % 4, KC))])

                def exps(b, p):
                    if b and p == 0:
                        act.wait_ge(l3_ready, g * GB + b)
                    for t in (2 * p, 2 * p + 1):
                        act.wait_ge(bias_ready, g * (2 * GB) + 2 * b + p + 1)
                        nc.scalar.activation(pr[:, t, 0:NK], ps[:, t, 0:NK], ACT.Exp, bias=mxq[:, 2, t:t + 1],
                                             scale=SCALE, accum_out=psum_e[:, t:t + 1]).then_inc(exp_done, 1)

                def normalize(b):
                    for t in range(4):
                        act.wait_ge(sum_ready, g * (2 * GB) + 2 * b + t // 2 + 1)
                        nc.scalar.activation(pr[:, t, 0:NK], pr[:, t, 0:NK], ACT.Copy,
                                             scale=rsum[:, t:t + 1]).then_inc(p_ready, 1)

                def slot(k):
                    for u in side.at(k):
                        side_unit(side, u, g + 1 if u in NEXT else g - 1)
                    if k == 10:
                        if len(side.units) > 2:
                            act.wait_ge(side_made, side.count("ot"))
                        act.dma_start(xn[:], a["x"][bass.ds((g + 1) * GR, GR), :].rearrange(
                            "(r p) d -> p r d", p=P)).then_inc(xn_ld, 16)
                    if k == 15 and len(side.units) > 2:
                        act.wait_ge(x2_stored, 16 * (g + 1))
                        act.dma_start(xg[:], a["x"][bass.ds(g * GR, GR), :].rearrange(
                            "(r p) d -> p r d", p=P)).then_inc(xg_ld, 16)

                exps(0, 0)
                exps(0, 1)
                normalize(0)
                for b in range(GB):
                    for k in range(2):
                        act.wait_ge(pt_made, g * (3 * GB) + 3 * b + k + 1)
                        copy(pt_h[:, k, :], ps[:, 4 + k, :]).then_inc(pt_hi, 1)
                    act.wait_ge(pt_made, g * (3 * GB) + 3 * b + 3)
                    copy(pl3[:], ps[0:3, UB, :]).then_inc(pt_hi, 1)
                    if b + 1 < GB:
                        exps(b + 1, 0)
                        exps(b + 1, 1)
                    for dt in range(KC):
                        act.wait_ge(u_made, g * (2 * GB) + 4 + 2 * b + dt + 1)
                        copy(qu_h[:, dt, b, :], ps[:, UB, :]).then_inc(u_hi, 1)
                        slot(2 * b + dt)
                        if dt == 0 and b + 1 < GB:
                            normalize(b + 1)
                for i in range(4):
                    high_part(U_ATT + i, [at_h[:, 2 * i + k, :] for k in range(2)],
                              [bank3(i, 2)[:, k, :] for k in range(2)],
                              [bv_sb[:, 2 * i + k:2 * i + k + 1] for k in range(2)])
                slot(TAIL)

            act.wait_ge(c3_stored, 48)
            groups(act, group)
            for u in LAST:
                side_unit(LAST_SIDE, u, NG - 1)

            def unit(i, s):
                act.wait_ge(gu_made, 2 * i + 1)
                if not isinstance(i, int) or i >= 2:
                    act.wait_ge(h_done, i - 1)
                rows = rows_of(s)
                nc.scalar.activation(sg[s % 2][0:rows], ps[0:rows, 4 + 2 * (s % 2), :], ACT.Silu
                                     ).then_inc(silu_done, 1)
                act.wait_ge(h_done, i + 1)
                if not isinstance(i, int) or i >= 2:
                    act.wait_ge(down_done, i - 1)
                copy(hh[s % 2][0:rows], hm[s % 2][0:rows]).then_inc(h_hi, 1)

            for_units(act, unit)
            act.wait_ge(down_done, NUNITS)
            for r in (0, 2):
                copy(fo[:, r // 2, 0:HALF], ps[:, r, :]).then_inc(fo_ready, 1)

        @block.vector
        def _(dve):
            V = nc.vector
            st = Steps(dve, setup_dve)
            dve.wait_ge(const_ld, 16 * N_CONST)
            st.link(V.memset(bkd[:], 0.0))
            st.add(V.tensor_copy(diag(bkd[0:DK], 0), bk_sb[0:DK, :]))
            st.add(V.tensor_copy(diag(bkd[DK:P], 1), bk_sb[DK:P, :]))
            dve.wait_ge(mask_ready, MASKS)
            V.tensor_reduce(of_head[:], ident[:].rearrange("p (h c) -> p h c", c=LD), AX.X, ALU.add
                            ).then_inc(mask_ready, 1)
            dve.wait_ge(mask_ready, MASKS + 1)

            def row_stats(steps, x):
                for r in range(RT):
                    steps.add(V.bn_stats(stats[:, r, :], x[:, r, :]))
                steps.wait()
                steps.add(V.memset(lnt[:, 3, :], 0.0))
                for r in range(RT):
                    steps.add(V.bn_aggr(mv[:, r, :], stats[:, r, :]))
                steps.wait()
                V.tensor_scalar(lnt[:, 0, :], mv[:, :, 1], LN_EPS, None, ALU.add).then_inc(ln_var, 1)

            def normalize_rows(steps, n, x):
                dve.wait_ge(ln_y, n)
                steps.link(V.tensor_tensor(lnt[:, 3, :], lnt[:, 2, :], lnt[:, 2, :], ALU.mult))
                steps.link(V.tensor_tensor(lnt[:, 3, :], lnt[:, 3, :], lnt[:, 0, :], ALU.mult))
                steps.link(V.tensor_scalar(lnt[:, 3, :], lnt[:, 3, :], -0.5, 1.5, ALU.mult, ALU.add))
                steps.link(V.tensor_tensor(lnt[:, 3, :], lnt[:, 2, :], lnt[:, 3, :], ALU.mult))
                for r in range(RT):
                    V.tensor_scalar(xn[:, r, :], x[:, r, :], mv[:, r, 0:1], lnt[:, 3, r:r + 1],
                                    ALU.subtract, ALU.mult).then_inc(xn_ready, 1)

            def features(g):
                dve.wait_ge(f_ln, g + 1)
                fl = [t[:].rearrange("p j k r -> p (j k r)") for t in (fm, fa)]
                V.scalar_tensor_tensor(fl[0], fl[0], EPS, fl[1], ALU.add, ALU.add).then_inc(f_sum, 1)
                dve.wait_ge(f_sum, g + 1)

            def head_queries(r):
                V.tensor_tensor(qx[0][:], fm[:, 0, 0, None, r * P:(r + 1) * P].broadcast_to([P, LH // KC, P]),
                                of_head[:, :, None].broadcast_to([P, LH // KC, P]), ALU.mult
                                ).then_inc(f_ready, 1)

            def side_unit(steps, side, u, g):
                src = bank3(SIDE, KC)
                if u in WITH_HIGH:
                    dve.wait_ge(side_high, side.high(u))
                else:
                    dve.wait_ge(side_made, side.count(u))
                if u in ("xn1", "xn2", "xn3", "ot"):
                    hi, lo = {"xn1": (x1_h[:], x1_l[:]), "ot": (ot_h[:], ot_l[:])}.get(u, (x2s[:, 0], x2s[:, 1]))
                    V.tensor_tensor(lo, src, f32(hi), ALU.subtract).then_inc(side_drained, 1)
                elif u == "qb":
                    V.tensor_scalar(qb_sb[:], ps[0:H, SIDE, 0:GR], bqk[:, 0:1], None, ALU.add
                                    ).then_inc(side_drained, 1)
                elif u in ("lq", "lk"):
                    if u == "lq":
                        dve.wait_ge(cb_stored, 16 * (g + 1))
                        dve.wait_ge(qb_stored, 16 * (g + 2))
                    V.tensor_scalar(fm[:, int(u == "lk")], src, 0.0, None, ALU.max).then_inc(side_drained, 1)
                elif u == "v":
                    V.tensor_copy(vaug[:, :, :, 0:LD], src.rearrange("p r (h e) -> p r h e", e=LD)
                                  ).then_inc(side_drained, 1)
                elif u in ("sc0", "sc1"):
                    V.tensor_tensor(am[:, int(u[2])], ps[:, SIDE, :].rearrange("p (h t) -> p h t", t=T),
                                    causal[:, None, :].broadcast_to([P, LH, T]), ALU.mult
                                    ).then_inc(side_drained, 1)
                elif u in ("pv0", "pv1"):
                    r = int(u[2])
                    nd = ps[:, SIDE, 0:LH * LV].rearrange("p (h e) -> p h e", e=LV)
                    steps.link(V.tensor_scalar(den[:, 0, r, :], nd[:, :, LD], EPS, None, ALU.add))
                    steps.link(V.reciprocal(den[:, 1, r, :], den[:, 0, r, :]))
                    V.tensor_tensor(xn[:, r, :].rearrange("p (h e) -> p h e", e=LD), nd[:, :, 0:LD],
                                    den[:, 1, r, :, None].broadcast_to([P, LH, LD]), ALU.mult
                                    ).then_inc(side_drained, 1)
                elif u == "y":
                    V.tensor_tensor(xg[:], src, xg[:], ALU.add).then_inc(side_drained, 1)
                elif u == "log":
                    logits(steps, side)
                elif u == "ct":
                    V.tensor_copy(combT[:], ps[0:E, SIDE, 0:GR]).then_inc(side_drained, 1)

            def wide(ap):
                return ap[:, :, None].broadcast_to([P, RT, E])

            def logits(steps, side):
                lg = ps[:, SIDE, 0:RT * E].rearrange("p (t e) -> p t e", e=E)
                steps.link(V.tensor_reduce(rsm[:, 0, :], lg, AX.X, ALU.max))
                V.tensor_tensor(rl[:], lg, wide(rsm[:, 0, :]), ALU.subtract).then_inc(side_drained, 1)
                dve.wait_ge(side_drained, side.count("log"))
                V.tensor_copy(rsm[:, 3, :], rsm[:, 0, :]).then_inc(logit_sub, 1)

            def route(steps, g):
                dve.wait_ge(logit_exp, g + 1)
                steps.link(V.tensor_reduce(rsm[:, 1, :], rl[:], AX.X, ALU.add))
                steps.link(V.reciprocal(rsm[:, 1, :], rsm[:, 1, :]))
                steps.link(V.tensor_tensor(rl[:], rl[:], wide(rsm[:, 1, :]), ALU.mult))
                of_e = rl[:, :, :, None].broadcast_to([P, RT, E, E])
                of_f = rl[:, :, None, :].broadcast_to([P, RT, E, E])
                steps.add(V.tensor_tensor(rgt[:], of_f, of_e, ALU.is_gt))
                steps.link(V.tensor_tensor(req[:], of_f, of_e, ALU.is_equal))
                steps.link(V.tensor_tensor(req[:], req[:], lower[:, None].broadcast_to([P, RT, E, E]), ALU.mult))
                steps.link(V.tensor_tensor(rgt[:], rgt[:], req[:], ALU.add))
                steps.link(V.tensor_reduce(rank[:], rgt[:], AX.X, ALU.add))
                steps.link(V.tensor_scalar(rank[:], rank[:], 1.5, None, ALU.is_lt))
                steps.link(V.tensor_tensor(rl[:], rl[:], rank[:], ALU.mult))
                steps.link(V.tensor_reduce(rsm[:, 2, :], rl[:], AX.X, ALU.add))
                steps.link(V.tensor_scalar(rsm[:, 2, :], rsm[:, 2, :], 1e-20, None, ALU.add))
                steps.link(V.reciprocal(rsm[:, 2, :], rsm[:, 2, :]))
                steps.link(V.tensor_scalar(rsm[:, 2, :], rsm[:, 2, :], ROUTE_SCALE, None, ALU.mult))
                V.tensor_tensor(comb[:], rl[:], wide(rsm[:, 2, :]), ALU.mult).then_inc(comb_ready, 1)

            first = Steps(dve, dve_steps)
            dve.wait_ge(xn_ld, 16)
            row_stats(first, xn)
            normalize_rows(first, 1, xn)
            assert first.n == DVE_FIRST, first.n
            dve.wait_ge(whi, 1)
            V.tensor_tensor(cl_l[:], cl_raw[:], f32(cl_h[:]), ALU.subtract).then_inc(wlo, 1)
            dve.wait_ge(whi, 2)
            V.tensor_tensor(gate_l[:], gateT[:], f32(gate_h[:]), ALU.subtract).then_inc(wlo, 1)
            dve.wait_ge(setup_pe, 1)
            st.link(V.tensor_copy(wqb[:].rearrange("p k h -> p (k h)"), ps[:, 0, 0:KC * H]))
            dve.wait_ge(setup_pe, 2)
            st.add(V.tensor_copy(bqk[:], ps[0:H, 1, 0:1]))
            for i, (lo_, raw, hi) in enumerate((
                    (wq_l[:], wq_raw[:], wq_h[:]), (wk_l[:], wk_raw[:], wk_h[:]),
                    (wv_l[:, :, :, 0:DK], wv_raw[:, :, :, 0:DK], wv_h[:, :, :, 0:DK]),
                    (wv_l[:, :, :, 2 * DK:3 * DK], wv_raw[:, :, :, DK:2 * DK], wv_h[:, :, :, 2 * DK:3 * DK]),
                    (wo_l[:], wo_raw[:], wo_h[:]), (lw_l[:], lw_raw[:], lw_h[:]),
                    (wqb_l[:], wqb[:], wqb_h[:]))):
                dve.wait_ge(whi, i + 3)
                V.tensor_tensor(lo_, raw, f32(hi), ALU.subtract).then_inc(wlo, 1)
            side_unit(first, FIRST_SIDE, "xn1", 0)
            side_unit(first, FIRST_SIDE, "qb", 0)

            def group(g):
                side = side_of(g)
                full = len(side.units) > 2
                ln = ln_base(g)
                steps = Steps(dve, dve_steps, dve_base(g))
                ln_rows = ln + 1
                if full:
                    row_stats(steps, xg)
                    ln = ln + 1

                def low_part(u, dst, src, hi, bias=None):
                    dve.wait_ge(high, g * N_HIGH + HIGH_OF[u])
                    for k in range(len(dst)):
                        if bias is None:
                            ins = V.tensor_tensor(dst[k], src[k], f32(hi[k]), ALU.subtract)
                        else:
                            ins = V.scalar_tensor_tensor(dst[k], src[k], bias[k], f32(hi[k]), ALU.add, ALU.subtract)
                    ins.then_inc(drained, 1)

                def maxima(b, p):
                    tt = slice(2 * p, 2 * p + 2)
                    dve.wait_ge(scores_made, g * (4 * GB) + 4 + 4 * b + 2 * p + 2)
                    steps.link(V.tensor_reduce(mxq[:, 0, tt], ps[:, tt, 0:NK], AX.X, ALU.max))
                    steps.link(V.tensor_tensor(mxq[:, 1, tt], mxq[:, 0, tt], qbt[:, tt, b], ALU.add))
                    V.scalar_tensor_tensor(mxq[:, 2, tt], mxq[:, 1, tt], -SCALE, qbs[:, tt, b],
                                           ALU.mult, ALU.add).then_inc(bias_ready, 1)

                for i in range(4):
                    low_part(U_Q + i, [q_l[:, 2 * i + k, :] for k in range(2)],
                             [bank3(U_Q + i, 2)[:, k, :] for k in range(2)],
                             [q_h[:, 2 * i + k, :] for k in range(2)],
                             [bq_sb[:, 2 * i + k:2 * i + k + 1] for k in range(2)])
                for h in range(H):
                    if h == 14:
                        dve.wait_ge(qb_ld, 64 * (g + 1))
                        steps.link(V.tensor_scalar(qbs[:], qbt[:], SCALE, None, ALU.mult))
                        maxima(0, 0)
                    low_part(U_QP + h, [head(qu_l, h)], [by_batch(bank3(4 + h % 4, KC))], [head(qu_h, h)])
                def sums(b):
                    for p in range(2):
                        tt = slice(2 * p, 2 * p + 2)
                        dve.wait_ge(exp_done, g * (4 * GB) + 4 * b + 2 * p + 2)
                        V.reciprocal(rsum[:, tt], psum_e[:, tt]).then_inc(sum_ready, 1)

                def last_key(b):
                    dve.wait_ge(p_ready, g * (4 * GB) + 4 * b + 4)
                    steps.link(V.tensor_copy(l3[:, :, 0], pr[:, :, NK - 1]))
                    steps.link(V.tensor_tensor(l3[:, :, 1], pr[:, :, NK - 1], f32(l3[:, :, 0]), ALU.subtract))
                    V.tensor_copy(l3[:, :, 2], l3[:, :, 0]).then_inc(l3_ready, 1)

                def slot(k):
                    for u in side.at(k):
                        side_unit(steps, side, u, g + 1 if u in NEXT else g - 1)
                    if k == 4 and full:
                        features(g - 1)
                    if k == 5 and full:
                        head_queries(0)
                    if k == 7 and full:
                        head_queries(1)
                    if k == 11:
                        dve.wait_ge(xn_ld, 16 * (g + 2))
                        row_stats(steps, xn)
                    if k == 12:
                        normalize_rows(steps, ln + 1, xn)
                        if full:
                            row_stats(steps, xg)
                    if k == 13 and full:
                        dve.wait_ge(side_made, side.count("xn1"))
                        normalize_rows(steps, ln + 2, xg)

                maxima(0, 1)
                sums(0)
                maxima(1, 0)
                last_key(0)
                if full:
                    normalize_rows(steps, ln_rows, xg)
                for b in range(GB):
                    for k in range(2):
                        dve.wait_ge(pt_hi, g * (3 * GB) + 3 * b + k + 1)
                        V.tensor_tensor(pt_l[:, k, :], ps[:, 4 + k, :], f32(pt_h[:, k, :]), ALU.subtract
                                        ).then_inc(pt_lo, 1)
                    if b + 1 < GB:
                        maxima(b + 1, 1)
                        sums(b + 1)
                    for dt in range(KC):
                        dve.wait_ge(u_hi, g * (2 * GB) + 2 * b + dt + 1)
                        V.tensor_tensor(qu_l[:, dt, b, :], ps[:, UB, :], f32(qu_h[:, dt, b, :]),
                                        ALU.subtract).then_inc(u_lo, 1)
                        slot(2 * b + dt)
                        if dt == 0 and b + 1 < GB:
                            last_key(b + 1)
                        if dt == 0 and b + 2 < GB:
                            maxima(b + 2, 0)
                if full:
                    route(steps, g - 1)
                for i in range(4):
                    low_part(U_ATT + i, [at_l[:, 2 * i + k, :] for k in range(2)],
                             [bank3(i, 2)[:, k, :] for k in range(2)],
                             [at_h[:, 2 * i + k, :] for k in range(2)],
                             [bv_sb[:, 2 * i + k:2 * i + k + 1] for k in range(2)])
                slot(TAIL)
                dve.wait_ge(xg_ld, 16 * (g + 1))
                for r in range(RT):
                    steps.add(V.tensor_tensor(xg[:, r, :], xg[:, r, :], bo_sb[:], ALU.add))
                steps.wait()
                dve.wait_ge(made, g * NU + U_O + 1)
                V.tensor_tensor(xg[:], bank3(4, RT), xg[:], ALU.add).then_inc(drained, 1)
                dve.wait_ge(drained, g * NU + U_O + 1)
                assert steps.n == (DVE_G if full else DVE_0), (full, steps.n)

            dve.wait_ge(c3_stored, 48)
            groups(dve, group)
            last = Steps(dve, dve_steps, DVE_FIRST + DVE_0 + (NG - 1) * DVE_G)
            row_stats(last, xg)
            normalize_rows(last, LN_LAST + 1, xg)
            for u in LAST:
                side_unit(last, LAST_SIDE, u, NG - 1)
                if u == "v":
                    features(NG - 1)
                    head_queries(0)
                if u == "pv0":
                    head_queries(1)
                if u == "log":
                    route(last, NG - 1)
                if u == "y":
                    dve.wait_ge(side_drained, LAST_SIDE.count("y"))
                    row_stats(last, xg)
                    normalize_rows(last, LN_LAST + 2, xg)

            def unit(i, s, e=None):
                rows = rows_of(s)
                dve.wait_ge(gu_made, 2 * i + 2)
                dve.wait_ge(silu_done, i + 1)
                if not isinstance(i, int) or i >= 2:
                    dve.wait_ge(h_hi, i - 1)
                up = ps[0:rows, 5 + 2 * (s % 2), :]
                if e is None:
                    V.tensor_tensor(hm[s % 2][0:rows], up, sg[s % 2][0:rows], ALU.mult).then_inc(h_done, 1)
                else:
                    V.tensor_tensor(sg[s % 2][0:rows], up, sg[s % 2][0:rows], ALU.mult).then_inc(h_mid, 1)
                    dve.wait_ge(h_mid, i - SHARED + 1)
                    half = s % 2
                    V.tensor_tensor(hm[s % 2][0:rows], sg[s % 2][0:rows],
                                    combB[0:rows, bass.ds(e, 1), half * HALF:(half + 1) * HALF].rearrange(
                                        "p o t -> p (o t)"), ALU.mult).then_inc(h_done, 1)
                dve.wait_ge(h_hi, i + 1)
                V.tensor_tensor(hl[s % 2][0:rows], hm[s % 2][0:rows], f32(hh[s % 2][0:rows]), ALU.subtract
                                ).then_inc(h_lo, 1)

            for_units(dve, unit, routed=lambda: dve.wait_ge(comb_ld, 16 * E), with_expert=True)
            dve.wait_ge(down_done, NUNITS)
            for r in (1, 3):
                V.tensor_copy(fo[:, r // 2, HALF:ROWS], ps[:, r, :]).then_inc(fo_ready, 1)
            dve.wait_ge(fx_ld, 16)
            for r in range(TILES):
                if r % 2 == 0:
                    dve.wait_ge(fy_made, r // 2 + 1)
                V.tensor_tensor(fy[:, r, :], ps[:, 4 + r // 2, (r % 2) * D:(r % 2 + 1) * D], fx[:, r, :],
                                ALU.add).then_inc(fy_ready, 1)

        @block.tensor
        def _(pe):
            mm = nc.tensor.matmul

            def mm3(dst, w, x, start, stop):
                mm(dst, w[0], x[0], start=start, stop=False)
                mm(dst, w[0], x[1], start=False, stop=False)
                return mm(dst, w[1], x[0], start=False, stop=stop)

            pe.wait_ge(weight_ld[0], 32)
            pe.wait_ge(setup_dve, 3)
            for kc in range(KC):
                for hp in range(HP):
                    ins = mm(ps[:, 0, kc * H:(kc + 1) * H], wqn_raw[:, hp, kc * P:(kc + 1) * P], bkd[:, hp, :],
                             start=hp == 0, stop=hp == HP - 1)
            ins.then_inc(setup_pe, 1)
            for hp in range(HP):
                ins = mm(ps[0:H, 1, 0:1], bkd[:, hp, :], bq_sb[:, hp:hp + 1], start=hp == 0, stop=hp == HP - 1)
            ins.then_inc(setup_pe, 1)
            pe.wait_ge(mask_ready, MASKS + 1)

            def transposes(dst):
                for kc in range(KC):
                    for r in range(RT):
                        ins = nc.tensor.transpose(dst[:, kc * GR + r * P:kc * GR + (r + 1) * P],
                                                  xn[:, r, kc * P:(kc + 1) * P], ident[:])
                return ins

            def projection(dst, j, et):
                w = slice(et * P, (et + 1) * P)
                for kc in range(KC):
                    ins = mm3(dst, (lw_h[:, j, kc, w], lw_l[:, j, kc, w]), (x2s[:, 0, kc], x2s[:, 1, kc]),
                              kc == 0, kc == 1)
                return ins

            def side_waits(side, u, g, ln):
                if u != side.units[0] or side is not FIRST_SIDE:
                    pe.wait_ge(side_drained, side.before(u))
                if u in ("xn1", "xn2", "xn3"):
                    pe.wait_ge(xn_ready, RT * ln)
                elif u in ("sc0", "sc1"):
                    pe.wait_ge(f_ready, 4 * g + 2 * int(u[2]) + 2)
                elif u == "ct":
                    pe.wait_ge(comb_ready, g + 1)

            def side_unit(side, u):
                bank = ps[:, SIDE, :]
                if u in ("xn1", "xn2", "xn3"):
                    ins = transposes(bank)
                elif u == "qb":
                    for kc in range(KC):
                        x = [t[:, kc, :].rearrange("p (b q) -> p q b", q=T) for t in (x1_h, x1_l)]
                        ins = mm3(ps[0:H, SIDE, 0:GR], (wqb_h[:, kc, :], wqb_l[:, kc, :]), x, kc == 0, kc == 1)
                elif u in ("lq", "lk"):
                    for et in range(KC):
                        ins = projection(bank[:, et * GR:(et + 1) * GR], int(u == "lk"), et)
                elif u == "v":
                    for r in range(RT):
                        w = slice(r * P, (r + 1) * P)
                        for kc in range(KC):
                            ins = mm3(bank[:, r * D:(r + 1) * D], (x2s[:, 0, kc, w], x2s[:, 1, kc, w]),
                                      (lw_h[:, 2, kc, :], lw_l[:, 2, kc, :]), kc == 0, kc == 1)
                elif u in ("sc0", "sc1"):
                    r = int(u[2])
                    for et in range(KC):
                        for b4 in range(4):
                            w = slice(r * P + T * b4, r * P + T * b4 + T)
                            ins = mm(ps[T * b4:T * b4 + T, SIDE, et * GR:(et + 1) * GR], fm[:, 1, et, w],
                                     qx[et][:, :, T * b4:T * b4 + T], start=True, stop=True)
                elif u in ("pv0", "pv1"):
                    r = int(u[2])
                    for b4 in range(4):
                        rows = slice(T * b4, T * b4 + T)
                        for h in range(LH):
                            ins = mm(ps[rows, SIDE, h * LV:(h + 1) * LV], am[rows, r, h, :], vaug[rows, r, h, :],
                                     start=True, stop=True)
                elif u == "ot":
                    ins = transposes(bank)
                elif u == "y":
                    for r in range(RT):
                        w = slice(r * P, (r + 1) * P)
                        for kc in range(KC):
                            ins = mm3(bank[:, r * D:(r + 1) * D], (ot_h[:, kc, w], ot_l[:, kc, w]),
                                      (lw_h[:, 3, kc, :], lw_l[:, 3, kc, :]), kc == 0, kc == 1)
                elif u == "log":
                    for r in range(RT):
                        w = slice(r * P, (r + 1) * P)
                        for kc in range(KC):
                            ins = mm3(bank[:, r * E:(r + 1) * E], (x2s[:, 0, kc, w], x2s[:, 1, kc, w]),
                                      (gate_h[:, kc, :], gate_l[:, kc, :]), kc == 0, kc == 1)
                elif u == "ct":
                    for r in range(RT):
                        ins = nc.tensor.transpose(ps[0:E, SIDE, r * P:(r + 1) * P], comb[:, r, :], ident[:])
                ins.then_inc(side_made, 1)

            side_waits(FIRST_SIDE, "xn1", 0, 1)
            side_unit(FIRST_SIDE, "xn1")
            pe.wait_ge(wlo, 9)
            pe.wait_ge(setup_dve, 5)
            side_waits(FIRST_SIDE, "qb", 0, 1)
            side_unit(FIRST_SIDE, "qb")
            pe.wait_ge(side_drained, 2)

            def group(g):
                side = side_of(g)
                full = len(side.units) > 2
                ln = ln_base(g)
                if full:
                    pe.wait_ge(side_drained, side.base)
                def scores(b, tiles):
                    if tiles[0] == 0:
                        pe.wait_ge(ct_split, g * (2 * GB) + 2 * b + 4)
                    for t in tiles:
                        if b:
                            pe.wait_ge(exp_done, g * (4 * GB) + 4 * (b - 1) + t + 1)
                        for kc in range(KC):
                            q = [x[:, kc, b, P * t:P * t + P] for x in (qu_h, qu_l)]
                            ins = mm3(ps[:, t, 0:NKP], q, (ct_h[:, kc, :], ct_l[:, kc, :]), kc == 0, kc == 1)
                        ins.then_inc(scores_made, 1)

                for i in range(4):
                    for k in range(2):
                        hp = 2 * i + k
                        for kc in range(KC):
                            w = slice(hp * P, (hp + 1) * P)
                            ins = mm3(ps[:, U_Q + i, k * GR:(k + 1) * GR],
                                      (wq_h[:, kc, w], wq_l[:, kc, w]), (x1_h[:, kc, :], x1_l[:, kc, :]),
                                      kc == 0, kc == 1)
                    ins.then_inc(made, 1)
                for h in range(H):
                    if full and h == 0:
                        pe.wait_ge(drained, g * NU)
                    if h >= 4:
                        pe.wait_ge(drained, g * NU + U_QP + h - 3)
                    pe.wait_ge(drained, g * NU + U_Q + h // 4 + 1)
                    rows = slice(DK * (h % 2), DK * (h % 2) + DK)
                    for dt in range(KC):
                        w = slice(dt * P, (dt + 1) * P)
                        ins = mm3(ps[:, 4 + h % 4, dt * GR:(dt + 1) * GR],
                                  (wk_h[rows, h // 2, w], wk_l[rows, h // 2, w]),
                                  (q_h[rows, h // 2, :], q_l[rows, h // 2, :]), True, True)
                    ins.then_inc(made, 1)
                    if h % 4 == 3 and h > 4:
                        scores(0, [h // 4 - 1])
                pe.wait_ge(drained, g * NU + U_QP + H)
                scores(0, [3])

                def probs_t(b):
                    for k in range(2):
                        for t in range(4):
                            if k == 0:
                                pe.wait_ge(p_ready, g * (4 * GB) + 4 * b + t + 1)
                            ins = nc.tensor.transpose(ps[:, 4 + k, t * P:(t + 1) * P],
                                                      pr[:, t, k * P:(k + 1) * P], ident[:])
                        ins.then_inc(pt_made, 1)

                def last_key_t(b):
                    pe.wait_ge(l3_ready, g * GB + b + 1)
                    if b:
                        pe.wait_ge(u_lo, g * (2 * GB) + 2 * b)
                    for t in range(4):
                        ins = nc.tensor.transpose(ps[0:3, UB, t * P:(t + 1) * P], f32(l3[:, t, :]), ident[:])
                    ins.then_inc(pt_made, 1)

                def attend(b, dt, waits):
                    s = b % 2
                    w = slice(dt * P, (dt + 1) * P)
                    if dt == 0:
                        pe.wait_ge(cn_split, g * (2 * GB) + 2 * b + 4)
                        pe.wait_ge(c3_ld[s], 16 * (g * (GB // 2) + b // 2 + 1))
                        pe.wait_ge(pt_hi, g * (3 * GB) + 3 * b + 3)
                    else:
                        pe.wait_ge(u_lo, g * (2 * GB) + 2 * b + 1)
                    for k in range(2):
                        if dt == 0:
                            pe.wait_ge(pt_lo, g * (2 * GB) + 2 * b + k + 1)
                        mm3(ps[:, UB, :], (cn_h[:, k, w], cn_l[:, k, w]), (pt_h[:, k, :], pt_l[:, k, :]),
                            k == 0, False)
                    waits()
                    mm(ps[:, UB, :], c3[s][0:3, w], pl3[0:3, :], start=False, stop=True).then_inc(u_made, 1)

                lns = {"xn2": ln + 1, "xn1": ln + 2, "xn3": ln + 3} if full else {"xn1": ln + 1}

                scores(1, range(2))
                for b in range(GB):
                    probs_t(b)
                    if b + 1 < GB:
                        scores(b + 1, [2])
                    last_key_t(b)
                    if b + 1 < GB:
                        scores(b + 1, [3])
                    for dt in range(KC):
                        units = side.at(2 * b + dt)

                        def waits():
                            for u in units:
                                side_waits(side, u, g + 1 if u in NEXT else g - 1, lns.get(u))

                        attend(b, dt, waits)
                        for u in units:
                            side_unit(side, u)
                        if dt == 0 and b + 2 < GB:
                            scores(b + 2, range(2))
                pe.wait_ge(u_lo, g * (2 * GB) + 2 * GB)
                for i in range(4):
                    for k in range(2):
                        hp = 2 * i + k
                        for j in range(2):
                            w = slice(DK * j, DK * j + P)
                            for kc in range(KC):
                                ins = mm3(ps[:, i, k * GR:(k + 1) * GR], (wv_h[:, kc, hp, w], wv_l[:, kc, hp, w]),
                                          (head(qu_h, 2 * hp + j)[:, kc], head(qu_l, 2 * hp + j)[:, kc]),
                                          j == 0 and kc == 0, j == 1 and kc == 1)
                    ins.then_inc(made, 1)
                for u in side.at(TAIL):
                    side_waits(side, u, g - 1, None)
                    side_unit(side, u)
                pe.wait_ge(drained, g * NU + U_ATT + 4)
                for r in range(RT):
                    w = slice(r * P, (r + 1) * P)
                    for hp in range(HP):
                        ins = mm3(ps[:, 4, r * D:(r + 1) * D], (at_h[:, hp, w], at_l[:, hp, w]),
                                  (wo_h[:, hp, :], wo_l[:, hp, :]), hp == 0, hp == HP - 1)
                ins.then_inc(made, 1)

            groups(pe, group)
            for u in LAST:
                side_waits(LAST_SIDE, u, NG - 1, {"xn2": LN_LAST + 1, "xn3": LN_LAST + 2}.get(u))
                side_unit(LAST_SIDE, u)

            pe.wait_ge(side_drained, LAST_SIDE.base + len(LAST))
            pe.wait_ge(ft_ld, 32 * NG)

            def down(i, s, es, start=False, stop=False):
                rows, tile, half = rows_of(s), s // 2, s % 2
                pe.wait_ge(h_lo, i + 1)
                for dt in range(KC):
                    w = slice(2 * KC * FE + tile * D + dt * P, 2 * KC * FE + tile * D + (dt + 1) * P)
                    ps_ = ps[:, 2 * dt + half, :]
                    x = (hh[s % 2][0:rows], hl[s % 2][0:rows])
                    mm(ps_, fw_h[es][0:rows, w], x[0], start=start, stop=False, skip_group_check=True)
                    mm(ps_, fw_h[es][0:rows, w], x[1], start=False, stop=False, skip_group_check=True)
                    ins = mm(ps_, fw_l[es][0:rows, w], x[0], start=False, stop=stop, skip_group_check=True)
                ins.then_inc(down_done, 1)

            def unit(i, s, e=None, es=0):
                tile, half = s // 2, s % 2
                f0, rows = FT[tile]
                if s == 0:
                    pe.wait_ge(fw_split, 2 * e + 2)
                if not isinstance(i, int) or i >= 2:
                    pe.wait_ge(h_lo, i - 1)
                for gu in range(2):
                    for kc in range(KC):
                        w = slice(gu * KC * FE + kc * FE + f0, gu * KC * FE + kc * FE + f0 + rows)
                        tok = slice(half * HALF, (half + 1) * HALF)
                        ins = mm3(ps[0:rows, 4 + 2 * (s % 2) + gu, :], (fw_h[es][:, w], fw_l[es][:, w]),
                                  (fts[:, 0, kc, tok], fts[:, 1, kc, tok]), kc == 0, kc == 1)
                    ins.then_inc(gu_made, 1)
                if not isinstance(i, int) or i >= 1:
                    ps_, pes = (s - 1, es) if s else (5, 1 - es)
                    down(i - 1, ps_, pes, start=isinstance(i, int) and i <= 2)

            for_units(pe, unit, with_expert=True, with_slot=True)
            down(NUNITS - 1, 5, 1, stop=True)
            pe.wait_ge(fo_ready, 4)
            for r in range(TILES):
                for dt in range(KC):
                    ins = nc.tensor.transpose(ps[:, 4 + r // 2, (r % 2) * D + dt * P:(r % 2) * D + (dt + 1) * P],
                                              fo[:, dt, r * P:(r + 1) * P], ident[:])
                if r % 2:
                    ins.then_inc(fy_made, 1)


def kernel(**inputs):
    import numpy as _np
    import concourse.bacc as _bacc
    from concourse import mybir as _mybir
    from concourse.bass_utils import run_bass_kernel_spmd as _run

    x = {k: _np.ascontiguousarray(v) for k, v in inputs.items()}

    def in_chunks(w):
        return w.reshape(w.shape[0] // 128, 128, w.shape[1]).transpose(1, 0, 2)

    ctx = x["ctx_1024"]
    ctxT = _np.zeros((32, 128, 2, 258), ctx.dtype)
    ctxT[:, :, :, 0:257] = ctx.transpose(0, 2, 1).reshape(32, 2, 128, 257).transpose(0, 2, 1, 3)

    def expert(gate, up, down):
        d = _np.zeros((128, 3, 256), down.dtype)
        for t in range(3):
            part = down[128 * t:min(128 * (t + 1), 352)]
            d[0:len(part), t] = part
        return _np.concatenate([in_chunks(gate).reshape(128, -1), in_chunks(up).reshape(128, -1),
                                d.reshape(128, -1)], axis=1)

    p = "L0_ffn_"
    ffn = [expert(x[p + "sw_gate"][:, 352 * j:352 * (j + 1)], x[p + "sw_up"][:, 352 * j:352 * (j + 1)],
                  x[p + "sw_down"][352 * j:352 * (j + 1)]) for j in range(2)]
    ffn += [expert(x[p + "w_gate"][e], x[p + "w_up"][e], x[p + "w_down"][e]) for e in range(8)]
    p = "L0_xattn_"
    laid = {
        "x": _np.concatenate([x["x"].reshape(1024, 256), _np.zeros((256, 256), x["x"].dtype)]),
        "ctx": ctx,
        "ctxT": ctxT,
        "wqn": in_chunks(x[p + "Wq"]),
        "wqT": in_chunks(x[p + "Wq"].T),
        "wk": in_chunks(x[p + "Wk"]),
        "wvT": in_chunks(x[p + "Wv"].T).reshape(128, 2, 8, 128),
        "woT": in_chunks(x[p + "Wo"].T),
        "bq": x[p + "bq"].reshape(8, 128).T,
        "bk": x[p + "bk"].reshape(8, 128).T,
        "bv": x[p + "bv"].reshape(8, 128).T,
        "bo": x[p + "bo"],
        "lwT": _np.stack([in_chunks(x["L0_attn_" + w].T) for w in ("Wq", "Wk", "Wv", "Wo")], axis=1),
        "gateT": in_chunks(x["L0_ffn_gate_w"].T),
        "ffn": _np.stack(ffn),
    }
    nc = _bacc.Bacc("TRN2", target_bir_lowering=False, num_devices=1)
    arrays, aps = {}, {}
    for name, v in laid.items():
        v = _np.ascontiguousarray(v)
        arrays[f"in_{name}"] = v
        aps[name] = nc.dram_tensor(f"in_{name}", v.shape, _mybir.dt.from_np(v.dtype), kind="ExternalInput").ap()
    out = nc.dram_tensor("out_0", (1024, 256), _mybir.dt.float32, kind="ExternalOutput").ap()
    build(nc, aps, out)
    r = _run(nc, [arrays], core_ids=[0])
    return r.results[0]["out_0"].reshape(32, 32, 256)
```

```python
from contextlib import ExitStack

import numpy as np
import concourse.bass as bass
from concourse import mybir

F32 = mybir.dt.float32
F32R = mybir.dt.float32r
ALU = mybir.AluOpType
ACT = mybir.ActivationFunctionType
AX = mybir.AxisListType

P = 128
D = 256
KC = D // P
B, T = 32, 32
NK = 257
NKP = NK + 1
H, DK = 16, 64
HP = H // 2
LH, LD = 16, 16
LV = LD + 2
GB = 8
NG = B // GB
GR = GB * T
RT = GR // P
ROWS = B * T
TILES = ROWS // P
E, FE = 8, 352
SHARED_TILES = -(-2 * FE // P)
ROUTED_TILES = E * FE // P
FTILES = SHARED_TILES + ROUTED_TILES
FW = 2 * KC * P + D
EARLY = 5
CB = 32
HALF = 512
SCALE = 1.0 / 8.0
LN_EPS = 1e-5
EPS = 1e-6
ROUTE_SCALE = 2.5

U_QP, U_ATT, U_O = 0, 16, 20
NU = 21
QU = 4
ATT_BANK = (4, 5, 6, 4)
O_BANK = 5
NEXT = ("xn1", "qb")
LINEAR = ("xn2", "lq", "lk", "v", "sc0", "pv0", "sc1", "pv1", "ot", "y")
FULL = LINEAR + ("xn1", "qb", "xn3", "log", "ct")
LAST = LINEAR + ("xn3", "log", "ct")
WITH_HIGH = ("xn1", "xn2", "lq", "lk", "ot", "xn3")
TAIL = 2 * GB
SLOT = {"xn2": 0, "lq": 1, "lk": 2, "v": 3, "sc0": 5, "pv0": 6, "sc1": 7, "pv1": 8, "ot": 9, "y": 10,
        "xn1": 12, "qb": 13, "xn3": 14, "log": 15, "ct": TAIL}


class Side:

    def __init__(self, units, base, base_high, bank=7):
        self.units, self.base, self.base_high, self.bank = units, base, base_high, bank
        self.highs = [u for u in units if u in WITH_HIGH]

    def count(self, u):
        return self.base + self.units.index(u) + 1

    def before(self, u):
        return self.base + self.units.index(u)

    def high(self, u):
        return self.base_high + self.highs.index(u) + 1

    def at(self, slot):
        return [u for u in self.units if SLOT[u] == slot]


def later_base(n):
    return n * len(FULL) + 2 * len(NEXT), n * len(WITH_HIGH) + 2


def side_of(g):
    if isinstance(g, int):
        assert g == 0
        return Side(NEXT, len(NEXT), 1)
    return Side(FULL, *later_base(g - 1))


FIRST_SIDE = Side(NEXT, 0, 0)
LAST_SIDE = Side(LAST, *later_base(NG - 1), bank=1)


def ffn_unit(u):
    return (u % EARLY, u // EARLY) if u < 2 * EARLY else (u // 2, u % 2)


def ffn_slot(t):
    return t if t < EARLY else t % 2


class Steps:

    def __init__(self, eng, sem, base=0):
        self.eng, self.sem, self.base, self.n = eng, sem, base, 0

    def add(self, ins):
        ins.then_inc(self.sem, 1)
        self.n += 1

    def wait(self):
        self.eng.wait_ge(self.sem, self.base + self.n)

    def link(self, ins):
        self.add(ins)
        self.wait()


def build(nc, a, out):
    ctx = ExitStack()
    with ctx:
        def sem(name):
            return ctx.enter_context(nc.semaphore(name))

        place = {"at": 16512}

        def at(offset, name, shape, dt):
            return nc.alloc_sbuf_tensor_at(name, shape, dt, offset=offset)

        def sb(name, shape, dt):
            offset = place["at"]
            place["at"] = (offset + int(np.prod(shape[1:])) * 4 + 31) // 32 * 32
            return at(offset, name, shape, dt)

        ident = sb("ident", [P, P], F32)
        causal = sb("causal", [P, T], F32)
        of_head = sb("of_head", [P, LH // KC], F32)
        zero = sb("zero", [P, 1], F32)
        minus_half = sb("minus_half", [P, 1], F32)
        lower = sb("lower", [P, E, E], F32)
        bq_sb = sb("bq_sb", [P, HP], F32)
        bv_sb = sb("bv_sb", [P, HP], F32)
        bo_sb = sb("bo_sb", [P, D], F32)
        gate_h = sb("gate_h", [P, KC, E], F32R)
        gate_l = sb("gate_l", [P, KC, E], F32R)
        stats = sb("stats", [P, RT, 6], F32)
        mv = sb("mv", [P, RT, 2], F32)
        lnt = sb("lnt", [P, 4, RT], F32)
        rl = sb("rl", [P, RT, E], F32)
        rsm = sb("rsm", [P, 3, RT], F32)
        rank = sb("rank", [P, RT, E], F32)
        comb = sb("comb", [P, RT, E], F32)
        PHASE = place["at"]
        bqk = sb("bqk", [H, 1], F32)
        wqb_h = sb("wqb_h", [P, KC, H], F32R)
        wqb_l = sb("wqb_l", [P, KC, H], F32R)
        wq_h = sb("wq_h", [P, KC, H * DK], F32R)
        wq_l = sb("wq_l", [P, KC, H * DK], F32R)
        wk_h = sb("wk_h", [P, HP, D], F32R)
        wk_l = sb("wk_l", [P, HP, D], F32R)
        wv_h = sb("wv_h", [P, KC, HP, 3 * DK], F32R)
        wv_l = sb("wv_l", [P, KC, HP, 3 * DK], F32R)
        wo_h = sb("wo_h", [P, HP, D], F32R)
        wo_l = sb("wo_l", [P, HP, D], F32R)
        lw_h = sb("lw_h", [P, 4, KC, D], F32R)
        lw_l = sb("lw_l", [P, 4, KC, D], F32R)
        xg = sb("xg", [P, RT, D], F32)
        xn = sb("xn", [P, RT, D], F32)
        qbt = sb("qbt", [P, 4, GB], F32)
        qbs = sb("qbs", [P, 4, GB], F32)
        vaug = sb("vaug", [P, RT, LH, LV], F32)
        den = sb("den", [P, 2, RT, LH], F32)
        mxq = sb("mxq", [P, 3, 4], F32)
        psum_e = sb("psum_e", [P, 4], F32)
        rsum = sb("rsum", [P, 4], F32)
        SF = place["at"]
        fm = sb("fm", [P, 2, KC, GR], F32)
        combT = at(SF, "combT", [E, GR], F32)
        qb_sb = at(SF + 1024, "qb_sb", [H, GR], F32)
        SA = place["at"]
        x2s = at(SA, "x2s", [P, 2, KC, GR], F32R)
        am = at(SA, "am", [P, RT, LH, T], F32)
        SB = SA + 4096
        fa = at(SB, "fa", [P, 2, KC, GR], F32)
        ot_h = at(SB, "ot_h", [P, KC, GR], F32R)
        ot_l = at(SB + 2048, "ot_l", [P, KC, GR], F32R)
        rgt = at(SB, "rgt", [P, RT, E, E], F32)
        req = at(SB + 512, "req", [P, RT, E, E], F32)
        SC = SB + 4096
        qx = [at((SB, SC)[et], f"qx{et}", [P, LH // KC, P], F32) for et in range(KC)]
        x1_h = at(SC, "x1_h", [P, KC, GR], F32R)
        x1_l = at(SC + 2048, "x1_l", [P, KC, GR], F32R)
        place["at"] = SC + 4096
        cn_raw = sb("cn_raw", [P, 2, D], F32)
        ct_raw = sb("ct_raw", [P, KC, NKP], F32)
        cn_h = sb("cn_h", [P, 2, D], F32R)
        cn_l = sb("cn_l", [P, 2, D], F32R)
        ct_h = sb("ct_h", [P, KC, NKP], F32R)
        ct_l = sb("ct_l", [P, KC, NKP], F32R)
        c3 = [sb(f"c3_{s}", [3, D], F32R) for s in range(2)]
        RA = place["at"]
        q_h = [at((SB, SA)[hp // 2] + 1024 * (hp % 2) if hp < 4 else RA + 1024 * hp, f"q_h{hp}", [P, GR], F32R)
               for hp in range(HP)]
        q_l = [at((SB, SA)[hp // 2] + 2048 + 1024 * (hp % 2) if hp < 4 else RA + 8192 + 1024 * hp, f"q_l{hp}",
                  [P, GR], F32R) for hp in range(HP)]
        pr = at(RA, "pr", [P, 4, NKP], F32)
        pl3 = at(RA + 4128, "pl3", [3, 512], F32R)
        l3 = at(RA + 6176, "l3", [P, 4, 3], F32R)
        pt_h = at(RA + 8192, "pt_h", [P, 2, 512], F32R)
        pt_l = at(RA + 12288, "pt_l", [P, 2, 512], F32R)
        at_h = at(RA, "at_h", [P, HP, GR], F32R)
        at_l = at(RA + 8192, "at_l", [P, HP, GR], F32R)
        RB = RA + 16384
        qu_h = at(RB, "qu_h", [P, KC, GB, H * T], F32R)
        qu_l = at(RB + 32768, "qu_l", [P, KC, GB, H * T], F32R)
        END = RB + 65536
        wq_raw = at(RB, "wq_raw", [P, KC, H * DK], F32)
        wqn_raw = at(RB + 8192, "wqn_raw", [P, HP, D], F32)
        wk_raw = at(RB + 16384, "wk_raw", [P, HP, D], F32)
        wv_raw = at(RB + 24576, "wv_raw", [P, KC, HP, P], F32)
        wo_raw = at(RB + 32768, "wo_raw", [P, HP, D], F32)
        lw_raw = at(SF + 2048, "lw_raw", [P, 4, KC, D], F32)
        cl_raw = at(RB + 49152, "cl_raw", [B, D], F32)
        cl_h = at(RB + 50176, "cl_h", [B, D], F32R)
        cl_l = at(RB + 51200, "cl_l", [B, D], F32R)
        bk_sb = at(RB + 52224, "bk_sb", [P, HP], F32)
        bkd = at(RB + 52288, "bkd", [P, HP, H], F32)
        wqb = at(RB + 52800, "wqb", [P, KC, H], F32)
        gateT = at(RB + 52928, "gateT", [P, KC, E], F32)
        assert END <= nc.sbuf_usable_end, (END, nc.sbuf_usable_end)

        place["at"] = RA
        sg = [sb(f"sg{s}", [P, HALF], F32) for s in range(2)]
        hm = [sb(f"hm{s}", [P, HALF], F32) for s in range(2)]
        hh = [sb(f"hh{s}", [P, HALF], F32R) for s in range(2)]
        hl = [sb(f"hl{s}", [P, HALF], F32R) for s in range(2)]
        assert place["at"] <= RB, place["at"]
        place["at"] = RB
        fts = sb("fts", [P, 2, KC, ROWS], F32R)
        fw_raw = [sb(f"fw_raw{s}", [P, FW], F32) for s in range(2)]
        cw = [sb(f"comb_rows{s}", [P, ROWS], F32) for s in range(2)]
        fw_h = [sb(f"fw_h{s}", [P, FW], F32R) for s in range(EARLY)]
        fw_l = [sb(f"fw_l{s}", [P, FW], F32R) for s in range(EARLY)]
        assert place["at"] <= nc.sbuf_usable_end, place["at"]
        place["at"] = PHASE
        fx = sb("fx", [P, TILES, D], F32)
        fo = sb("fo", [P, KC, ROWS], F32)
        fy = sb("fy", [P, TILES, D], F32)
        assert place["at"] <= SA, place["at"]

        ps = ctx.enter_context(nc.psum_tensor("ps", [P, 8, 512], F32))
        UB = 6

        c3_d = nc.dram_tensor("c3_scratch", [B, 3, D], F32).ap()
        qb_d = nc.dram_tensor("qb_scratch", [NG + 1, H, GR], F32).ap()
        x2_d = nc.dram_tensor("x2_scratch", [ROWS, D], F32).ap()
        ft_d = nc.dram_tensor("xt_scratch", [NG, P, 2, KC, GR], F32).ap()
        cb_d = nc.dram_tensor("comb_scratch", [E, FE // CB, ROWS], F32).ap()

        def bank3(i, n):
            return ps[:, i, :].rearrange("p (n c) -> p n c", n=n)

        def head(t, h):
            return t[:, :, :, T * h:T * h + T]

        def by_batch(ap):
            return ap.rearrange("p k (b q) -> p k b q", q=T)

        def diag(ap, j):
            flat = ap.rearrange("p a h -> p (a h)")
            return flat[:, j:j + (HP - 1) * (H + 2) + 1:H + 2]

        def groups(eng, body):
            body(0)
            with eng.Fori(1, NG) as g:
                body(g)

        def for_routed(eng, unit):
            with eng.Fori(0, ROUTED_TILES // 2) as j:
                for s in range(2):
                    for half in range(2):
                        unit(j * 4 + 2 * SHARED_TILES + 2 * s + half, half, half, s, j)

        const_ld = sem("const_loaded")
        weight_ld = {w: sem(f"{w}_loaded") for w in ("cl", "wqn", "wq", "wk", "wv", "wo", "lw")}
        lw_ready = sem("linear_weights_split")
        mask_ready = sem("mask_ready")
        setup_pe = sem("setup_pe")
        setup_dve = sem("setup_dve")
        whi = sem("weight_high")
        wlo = sem("weight_low")
        c3_stored = sem("c3_stored")
        xn_ld = sem("next_rows_loaded")
        xg_ld = sem("residual_rows_loaded")
        ln_var = sem("ln_var_ready")
        ln_y = sem("ln_guess_ready")
        xn_ready = sem("xn_ready")
        q_made = sem("queries_made")
        q_high = sem("queries_high")
        q_drained = sem("queries_drained")
        made = sem("unit_made")
        high = sem("unit_high")
        drained = sem("unit_drained")
        side_made = sem("side_unit_made")
        side_high = sem("side_unit_high")
        side_drained = sem("side_unit_drained")
        qb_stored = sem("qb_stored")
        qb_ld = sem("qb_loaded")
        ct_ld = sem("context_transposed_loaded")
        cn_ld = sem("context_loaded")
        c3_ld = [sem(f"c3_loaded{s}") for s in range(2)]
        ct_split = sem("context_transposed_split")
        cn_split = sem("context_split")
        scores_made = sem("scores_made")
        bias_ready = sem("exp_bias_ready")
        exp_done = sem("exp_done")
        sum_ready = sem("exp_sum_inverted")
        p_ready = sem("probs_ready")
        l3_ready = sem("last_key_ready")
        pt_made = sem("probs_transposed")
        pt_hi = sem("probs_high")
        pt_lo = sem("probs_low")
        u_made = sem("attended_made")
        u_hi = sem("attended_high")
        u_lo = sem("attended_low")
        act_steps = sem("feature_exp_done")
        dve_steps = sem("dve_steps")
        f_ln = sem("feature_log_ready")
        f_sum = sem("features_ready")
        f_ready = sem("head_queries_ready")
        logit_exp = sem("logits_exp")
        comb_ready = sem("comb_ready")
        x2_stored = sem("x2_stored")
        x3_stored = sem("xt_stored")
        cb_stored = sem("comb_stored")
        ft_ld = [sem(f"ffn_xT_loaded{h}") for h in range(2)]
        fx_ld = sem("ffn_x_loaded")
        comb_ld = [sem(f"comb_loaded{s}") for s in range(2)]
        fw_ld = [sem(f"ffn_weights_loaded{s}") for s in range(2)]
        fw_split = sem("ffn_weights_split")
        gu_made = sem("gate_up_made")
        silu_done = sem("silu_done")
        h_mid = sem("h_unweighted_done")
        h_done = sem("h_done")
        h_hi = sem("h_high")
        h_lo = sem("h_low")
        down_done = sem("down_done")
        fo_ready = [sem(f"ffn_sum_copied{h}") for h in range(2)]
        fy_made = sem("ffn_rows_made")
        fy_ready = sem("ffn_rows_ready")
        stored = sem("out_stored")

        def f32(ap):
            return ap.bitcast(F32)

        N_CONST = 5
        NUNITS = 2 * FTILES
        MASKS = 11
        N_HIGH = U_O
        DVE_FIRST, DVE_0, DVE_G = 9, 60, 97

        def dve_base(g):
            return DVE_FIRST if isinstance(g, int) else (g - 1) * DVE_G + DVE_FIRST + DVE_0

        def ln_base(g):
            return 1 if isinstance(g, int) else (g - 1) * 3 + 2

        LN_LAST = 2 + 3 * (NG - 1)

        block = ctx.enter_context(nc.Block())

        @block.sync
        def _(sp):
            sp.dma_start(bq_sb[:], a["bq"]).then_inc(const_ld, 16)
            sp.dma_start(bk_sb[:], a["bk"]).then_inc(const_ld, 16)
            sp.dma_start(bv_sb[:], a["bv"]).then_inc(const_ld, 16)
            sp.dma_start(bo_sb[:], a["bo"].partition_broadcast(P)).then_inc(const_ld, 16)
            sp.dma_start(gateT[:], a["gateT"]).then_inc(const_ld, 16)
            sp.dma_start(xn[:], a["x"][0:GR, :].rearrange("(r p) d -> p r d", p=P)).then_inc(xn_ld, 16)
            sp.dma_start(cl_raw[:], a["ctx"][:, NK - 1, :]).then_inc(weight_ld["cl"], 16)
            sp.dma_start(wq_raw[:], a["wqT"]).then_inc(weight_ld["wq"], 16)
            sp.dma_start(wqn_raw[:], a["wqn"]).then_inc(weight_ld["wqn"], 16)
            sp.dma_start(wk_raw[:], a["wk"]).then_inc(weight_ld["wk"], 16)
            sp.dma_start(wv_raw[:], a["wvT"]).then_inc(weight_ld["wv"], 16)
            sp.dma_start(wo_raw[:], a["woT"]).then_inc(weight_ld["wo"], 16)
            sp.wait_ge(wlo, 1)
            for j, src in enumerate((cl_h, cl_h, cl_l)):
                sp.dma_start(c3_d[:, j, :], f32(src[:])).then_inc(c3_stored, 16)
            sp.wait_ge(c3_stored, 48)
            sp.dma_start(xg[:], a["x"][0:GR, :].rearrange("(r p) d -> p r d", p=P)).then_inc(xg_ld, 16)
            with sp.Fori(0, NG) as g:
                for b in range(GB + 1):
                    n = g * GB + b
                    if b < GB:
                        sp.wait_ge(ct_split, 4 * n + 4)
                        sp.dma_start(ct_raw[:], a["ctxT"][bass.ds(n, 1)].rearrange("o p k c -> p (o k) c")
                                     ).then_inc(ct_ld, 16)
                    if b == 0:
                        sp.wait_ge(qb_stored, 16 * (g + 1))
                        for f in range(4):
                            sp.dma_start(qbt[T * f:T * f + T, :, :],
                                         qb_d[bass.ds(g, 1)].rearrange("o (t f) (q b) -> (o f) q t b", f=4, b=GB)[f]
                                         ).then_inc(qb_ld, 16)
                    if b > 0:
                        sp.wait_ge(cn_split, 4 * n)
                        sp.dma_start(cn_raw[:], a["ctx"][bass.ds(n - 1, 1), 0:2 * P, :].rearrange(
                            "o (k p) d -> p (o k) d", p=P)).then_inc(cn_ld, 16)
                        s = (b - 1) % 2
                        sp.wait_ge(u_made, 2 * n)
                        sp.dma_start(f32(c3[s][:]), c3_d[bass.ds(n - 1, 1)].rearrange("o j d -> (o j) d")
                                     ).then_inc(c3_ld[s], 16)
            sp.wait_ge(made, (NG - 1) * NU + U_O)
            for t in range(2):
                sp.dma_start(fw_raw[t][:], a["ffn"][t]).then_inc(fw_ld[t], 16)
            for g in range(NG - 1):
                sp.wait_ge(x3_stored, 16 * (g + 2))
                for k in range(2):
                    sp.dma_start(f32(fts[:, k, :, g * GR:(g + 1) * GR]), ft_d[g, :, k]
                                 ).then_inc(ft_ld[g // (NG // 2)], 16)
            for t in range(2, SHARED_TILES):
                sp.wait_ge(fw_split, 2 * (t - 1))
                sp.dma_start(fw_raw[t % 2][:], a["ffn"][t]).then_inc(fw_ld[t % 2], 16)
            sp.wait_ge(x2_stored, 16 * (NG + 1))
            sp.dma_start(fx[:], x2_d.rearrange("(r p) d -> p r d", p=P)).then_inc(fx_ld, 16)
            sp.wait_ge(cb_stored, 16 * (NG + 1))
            with sp.Fori(0, ROUTED_TILES // 2) as j:
                for s in range(2):
                    r = j * 2 + s
                    t = r + SHARED_TILES
                    sp.wait_ge(fw_split, 2 * (t - 1))
                    sp.dma_start(fw_raw[s][:], a["ffn"][bass.ds(t, 1)].rearrange("o p w -> p (o w)")
                                 ).then_inc(fw_ld[s], 16)
                    sp.wait_ge(h_done, 2 * (t - 1))
                    for k in range(P // CB):
                        sp.dma_start(cw[s][CB * k:CB * (k + 1), :],
                                     cb_d.rearrange("e r t -> (e r) t")[bass.ds(r * (P // CB) + k, 1), :]
                                     .partition_broadcast(CB).rearrange("p o t -> p (o t)")
                                     ).then_inc(comb_ld[s], 16)
            for h in range(TILES // 2):
                sp.wait_ge(fy_ready, 2 * (h + 1))
                sp.dma_start(out[h * 2 * P:(h + 1) * 2 * P, :].rearrange("(r p) d -> p r d", p=P),
                             fy[:, 2 * h:2 * h + 2, :]).then_inc(stored, 16)
            sp.wait_ge(stored, 16 * (TILES // 2))

        @block.gpsimd
        def _(pool):
            def round_high(dst, src):
                return nc.gpsimd.tensor_tensor(dst, src, zero[:, 0:1].broadcast_to(list(src.shape)), ALU.add)

            st = Steps(pool, mask_ready)
            st.link(nc.gpsimd.memset(zero[:], 0.0))
            st.link(nc.gpsimd.memset(minus_half[:], -0.5))
            st.link(nc.gpsimd.memset(ident[:], 0.0))
            st.link(nc.gpsimd.affine_select(out=ident[:], in_=ident[:], compare_op=ALU.not_equal, fill=1.0,
                                            base=0, pattern=[[-1, P]], channel_multiplier=1))
            st.link(nc.gpsimd.memset(causal[:], 1.0))
            for b4 in range(4):
                st.link(nc.gpsimd.affine_select(
                    out=causal[T * b4:T * b4 + T, :], in_=causal[T * b4:T * b4 + T, :],
                    compare_op=ALU.is_ge, fill=0.0, base=0, pattern=[[1, T]], channel_multiplier=-1))
            st.link(nc.gpsimd.memset(lower[:], 1.0))
            st.link(nc.gpsimd.affine_select(out=lower[:], in_=lower[:], compare_op=ALU.is_gt, fill=0.0,
                                            base=0, pattern=[[1, E], [-1, E]], channel_multiplier=0))
            for t in (wv_h, wv_l):
                nc.gpsimd.memset(f32(t[:, :, :, DK:2 * DK]), 0.0).then_inc(ct_split, 2)
            nc.gpsimd.memset(vaug[:, :, :, LD:LD + 1], 1.0).then_inc(cn_split, 4)
            nc.gpsimd.memset(vaug[:, :, :, LD + 1:LV], 0.0).then_inc(scores_made, 4)
            nc.gpsimd.memset(combT[:], 0.0).then_inc(u_made, 4)
            nc.gpsimd.memset(rsm[:], 0.0).then_inc(x2_stored, 16)
            nc.gpsimd.memset(rank[:], 0.0).then_inc(x3_stored, 16)
            nc.gpsimd.memset(comb[:], 0.0).then_inc(cb_stored, 16)

            def root(n):
                pool.wait_ge(ln_var, n)
                nc.gpsimd.tensor_tensor(lnt[:, 2, :], lnt[:, 0, :], minus_half[:, 0:1].broadcast_to([P, RT]),
                                        ALU.pow).then_inc(ln_y, 1)

            def head_queries(r, g, side):
                pool.wait_ge(f_sum, g + 1)
                if r:
                    pool.wait_ge(side_made, side.count("sc0"))
                nc.gpsimd.tensor_tensor(qx[1][:], fm[:, 0, 1, None, r * P:(r + 1) * P].broadcast_to([P, LH // KC, P]),
                                        of_head[:, :, None].broadcast_to([P, LH // KC, P]), ALU.mult
                                        ).then_inc(f_ready, 1)

            def split_halves(parts, done, n):
                hi, lo, raw = parts
                for k in range(2):
                    round_high(hi[:, k, :], raw[:, k, :]).then_inc(done, 1)
                for k in range(2):
                    pool.wait_ge(done, 4 * n + 4 + k + 1)
                    nc.gpsimd.tensor_tensor(lo[:, k, :], raw[:, k, :], f32(hi[:, k, :]), ALU.subtract
                                            ).then_inc(done, 1)

            def split_ct(n):
                pool.wait_ge(ct_ld, 16 * (n + 1))
                pool.wait_ge(scores_made, 4 * n + 4)
                split_halves((ct_h, ct_l, ct_raw), ct_split, n)

            def split_cn(n):
                pool.wait_ge(cn_ld, 16 * (n + 1))
                pool.wait_ge(u_made, 2 * n + 4)
                split_halves((cn_h, cn_l, cn_raw), cn_split, n)

            root(1)

            def split_linear(j):
                pool.wait_ge(weight_ld["lw"], 16)
                round_high(lw_h[:, j], lw_raw[:, j]).then_inc(lw_ready, 1)
                pool.wait_ge(lw_ready, 2 * j + 1)
                nc.gpsimd.tensor_tensor(lw_l[:, j], lw_raw[:, j], f32(lw_h[:, j]), ALU.subtract
                                        ).then_inc(lw_ready, 1)

            def group(g):
                side = side_of(g)
                ln = ln_base(g)
                full = len(side.units) > 2
                split_ct(g * GB)
                if full:
                    root(ln + 1)
                    ln = ln + 1
                split_cn(g * GB)
                split_ct(g * GB + 1)
                for b in range(GB):
                    n = g * GB + b
                    if b + 2 < GB:
                        split_ct(n + 2)
                    if b < 4 and not full:
                        split_linear(b)
                    if b == 2 and full:
                        head_queries(0, g - 1, side)
                    if b == 3 and full:
                        head_queries(1, g - 1, side)
                    if b == 5:
                        root(ln + 1)
                    if b == 6 and full:
                        root(ln + 2)
                    if b + 1 < GB:
                        split_cn(n + 1)

            groups(pool, group)
            def split(t, s, raw, turn):
                pool.wait_ge(fw_ld[raw], 16 * turn)
                if not isinstance(t, int):
                    pool.wait_ge(down_done, 2 * (t - 1))
                round_high(fw_h[s][:], fw_raw[raw][:]).then_inc(fw_split, 1)
                pool.wait_ge(fw_split, 2 * t + 1)
                nc.gpsimd.tensor_tensor(fw_l[s][:], fw_raw[raw][:], f32(fw_h[s][:]), ALU.subtract
                                        ).then_inc(fw_split, 1)

            split(0, 0, 0, 1)
            root(LN_LAST + 1)
            split(1, 1, 1, 1)
            split(2, 2, 0, 2)
            split(3, 3, 1, 2)
            head_queries(0, NG - 1, LAST_SIDE)
            split(4, 4, 0, 3)
            head_queries(1, NG - 1, LAST_SIDE)
            root(LN_LAST + 2)
            pool.wait_ge(down_done, EARLY + 2)
            split(5, ffn_slot(5), 1, 3)
            with pool.Fori(0, ROUTED_TILES // 2) as j:
                for s in range(2):
                    split(j * 2 + SHARED_TILES + s, s, s, j + SHARED_TILES // 2 + 1)

        @block.scalar
        def _(act):
            def copy(dst, src):
                return nc.scalar.activation(dst, src, ACT.Identity)

            def queries_high(g, units=range(QU)):
                for i in units:
                    act.wait_ge(q_made, g * QU + i + 1)
                    for k in range(2):
                        ins = nc.scalar.activation(q_h[2 * i + k][:], bank3(i, 2)[:, k, :], ACT.Identity,
                                                   bias=bq_sb[:, 2 * i + k:2 * i + k + 1])
                    ins.then_inc(q_high, 1)

            def side_unit(side, u, g):
                if u in WITH_HIGH:
                    act.wait_ge(side_made, side.count(u))
                src = bank3(side.bank, KC)
                if u == "xn1":
                    copy(x1_h[:], src).then_inc(side_high, 1)
                elif u == "qb":
                    act.wait_ge(side_drained, side.count(u))
                    act.dma_start(qb_d[bass.ds(g, 1)].rearrange("o h r -> (o h) r"), qb_sb[:]
                                  ).then_inc(qb_stored, 16)
                elif u == "xn2":
                    act.wait_ge(x3_stored, 16 * (g + 1))
                    copy(x2s[:, 0], src).then_inc(side_high, 1)
                elif u in ("lq", "lk"):
                    nc.scalar.activation(fa[:, int(u == "lk")], src, ACT.Abs).then_inc(side_high, 1)
                    if u == "lk":
                        act.wait_ge(side_high, side.high(u))
                        nc.scalar.activation(fa[:], fa[:], ACT.Exp, scale=-1.0).then_inc(act_steps, 1)
                elif u == "v":
                    act.wait_ge(act_steps, g + 1)
                    nc.scalar.activation(fa[:], fa[:], ACT.Ln, bias=1.0).then_inc(f_ln, 1)
                elif u == "ot":
                    copy(ot_h[:], src).then_inc(side_high, 1)
                elif u == "y":
                    act.wait_ge(side_drained, side.count(u))
                    act.dma_start(x2_d[bass.ds(g * GR, GR), :].rearrange("(r p) d -> p r d", p=P), xg[:]
                                  ).then_inc(x2_stored, 16)
                elif u == "xn3":
                    copy(x2s[:, 0], src).then_inc(side_high, 1)
                    act.wait_ge(side_drained, side.count(u))
                    if side is LAST_SIDE:
                        act.dma_start(f32(fts[:, :, :, (NG - 1) * GR:]), f32(x2s[:])).then_inc(ft_ld[1], 16)
                        return
                    act.dma_start(ft_d[bass.ds(g, 1)].rearrange("o p k c r -> p (o k c) r"),
                                  f32(x2s[:].rearrange("p k c r -> p (k c) r"))).then_inc(x3_stored, 16)
                elif u == "log":
                    act.wait_ge(side_drained, side.count(u))
                    nc.scalar.activation(rl[:], rl[:], ACT.Exp).then_inc(logit_exp, 1)
                elif u == "ct":
                    act.wait_ge(side_drained, side.count(u))
                    act.dma_start(cb_d[:, :, bass.ds(g * GR, GR)],
                                  combT[:, None, :].broadcast_to([E, FE // CB, GR])).then_inc(cb_stored, 16)

            act.wait_ge(weight_ld["cl"], 16)
            copy(cl_h[:], cl_raw[:]).then_inc(whi, 1)
            act.wait_ge(const_ld, 16 * N_CONST)
            copy(gate_h[:], gateT[:]).then_inc(whi, 1)
            side_unit(FIRST_SIDE, "xn1", 0)
            act.wait_ge(weight_ld["wq"], 16)
            copy(wq_h[:], wq_raw[:]).then_inc(whi, 1)
            act.wait_ge(setup_dve, 4)
            copy(wqb_h[:], wqb[:]).then_inc(whi, 1)
            act.wait_ge(weight_ld["wk"], 16)
            copy(wk_h[:], wk_raw[:]).then_inc(whi, 1)
            act.wait_ge(weight_ld["wv"], 16)
            copy(wv_h[:, :, :, 0:DK], wv_raw[:, :, :, 0:DK]).then_inc(whi, 1)
            copy(wv_h[:, :, :, 2 * DK:3 * DK], wv_raw[:, :, :, DK:2 * DK]).then_inc(whi, 1)
            queries_high(0, [0, 1])
            act.wait_ge(weight_ld["wo"], 16)
            copy(wo_h[:], wo_raw[:]).then_inc(whi, 1)
            side_unit(FIRST_SIDE, "qb", 0)
            queries_high(0, [2, 3])

            def group(g):
                side = side_of(g)

                def high_part(u, dst, src, bias=None):
                    act.wait_ge(made, g * NU + u + 1)
                    for k in range(len(dst)):
                        ins = nc.scalar.activation(dst[k], src[k], ACT.Identity,
                                                   **({} if bias is None else {"bias": bias[k]}))
                    ins.then_inc(high, 1)

                if len(side.units) > 2:
                    act.wait_ge(made, g * NU)
                    queries_high(g, [2, 3])

                def exps(b, p):
                    if b and p == 0:
                        act.wait_ge(l3_ready, g * GB + b)
                    for t in (2 * p, 2 * p + 1):
                        act.wait_ge(bias_ready, g * (2 * GB) + 2 * b + p + 1)
                        nc.scalar.activation(pr[:, t, 0:NK], ps[:, t, 0:NK], ACT.Exp, bias=mxq[:, 2, t:t + 1],
                                             scale=SCALE, accum_out=psum_e[:, t:t + 1]).then_inc(exp_done, 1)

                def normalize(b, tiles=range(4)):
                    for t in tiles:
                        act.wait_ge(sum_ready, g * (2 * GB) + 2 * b + t // 2 + 1)
                        nc.scalar.activation(pr[:, t, 0:NK], pr[:, t, 0:NK], ACT.Copy,
                                             scale=rsum[:, t:t + 1]).then_inc(p_ready, 1)

                def slot(k):
                    for u in side.at(k):
                        side_unit(side, u, g + 1 if u in NEXT else g - 1)
                    if k == 9:
                        if len(side.units) > 2:
                            act.wait_ge(side_made, side.count("ot"))
                        act.dma_start(xn[:], a["x"][bass.ds((g + 1) * GR, GR), :].rearrange(
                            "(r p) d -> p r d", p=P)).then_inc(xn_ld, 16)
                    if k == 15 and len(side.units) > 2:
                        act.wait_ge(x2_stored, 16 * (g + 1))
                        act.dma_start(xg[:], a["x"][bass.ds(g * GR, GR), :].rearrange(
                            "(r p) d -> p r d", p=P)).then_inc(xg_ld, 16)

                for h in range(H):
                    high_part(U_QP + h, [head(qu_h, h)], [by_batch(bank3(4 + h % 4, KC))])
                if len(side.units) == 2:
                    act.dma_start(lw_raw[:], a["lwT"]).then_inc(weight_ld["lw"], 16)
                exps(0, 0)
                normalize(0, range(2))
                exps(0, 1)
                normalize(0, range(2, 4))
                for b in range(GB):
                    for k in range(2):
                        act.wait_ge(pt_made, g * (3 * GB) + 3 * b + k + 1)
                        copy(pt_h[:, k, :], ps[:, 4 + k, :]).then_inc(pt_hi, 1)
                    act.wait_ge(pt_made, g * (3 * GB) + 3 * b + 3)
                    copy(pl3[:], ps[0:3, UB, :]).then_inc(pt_hi, 1)
                    if b + 1 < GB:
                        exps(b + 1, 0)
                        exps(b + 1, 1)
                    for dt in range(KC):
                        act.wait_ge(u_made, g * (2 * GB) + 4 + 2 * b + dt + 1)
                        copy(qu_h[:, dt, b, :], ps[:, UB, :]).then_inc(u_hi, 1)
                        slot(2 * b + dt)
                        if dt == 0 and b + 1 < GB:
                            normalize(b + 1)
                for i in range(4):
                    high_part(U_ATT + i, [at_h[:, 2 * i + k, :] for k in range(2)],
                              [bank3(ATT_BANK[i], 2)[:, k, :] for k in range(2)],
                              [bv_sb[:, 2 * i + k:2 * i + k + 1] for k in range(2)])
                slot(TAIL)
                if len(side.units) > 2:
                    act.wait_ge(comb_ready, g)
                    act.wait_ge(x3_stored, 16 * (g + 1))
                else:
                    act.wait_ge(lw_ready, 8)
                queries_high(g + 1, [0, 1])

            act.wait_ge(c3_stored, 48)
            act.wait_ge(wlo, 8)
            groups(act, group)

            def last_side(u):
                side_unit(LAST_SIDE, u, NG - 1)

            def silu(i, p):
                act.wait_ge(gu_made, 2 * i + 1)
                if not isinstance(i, int) or i >= 2:
                    act.wait_ge(h_done, i - 1)
                nc.scalar.activation(sg[p][:], ps[:, 4 + 2 * p, :], ACT.Silu).then_inc(silu_done, 1)

            def hidden_high(i, p):
                act.wait_ge(h_done, i + 1)
                if not isinstance(i, int) or i >= 2:
                    act.wait_ge(down_done, i - 1)
                copy(hh[p][:], hm[p][:]).then_inc(h_hi, 1)

            act.wait_ge(made, NG * NU)
            silu(0, 0)
            last_side("xn2")
            hidden_high(0, 0)
            silu(1, 1)
            hidden_high(1, 1)
            last_side("lq")
            last_side("lk")
            last_side("v")
            silu(2, 0)
            hidden_high(2, 0)
            silu(3, 1)
            hidden_high(3, 1)
            silu(4, 0)
            hidden_high(4, 0)
            last_side("ot")
            last_side("y")
            last_side("xn3")
            last_side("log")
            silu(5, 1)
            hidden_high(5, 1)
            last_side("ct")
            for u in range(6, 2 * SHARED_TILES):
                silu(u, u % 2)
                hidden_high(u, u % 2)

            def unit(i, half, p, s, j):
                silu(i, p)
                hidden_high(i, p)

            for_routed(act, unit)
            for half in range(2):
                act.wait_ge(down_done, NUNITS - 1 + half)
                copy(fo[:, 0, half * HALF:(half + 1) * HALF], ps[:, half, :]).then_inc(fo_ready[half], 1)

        @block.vector
        def _(dve):
            V = nc.vector
            st = Steps(dve, setup_dve)
            dve.wait_ge(const_ld, 16 * N_CONST)
            st.link(V.memset(bkd[:], 0.0))
            st.add(V.tensor_copy(diag(bkd[0:DK], 0), bk_sb[0:DK, :]))
            st.add(V.tensor_copy(diag(bkd[DK:P], 1), bk_sb[DK:P, :]))
            dve.wait_ge(mask_ready, MASKS)
            V.tensor_reduce(of_head[:], ident[:].rearrange("p (h c) -> p h c", c=LD), AX.X, ALU.add
                            ).then_inc(mask_ready, 1)
            dve.wait_ge(mask_ready, MASKS + 1)

            def row_stats(steps, x):
                for r in range(RT):
                    steps.add(V.bn_stats(stats[:, r, :], x[:, r, :]))
                steps.wait()
                steps.add(V.memset(lnt[:, 3, :], 0.0))
                for r in range(RT):
                    steps.add(V.bn_aggr(mv[:, r, :], stats[:, r, :]))
                steps.wait()
                V.tensor_scalar(lnt[:, 0, :], mv[:, :, 1], LN_EPS, None, ALU.add).then_inc(ln_var, 1)

            def normalize_rows(steps, n, x):
                dve.wait_ge(ln_y, n)
                steps.link(V.tensor_tensor(lnt[:, 3, :], lnt[:, 2, :], lnt[:, 2, :], ALU.mult))
                steps.link(V.tensor_tensor(lnt[:, 3, :], lnt[:, 3, :], lnt[:, 0, :], ALU.mult))
                steps.link(V.tensor_scalar(lnt[:, 3, :], lnt[:, 3, :], -0.5, 1.5, ALU.mult, ALU.add))
                steps.link(V.tensor_tensor(lnt[:, 3, :], lnt[:, 2, :], lnt[:, 3, :], ALU.mult))
                for r in range(RT):
                    V.tensor_scalar(xn[:, r, :], x[:, r, :], mv[:, r, 0:1], lnt[:, 3, r:r + 1],
                                    ALU.subtract, ALU.mult).then_inc(xn_ready, 1)

            def features(g):
                dve.wait_ge(f_ln, g + 1)
                fl = [t[:].rearrange("p j k r -> p (j k r)") for t in (fm, fa)]
                V.scalar_tensor_tensor(fl[0], fl[0], EPS, fl[1], ALU.add, ALU.add).then_inc(f_sum, 1)
                dve.wait_ge(f_sum, g + 1)

            def head_queries(r):
                V.tensor_tensor(qx[0][:], fm[:, 0, 0, None, r * P:(r + 1) * P].broadcast_to([P, LH // KC, P]),
                                of_head[:, :, None].broadcast_to([P, LH // KC, P]), ALU.mult
                                ).then_inc(f_ready, 1)

            def side_unit(steps, side, u, g):
                src = bank3(side.bank, KC)
                if u in WITH_HIGH:
                    dve.wait_ge(side_high, side.high(u))
                else:
                    dve.wait_ge(side_made, side.count(u))
                if u in ("xn1", "xn2", "xn3", "ot"):
                    hi, lo = {"xn1": (x1_h[:], x1_l[:]), "ot": (ot_h[:], ot_l[:])}.get(u, (x2s[:, 0], x2s[:, 1]))
                    V.tensor_tensor(lo, src, f32(hi), ALU.subtract).then_inc(side_drained, 1)
                elif u == "qb":
                    V.tensor_scalar(qb_sb[:], ps[0:H, side.bank, 0:GR], bqk[:, 0:1], None, ALU.add
                                    ).then_inc(side_drained, 1)
                elif u in ("lq", "lk"):
                    if u == "lq":
                        dve.wait_ge(cb_stored, 16 * (g + 1))
                        dve.wait_ge(qb_stored, 16 * (g + 2))
                    V.tensor_scalar(fm[:, int(u == "lk")], src, 0.0, None, ALU.max).then_inc(side_drained, 1)
                elif u == "v":
                    V.tensor_copy(vaug[:, :, :, 0:LD], src.rearrange("p r (h e) -> p r h e", e=LD)
                                  ).then_inc(side_drained, 1)
                elif u in ("sc0", "sc1"):
                    V.tensor_tensor(am[:, int(u[2])], ps[:, side.bank, :].rearrange("p (h t) -> p h t", t=T),
                                    causal[:, None, :].broadcast_to([P, LH, T]), ALU.mult
                                    ).then_inc(side_drained, 1)
                elif u in ("pv0", "pv1"):
                    r = int(u[2])
                    nd = ps[:, side.bank, 0:LH * LV].rearrange("p (h e) -> p h e", e=LV)
                    steps.link(V.tensor_scalar(den[:, 0, r, :], nd[:, :, LD], EPS, None, ALU.add))
                    steps.link(V.reciprocal(den[:, 1, r, :], den[:, 0, r, :]))
                    V.tensor_tensor(xn[:, r, :].rearrange("p (h e) -> p h e", e=LD), nd[:, :, 0:LD],
                                    den[:, 1, r, :, None].broadcast_to([P, LH, LD]), ALU.mult
                                    ).then_inc(side_drained, 1)
                elif u == "y":
                    V.tensor_tensor(xg[:], src, xg[:], ALU.add).then_inc(side_drained, 1)
                elif u == "log":
                    logits(steps, side)
                elif u == "ct":
                    V.tensor_copy(combT[:], ps[0:E, side.bank, 0:GR]).then_inc(side_drained, 1)

            def wide(ap):
                return ap[:, :, None].broadcast_to([P, RT, E])

            def logits(steps, side):
                lg = ps[:, side.bank, 0:RT * E].rearrange("p (t e) -> p t e", e=E)
                steps.link(V.tensor_reduce(rsm[:, 0, :], lg, AX.X, ALU.max))
                V.tensor_tensor(rl[:], lg, wide(rsm[:, 0, :]), ALU.subtract).then_inc(side_drained, 1)

            def route(steps, g):
                dve.wait_ge(logit_exp, g + 1)
                steps.link(V.tensor_reduce(rsm[:, 1, :], rl[:], AX.X, ALU.add))
                steps.link(V.reciprocal(rsm[:, 1, :], rsm[:, 1, :]))
                steps.link(V.tensor_tensor(rl[:], rl[:], wide(rsm[:, 1, :]), ALU.mult))
                of_e = rl[:, :, :, None].broadcast_to([P, RT, E, E])
                of_f = rl[:, :, None, :].broadcast_to([P, RT, E, E])
                steps.add(V.tensor_tensor(rgt[:], of_f, of_e, ALU.is_gt))
                steps.link(V.tensor_tensor(req[:], of_f, of_e, ALU.is_equal))
                steps.link(V.tensor_tensor(req[:], req[:], lower[:, None].broadcast_to([P, RT, E, E]), ALU.mult))
                steps.link(V.tensor_tensor(rgt[:], rgt[:], req[:], ALU.add))
                steps.link(V.tensor_reduce(rank[:], rgt[:], AX.X, ALU.add))
                steps.link(V.tensor_scalar(rank[:], rank[:], 1.5, None, ALU.is_lt))
                steps.link(V.tensor_tensor(rl[:], rl[:], rank[:], ALU.mult))
                steps.link(V.tensor_reduce(rsm[:, 2, :], rl[:], AX.X, ALU.add))
                steps.link(V.tensor_scalar(rsm[:, 2, :], rsm[:, 2, :], 1e-20, None, ALU.add))
                steps.link(V.reciprocal(rsm[:, 2, :], rsm[:, 2, :]))
                steps.link(V.tensor_scalar(rsm[:, 2, :], rsm[:, 2, :], ROUTE_SCALE, None, ALU.mult))
                V.tensor_tensor(comb[:], rl[:], wide(rsm[:, 2, :]), ALU.mult).then_inc(comb_ready, 1)

            first = Steps(dve, dve_steps)
            dve.wait_ge(xn_ld, 16)
            row_stats(first, xn)
            normalize_rows(first, 1, xn)
            assert first.n == DVE_FIRST, first.n
            dve.wait_ge(whi, 1)
            V.tensor_tensor(cl_l[:], cl_raw[:], f32(cl_h[:]), ALU.subtract).then_inc(wlo, 1)
            dve.wait_ge(whi, 2)
            V.tensor_tensor(gate_l[:], gateT[:], f32(gate_h[:]), ALU.subtract).then_inc(wlo, 1)
            side_unit(first, FIRST_SIDE, "xn1", 0)

            def queries_low(g, units=range(QU)):
                for i in units:
                    dve.wait_ge(q_high, g * QU + i + 1)
                    for k in range(2):
                        hp = 2 * i + k
                        ins = V.scalar_tensor_tensor(q_l[hp][:], bank3(i, 2)[:, k, :], bq_sb[:, hp:hp + 1],
                                                     f32(q_h[hp][:]), ALU.add, ALU.subtract)
                    ins.then_inc(q_drained, 1)

            def weight_low(n, lo_, raw, hi):
                dve.wait_ge(whi, n)
                V.tensor_tensor(lo_, raw, f32(hi), ALU.subtract).then_inc(wlo, 1)

            weight_low(3, wq_l[:], wq_raw[:], wq_h[:])
            dve.wait_ge(setup_pe, 1)
            st.link(V.tensor_copy(wqb[:].rearrange("p k h -> p (k h)"), ps[:, 4, 0:KC * H]))
            dve.wait_ge(setup_pe, 2)
            st.add(V.tensor_copy(bqk[:], ps[0:H, 5, 0:1]))
            weight_low(4, wqb_l[:], wqb[:], wqb_h[:])
            weight_low(5, wk_l[:], wk_raw[:], wk_h[:])
            weight_low(6, wv_l[:, :, :, 0:DK], wv_raw[:, :, :, 0:DK], wv_h[:, :, :, 0:DK])
            weight_low(7, wv_l[:, :, :, 2 * DK:3 * DK], wv_raw[:, :, :, DK:2 * DK], wv_h[:, :, :, 2 * DK:3 * DK])
            queries_low(0, [0, 1])
            side_unit(first, FIRST_SIDE, "qb", 0)
            weight_low(8, wo_l[:], wo_raw[:], wo_h[:])
            queries_low(0, [2, 3])

            def group(g):
                side = side_of(g)
                full = len(side.units) > 2
                ln = ln_base(g)
                steps = Steps(dve, dve_steps, dve_base(g))
                ln_rows = ln + 1
                if full:
                    ln = ln + 1

                def low_part(u, dst, src, hi, bias=None):
                    dve.wait_ge(high, g * N_HIGH + u + 1)
                    for k in range(len(dst)):
                        if bias is None:
                            ins = V.tensor_tensor(dst[k], src[k], f32(hi[k]), ALU.subtract)
                        else:
                            ins = V.scalar_tensor_tensor(dst[k], src[k], bias[k], f32(hi[k]), ALU.add, ALU.subtract)
                    ins.then_inc(drained, 1)

                def maxima(b, p):
                    tt = slice(2 * p, 2 * p + 2)
                    dve.wait_ge(scores_made, g * (4 * GB) + 4 + 4 * b + 2 * p + 2)
                    steps.link(V.tensor_reduce(mxq[:, 0, tt], ps[:, tt, 0:NK], AX.X, ALU.max))
                    steps.link(V.tensor_tensor(mxq[:, 1, tt], mxq[:, 0, tt], qbt[:, tt, b], ALU.add))
                    V.scalar_tensor_tensor(mxq[:, 2, tt], mxq[:, 1, tt], -SCALE, qbs[:, tt, b],
                                           ALU.mult, ALU.add).then_inc(bias_ready, 1)

                if full:
                    queries_low(g, [2, 3])
                for h in range(H):
                    if h == 4 and full:
                        row_stats(steps, xg)
                    if h == 12:
                        dve.wait_ge(qb_ld, 64 * (g + 1))
                        steps.link(V.tensor_scalar(qbs[:], qbt[:], SCALE, None, ALU.mult))
                        maxima(0, 0)
                    low_part(U_QP + h, [head(qu_l, h)], [by_batch(bank3(4 + h % 4, KC))], [head(qu_h, h)])
                def sums(b, halves=range(2)):
                    for p in halves:
                        tt = slice(2 * p, 2 * p + 2)
                        dve.wait_ge(exp_done, g * (4 * GB) + 4 * b + 2 * p + 2)
                        V.reciprocal(rsum[:, tt], psum_e[:, tt]).then_inc(sum_ready, 1)

                def last_key(b):
                    dve.wait_ge(p_ready, g * (4 * GB) + 4 * b + 4)
                    steps.link(V.tensor_copy(l3[:, :, 0], pr[:, :, NK - 1]))
                    steps.link(V.tensor_tensor(l3[:, :, 1], pr[:, :, NK - 1], f32(l3[:, :, 0]), ALU.subtract))
                    V.tensor_copy(l3[:, :, 2], l3[:, :, 0]).then_inc(l3_ready, 1)

                def slot(k):
                    for u in side.at(k):
                        side_unit(steps, side, u, g + 1 if u in NEXT else g - 1)

                sums(0, [0])
                maxima(0, 1)
                sums(0, [1])
                maxima(1, 0)
                last_key(0)
                if full:
                    normalize_rows(steps, ln_rows, xg)
                for b in range(GB):
                    for k in range(2):
                        dve.wait_ge(pt_hi, g * (3 * GB) + 3 * b + k + 1)
                        V.tensor_tensor(pt_l[:, k, :], ps[:, 4 + k, :], f32(pt_h[:, k, :]), ALU.subtract
                                        ).then_inc(pt_lo, 1)
                    if b + 1 < GB:
                        maxima(b + 1, 1)
                        if b == 2 and full:
                            features(g - 1)
                        if b == 3 and full:
                            head_queries(1)
                        if b == 5:
                            dve.wait_ge(xn_ld, 16 * (g + 2))
                            row_stats(steps, xn)
                        if b == 6:
                            normalize_rows(steps, ln + 1, xn)
                            if full:
                                row_stats(steps, xg)
                        sums(b + 1)
                    elif full:
                        dve.wait_ge(side_made, side.count("xn1"))
                        normalize_rows(steps, ln + 2, xg)
                    for dt in range(KC):
                        dve.wait_ge(u_hi, g * (2 * GB) + 2 * b + dt + 1)
                        V.tensor_tensor(qu_l[:, dt, b, :], ps[:, UB, :], f32(qu_h[:, dt, b, :]),
                                        ALU.subtract).then_inc(u_lo, 1)
                        slot(2 * b + dt)
                        if dt == 0 and b == 2 and full:
                            head_queries(0)
                        if dt == 0 and b + 1 < GB:
                            last_key(b + 1)
                        if dt == 0 and b + 2 < GB:
                            maxima(b + 2, 0)
                if full:
                    route(steps, g - 1)
                for i in range(4):
                    low_part(U_ATT + i, [at_l[:, 2 * i + k, :] for k in range(2)],
                             [bank3(ATT_BANK[i], 2)[:, k, :] for k in range(2)],
                             [at_h[:, 2 * i + k, :] for k in range(2)],
                             [bv_sb[:, 2 * i + k:2 * i + k + 1] for k in range(2)])
                slot(TAIL)
                if full:
                    dve.wait_ge(x3_stored, 16 * (g + 1))
                else:
                    dve.wait_ge(lw_ready, 8)
                queries_low(g + 1, [0, 1])
                dve.wait_ge(xg_ld, 16 * (g + 1))
                for r in range(RT):
                    steps.add(V.tensor_tensor(xg[:, r, :], xg[:, r, :], bo_sb[:], ALU.add))
                steps.wait()
                dve.wait_ge(made, g * NU + U_O + 1)
                V.tensor_tensor(xg[:], bank3(O_BANK, RT), xg[:], ALU.add).then_inc(drained, 1)
                dve.wait_ge(drained, g * NU + U_O + 1)
                assert steps.n == (DVE_G if full else DVE_0), (full, steps.n)

            dve.wait_ge(c3_stored, 48)
            groups(dve, group)
            last = Steps(dve, dve_steps, DVE_FIRST + DVE_0 + (NG - 1) * DVE_G)
            row_stats(last, xg)
            normalize_rows(last, LN_LAST + 1, xg)

            def last_side(u):
                side_unit(last, LAST_SIDE, u, NG - 1)

            def hidden(i, p, comb_row=None):
                dve.wait_ge(gu_made, 2 * i + 2)
                dve.wait_ge(silu_done, i + 1)
                if not isinstance(i, int) or i >= 2:
                    dve.wait_ge(h_hi, i - 1)
                up = ps[:, 5 + 2 * p, :]
                if comb_row is None:
                    V.tensor_tensor(hm[p][:], up, sg[p][:], ALU.mult).then_inc(h_done, 1)
                else:
                    V.tensor_tensor(sg[p][:], up, sg[p][:], ALU.mult).then_inc(h_mid, 1)
                    dve.wait_ge(h_mid, i - 2 * SHARED_TILES + 1)
                    V.tensor_tensor(hm[p][:], sg[p][:], comb_row, ALU.mult).then_inc(h_done, 1)

            def hidden_low(i, p):
                dve.wait_ge(h_hi, i + 1)
                V.tensor_tensor(hl[p][:], hm[p][:], f32(hh[p][:]), ALU.subtract).then_inc(h_lo, 1)

            hidden(0, 0)
            last_side("xn2")
            hidden_low(0, 0)
            hidden(1, 1)
            hidden_low(1, 1)
            last_side("lq")
            last_side("lk")
            last_side("v")
            features(NG - 1)
            head_queries(0)
            hidden(2, 0)
            hidden_low(2, 0)
            hidden(3, 1)
            hidden_low(3, 1)
            last_side("sc0")
            head_queries(1)
            last_side("pv0")
            last_side("sc1")
            hidden(4, 0)
            hidden_low(4, 0)
            last_side("pv1")
            last_side("ot")
            last_side("y")
            dve.wait_ge(side_drained, LAST_SIDE.count("y"))
            row_stats(last, xg)
            normalize_rows(last, LN_LAST + 2, xg)
            last_side("xn3")
            last_side("log")
            route(last, NG - 1)
            hidden(5, 1)
            hidden_low(5, 1)
            last_side("ct")
            for u in range(6, 2 * SHARED_TILES):
                hidden(u, u % 2)
                hidden_low(u, u % 2)

            def unit(i, half, p, s, j):
                if half == 0:
                    dve.wait_ge(comb_ld[s], (P // CB) * 16 * (j + 1))
                hidden(i, p, cw[s][:, half * HALF:(half + 1) * HALF])
                hidden_low(i, p)

            for_routed(dve, unit)
            for half in range(2):
                dve.wait_ge(down_done, NUNITS - 1 + half)
                V.tensor_copy(fo[:, 1, half * HALF:(half + 1) * HALF], ps[:, 2 + half, :]
                              ).then_inc(fo_ready[half], 1)
            dve.wait_ge(fx_ld, 16)
            for r in range(TILES):
                if r % 2 == 0:
                    dve.wait_ge(fy_made, r // 2 + 1)
                V.tensor_tensor(fy[:, r, :], ps[:, 4 + r // 2, (r % 2) * D:(r % 2 + 1) * D], fx[:, r, :],
                                ALU.add).then_inc(fy_ready, 1)

        @block.tensor
        def _(pe):
            mm = nc.tensor.matmul

            def mm3(dst, w, x, start, stop):
                mm(dst, w[0], x[0], start=start, stop=False)
                mm(dst, w[0], x[1], start=False, stop=False)
                return mm(dst, w[1], x[0], start=False, stop=stop)

            pe.wait_ge(mask_ready, MASKS + 1)

            def transposes(dst):
                for kc in range(KC):
                    for r in range(RT):
                        ins = nc.tensor.transpose(dst[:, kc * GR + r * P:kc * GR + (r + 1) * P],
                                                  xn[:, r, kc * P:(kc + 1) * P], ident[:])
                return ins

            def projection(dst, j, et):
                w = slice(et * P, (et + 1) * P)
                for kc in range(KC):
                    ins = mm3(dst, (lw_h[:, j, kc, w], lw_l[:, j, kc, w]), (x2s[:, 0, kc], x2s[:, 1, kc]),
                              kc == 0, kc == 1)
                return ins

            def side_waits(side, u, g, ln):
                if u != side.units[0] or side is not FIRST_SIDE:
                    pe.wait_ge(side_drained, side.before(u))
                if u in ("xn1", "xn2", "xn3"):
                    pe.wait_ge(xn_ready, RT * ln)
                elif u == "lq":
                    pe.wait_ge(lw_ready, 8)
                elif u in ("sc0", "sc1"):
                    pe.wait_ge(f_ready, 4 * g + 2 * int(u[2]) + 2)
                elif u == "ct":
                    pe.wait_ge(comb_ready, g + 1)

            def side_unit(side, u):
                bank = ps[:, side.bank, :]
                if u in ("xn1", "xn2", "xn3"):
                    ins = transposes(bank)
                elif u == "qb":
                    for kc in range(KC):
                        x = [t[:, kc, :].rearrange("p (b q) -> p q b", q=T) for t in (x1_h, x1_l)]
                        ins = mm3(ps[0:H, side.bank, 0:GR], (wqb_h[:, kc, :], wqb_l[:, kc, :]), x, kc == 0, kc == 1)
                elif u in ("lq", "lk"):
                    for et in range(KC):
                        ins = projection(bank[:, et * GR:(et + 1) * GR], int(u == "lk"), et)
                elif u == "v":
                    for r in range(RT):
                        w = slice(r * P, (r + 1) * P)
                        for kc in range(KC):
                            ins = mm3(bank[:, r * D:(r + 1) * D], (x2s[:, 0, kc, w], x2s[:, 1, kc, w]),
                                      (lw_h[:, 2, kc, :], lw_l[:, 2, kc, :]), kc == 0, kc == 1)
                elif u in ("sc0", "sc1"):
                    r = int(u[2])
                    for et in range(KC):
                        for b4 in range(4):
                            w = slice(r * P + T * b4, r * P + T * b4 + T)
                            ins = mm(ps[T * b4:T * b4 + T, side.bank, et * GR:(et + 1) * GR], fm[:, 1, et, w],
                                     qx[et][:, :, T * b4:T * b4 + T], start=True, stop=True)
                elif u in ("pv0", "pv1"):
                    r = int(u[2])
                    for b4 in range(4):
                        rows = slice(T * b4, T * b4 + T)
                        for h in range(LH):
                            ins = mm(ps[rows, side.bank, h * LV:(h + 1) * LV], am[rows, r, h, :], vaug[rows, r, h, :],
                                     start=True, stop=True)
                elif u == "ot":
                    ins = transposes(bank)
                elif u == "y":
                    for r in range(RT):
                        w = slice(r * P, (r + 1) * P)
                        for kc in range(KC):
                            ins = mm3(bank[:, r * D:(r + 1) * D], (ot_h[:, kc, w], ot_l[:, kc, w]),
                                      (lw_h[:, 3, kc, :], lw_l[:, 3, kc, :]), kc == 0, kc == 1)
                elif u == "log":
                    for r in range(RT):
                        w = slice(r * P, (r + 1) * P)
                        for kc in range(KC):
                            ins = mm3(bank[:, r * E:(r + 1) * E], (x2s[:, 0, kc, w], x2s[:, 1, kc, w]),
                                      (gate_h[:, kc, :], gate_l[:, kc, :]), kc == 0, kc == 1)
                elif u == "ct":
                    for r in range(RT):
                        ins = nc.tensor.transpose(ps[0:E, side.bank, r * P:(r + 1) * P], comb[:, r, :], ident[:])
                ins.then_inc(side_made, 1)

            side_waits(FIRST_SIDE, "xn1", 0, 1)
            side_unit(FIRST_SIDE, "xn1")
            def queries(i):
                for k in range(2):
                    hp = 2 * i + k
                    for kc in range(KC):
                        w = slice(hp * P, (hp + 1) * P)
                        ins = mm3(ps[:, i, k * GR:(k + 1) * GR],
                                  (wq_h[:, kc, w], wq_l[:, kc, w]), (x1_h[:, kc, :], x1_l[:, kc, :]),
                                  kc == 0, kc == 1)
                ins.then_inc(q_made, 1)

            pe.wait_ge(weight_ld["wqn"], 16)
            pe.wait_ge(setup_dve, 3)
            for kc in range(KC):
                for hp in range(HP):
                    ins = mm(ps[:, 4, kc * H:(kc + 1) * H], wqn_raw[:, hp, kc * P:(kc + 1) * P], bkd[:, hp, :],
                             start=hp == 0, stop=hp == HP - 1)
            ins.then_inc(setup_pe, 1)
            for hp in range(HP):
                ins = mm(ps[0:H, 5, 0:1], bkd[:, hp, :], bq_sb[:, hp:hp + 1], start=hp == 0, stop=hp == HP - 1)
            ins.then_inc(setup_pe, 1)
            pe.wait_ge(wlo, 3)
            pe.wait_ge(side_drained, 1)
            queries(0)
            queries(1)
            pe.wait_ge(wlo, 4)
            pe.wait_ge(setup_dve, 5)
            side_waits(FIRST_SIDE, "qb", 0, 1)
            side_unit(FIRST_SIDE, "qb")
            pe.wait_ge(wlo, 7)
            queries(2)
            queries(3)

            def group(g):
                side = side_of(g)
                full = len(side.units) > 2
                ln = ln_base(g)
                def scores(b, tiles):
                    for kc in range(KC):
                        for t in tiles:
                            if b and kc == 0:
                                pe.wait_ge(exp_done, g * (4 * GB) + 4 * (b - 1) + t + 1)
                            if t == 0:
                                pe.wait_ge(ct_split, (g * GB + b) * 4 + 4 + kc + 3)
                            q = [x[:, kc, b, P * t:P * t + P] for x in (qu_h, qu_l)]
                            ins = mm3(ps[:, t, 0:NKP], q, (ct_h[:, kc, :], ct_l[:, kc, :]), kc == 0, kc == 1)
                            if kc == 1:
                                ins.then_inc(scores_made, 1)

                for h in range(H):
                    if full and h == 1:
                        pe.wait_ge(drained, g * NU)
                    if not full and h == 3:
                        pe.wait_ge(side_drained, 2)
                        pe.wait_ge(wlo, 8)
                    if full and h == 3:
                        pe.wait_ge(side_drained, side.base)
                    if h >= 4:
                        pe.wait_ge(drained, g * NU + U_QP + h - 3)
                    pe.wait_ge(q_drained, g * QU + h // 4 + 1)
                    rows = slice(DK * (h % 2), DK * (h % 2) + DK)
                    for dt in range(KC):
                        w = slice(dt * P, (dt + 1) * P)
                        ins = mm3(ps[:, 4 + h % 4, dt * GR:(dt + 1) * GR],
                                  (wk_h[rows, h // 2, w], wk_l[rows, h // 2, w]),
                                  (q_h[h // 2][rows, :], q_l[h // 2][rows, :]), True, True)
                    ins.then_inc(made, 1)
                    if h % 4 == 3 and h > 4:
                        scores(0, [h // 4 - 1])
                pe.wait_ge(drained, g * NU + U_QP + H)
                scores(0, [3])

                def probs_t(b):
                    for k in range(2):
                        for t in range(4):
                            if k == 0:
                                pe.wait_ge(p_ready, g * (4 * GB) + 4 * b + t + 1)
                            ins = nc.tensor.transpose(ps[:, 4 + k, t * P:(t + 1) * P],
                                                      pr[:, t, k * P:(k + 1) * P], ident[:])
                        ins.then_inc(pt_made, 1)

                def last_key_t(b):
                    pe.wait_ge(l3_ready, g * GB + b + 1)
                    if b:
                        pe.wait_ge(u_lo, g * (2 * GB) + 2 * b)
                    for t in range(4):
                        ins = nc.tensor.transpose(ps[0:3, UB, t * P:(t + 1) * P], f32(l3[:, t, :]), ident[:])
                    ins.then_inc(pt_made, 1)

                def attend(b, dt, waits):
                    s = b % 2
                    w = slice(dt * P, (dt + 1) * P)
                    if dt == 0:
                        pe.wait_ge(c3_ld[s], 16 * (g * (GB // 2) + b // 2 + 1))
                        pe.wait_ge(pt_hi, g * (3 * GB) + 3 * b + 3)
                    else:
                        pe.wait_ge(u_lo, g * (2 * GB) + 2 * b + 1)
                    for k in range(2):
                        if dt == 0:
                            pe.wait_ge(cn_split, (g * GB + b) * 4 + 4 + k + 3)
                            pe.wait_ge(pt_lo, g * (2 * GB) + 2 * b + k + 1)
                        mm3(ps[:, UB, :], (cn_h[:, k, w], cn_l[:, k, w]), (pt_h[:, k, :], pt_l[:, k, :]),
                            k == 0, False)
                    waits()
                    mm(ps[:, UB, :], c3[s][0:3, w], pl3[0:3, :], start=False, stop=True).then_inc(u_made, 1)

                lns = {"xn2": ln + 1, "xn1": ln + 2, "xn3": ln + 3} if full else {"xn1": ln + 1}

                scores(1, range(2))
                for b in range(GB):
                    probs_t(b)
                    if b + 1 < GB:
                        scores(b + 1, [2])
                    last_key_t(b)
                    if b + 1 < GB:
                        scores(b + 1, [3])
                    else:
                        pe.wait_ge(exp_done, g * (4 * GB) + 4 * GB - 3)
                        queries(0)
                    for dt in range(KC):
                        units = side.at(2 * b + dt)

                        def waits():
                            for u in units:
                                side_waits(side, u, g + 1 if u in NEXT else g - 1, lns.get(u))

                        small = units and units[0] in ("sc0", "pv0", "sc1", "pv1")
                        attend(b, dt, waits if small else lambda: None)
                        if not small:
                            waits()
                        for u in units:
                            side_unit(side, u)
                        if dt == 0 and b + 2 < GB:
                            scores(b + 2, range(2))
                        if b + 1 == GB and dt == 0:
                            pe.wait_ge(exp_done, g * (4 * GB) + 4 * GB)
                            queries(1)
                pe.wait_ge(u_lo, g * (2 * GB) + 2 * GB)
                for i in range(4):
                    if i == 3:
                        pe.wait_ge(drained, g * NU + U_ATT + 1)
                    for k in range(2):
                        hp = 2 * i + k
                        for j in range(2):
                            w = slice(DK * j, DK * j + P)
                            for kc in range(KC):
                                ins = mm3(ps[:, ATT_BANK[i], k * GR:(k + 1) * GR], (wv_h[:, kc, hp, w], wv_l[:, kc, hp, w]),
                                          (head(qu_h, 2 * hp + j)[:, kc], head(qu_l, 2 * hp + j)[:, kc]),
                                          j == 0 and kc == 0, j == 1 and kc == 1)
                    ins.then_inc(made, 1)
                for u in side.at(TAIL):
                    side_waits(side, u, g - 1, None)
                    side_unit(side, u)
                queries(2)
                pe.wait_ge(drained, g * NU + U_ATT + 4)
                for r in range(RT):
                    w = slice(r * P, (r + 1) * P)
                    for hp in range(HP):
                        ins = mm3(ps[:, O_BANK, r * D:(r + 1) * D], (at_h[:, hp, w], at_l[:, hp, w]),
                                  (wo_h[:, hp, :], wo_l[:, hp, :]), hp == 0, hp == HP - 1)
                ins.then_inc(made, 1)
                queries(3)

            groups(pe, group)

            def last_side(u):
                side_waits(LAST_SIDE, u, NG - 1, {"xn2": LN_LAST + 1, "xn3": LN_LAST + 2}.get(u))
                side_unit(LAST_SIDE, u)

            def gate_up(i, half, p, s):
                if not isinstance(i, int) or i >= 2:
                    pe.wait_ge(h_lo, i - 1)
                tok = slice(half * HALF, (half + 1) * HALF)
                for gu in range(2):
                    if isinstance(i, int) and i == 0 and gu == 1:
                        pe.wait_ge(drained, NG * NU)
                    for kc in range(KC):
                        w = slice((gu * KC + kc) * P, (gu * KC + kc + 1) * P)
                        ins = mm3(ps[:, 4 + 2 * p + gu, :], (fw_h[s][:, w], fw_l[s][:, w]),
                                  (fts[:, 0, kc, tok], fts[:, 1, kc, tok]), kc == 0, kc == 1)
                    ins.then_inc(gu_made, 1)

            def down(i, half, p, s, start=False, stop=False):
                pe.wait_ge(h_lo, i + 1)
                for dt in range(KC):
                    w = slice(2 * KC * P + dt * P, 2 * KC * P + (dt + 1) * P)
                    ps_ = ps[:, 2 * dt + half, :]
                    mm(ps_, fw_h[s][:, w], hh[p][:], start=start, stop=False, skip_group_check=True)
                    mm(ps_, fw_h[s][:, w], hl[p][:], start=False, stop=False, skip_group_check=True)
                    ins = mm(ps_, fw_l[s][:, w], hh[p][:], start=False, stop=stop, skip_group_check=True)
                ins.then_inc(down_done, 1)

            def first_gate_up(u):
                t, half = ffn_unit(u)
                pe.wait_ge(fw_split, 2 * t + 2)
                gate_up(u, half, u % 2, ffn_slot(t))

            def first_down(u):
                t, half = ffn_unit(u)
                down(u, half, u % 2, ffn_slot(t), start=t == 0)

            pe.wait_ge(ft_ld[0], 2 * 16 * (NG // 2))
            first_gate_up(0)
            last_side("xn2")
            first_gate_up(1)
            first_down(0)
            last_side("lq")
            last_side("lk")
            first_down(1)
            last_side("v")
            first_gate_up(2)
            first_gate_up(3)
            last_side("sc0")
            first_down(2)
            last_side("pv0")
            first_down(3)
            last_side("sc1")
            first_gate_up(4)
            last_side("pv1")
            last_side("ot")
            last_side("y")
            first_down(4)
            last_side("xn3")
            last_side("log")
            pe.wait_ge(ft_ld[1], 2 * 16 * (NG // 2 - 1) + 16)
            first_gate_up(5)
            first_gate_up(6)
            last_side("ct")
            pe.wait_ge(side_drained, LAST_SIDE.base + len(LAST))
            first_down(5)
            for u in range(7, 2 * SHARED_TILES):
                first_gate_up(u)
                first_down(u - 1)

            def unit(i, half, p, s, j):
                if half == 0:
                    pe.wait_ge(fw_split, i + 2)
                gate_up(i, half, p, s)
                if half:
                    down(i - 1, 0, 0, s)
                else:
                    down(i - 1, 1, 1, 1 - s)

            for_routed(pe, unit)
            down(NUNITS - 1, 1, 1, (FTILES - 1) % 2, stop=True)
            for r in range(TILES):
                if r % (TILES // 2) == 0:
                    pe.wait_ge(fo_ready[r // (TILES // 2)], 2)
                for dt in range(KC):
                    ins = nc.tensor.transpose(ps[:, 4 + r // 2, (r % 2) * D + dt * P:(r % 2) * D + (dt + 1) * P],
                                              fo[:, dt, r * P:(r + 1) * P], ident[:])
                if r % 2:
                    ins.then_inc(fy_made, 1)


def kernel(**inputs):
    import numpy as _np
    import concourse.bacc as _bacc
    from concourse import mybir as _mybir
    from concourse.bass_utils import run_bass_kernel_spmd as _run

    x = {k: _np.ascontiguousarray(v) for k, v in inputs.items()}

    def in_chunks(w):
        return w.reshape(w.shape[0] // 128, 128, w.shape[1]).transpose(1, 0, 2)

    ctx = x["ctx_1024"]
    ctxT = _np.zeros((32, 128, 2, 258), ctx.dtype)
    ctxT[:, :, :, 0:257] = ctx.transpose(0, 2, 1).reshape(32, 2, 128, 257).transpose(0, 2, 1, 3)

    def tiles(gate, up, down):
        n = -(-down.shape[0] // 128)
        parts = []
        for w in (gate, up):
            full = _np.zeros((256, 128 * n), w.dtype)
            full[:, 0:w.shape[1]] = w
            parts.append(full.reshape(2, 128, n, 128).transpose(2, 1, 0, 3).reshape(n, 128, 256))
        rows = _np.zeros((128 * n, 256), down.dtype)
        rows[0:down.shape[0]] = down
        return _np.concatenate(parts + [rows.reshape(n, 128, 256)], axis=2)

    p = "L0_ffn_"
    ffn = [tiles(x[p + "sw_gate"], x[p + "sw_up"], x[p + "sw_down"]),
           tiles(x[p + "w_gate"].transpose(1, 0, 2).reshape(256, -1),
                 x[p + "w_up"].transpose(1, 0, 2).reshape(256, -1), x[p + "w_down"].reshape(-1, 256))]
    p = "L0_xattn_"
    laid = {
        "x": _np.concatenate([x["x"].reshape(1024, 256), _np.zeros((256, 256), x["x"].dtype)]),
        "ctx": ctx,
        "ctxT": ctxT,
        "wqn": in_chunks(x[p + "Wq"]),
        "wqT": in_chunks(x[p + "Wq"].T),
        "wk": in_chunks(x[p + "Wk"]),
        "wvT": in_chunks(x[p + "Wv"].T).reshape(128, 2, 8, 128),
        "woT": in_chunks(x[p + "Wo"].T),
        "bq": x[p + "bq"].reshape(8, 128).T,
        "bk": x[p + "bk"].reshape(8, 128).T,
        "bv": x[p + "bv"].reshape(8, 128).T,
        "bo": x[p + "bo"],
        "lwT": _np.stack([in_chunks(x["L0_attn_" + w].T) for w in ("Wq", "Wk", "Wv", "Wo")], axis=1),
        "gateT": in_chunks(x["L0_ffn_gate_w"].T),
        "ffn": _np.concatenate(ffn),
    }
    nc = _bacc.Bacc("TRN2", target_bir_lowering=False, num_devices=1)
    arrays, aps = {}, {}
    for name, v in laid.items():
        v = _np.ascontiguousarray(v)
        arrays[f"in_{name}"] = v
        aps[name] = nc.dram_tensor(f"in_{name}", v.shape, _mybir.dt.from_np(v.dtype), kind="ExternalInput").ap()
    out = nc.dram_tensor("out_0", (1024, 256), _mybir.dt.float32, kind="ExternalOutput").ap()
    build(nc, aps, out)
    r = _run(nc, [arrays], core_ids=[0])
    return r.results[0]["out_0"].reshape(32, 32, 256)
```
